# Optimizing a Trainium2 kernel written in Bass

```python
import numpy as np
import jax
import jax.numpy as jnp

def _softmax(x, axis=-1):
    return jax.nn.softmax(x, axis=axis)

def _gelu(x):
    return jax.nn.gelu(x, approximate=True)

def _silu(x):
    return jax.nn.silu(x)

def _sigmoid(x):
    return jax.nn.sigmoid(x)

def _layernorm(x, axis=-1, eps=1e-05):
    m = jnp.mean(x, axis=axis, keepdims=True)
    v = jnp.var(x, axis=axis, keepdims=True)
    return (x - m) / jnp.sqrt(v + eps)

def _scatter_add(tgt, idx, src, axis=0):
    return tgt.at[idx].add(src)

def _segment_sum(src, seg, n):
    return jax.ops.segment_sum(src, seg, n)
kernel_name = 'mk_seq_postln_d2_jaxref_r8_2346e7'

def setup_inputs(seed: int=0):
    np.random.seed(seed)
    _w = jnp.asarray

    def _L0_attn_setup():
        import jax, jax.numpy as jnp
        import numpy as np
        D_MODEL = 128
        D_STATE = 64
        EPS = 1e-05
        key = jax.random.key(seed)
        ks = jax.random.split(key, 10)
        B, L, M, S = (4, 512, D_MODEL, D_STATE)
        s = 0.02
        return {'x': jax.random.normal(ks[0], (B, L, M), jnp.float32), 'A_log': jax.random.normal(ks[1], (1, 1, S), jnp.float32), 'Dmat': jax.random.normal(ks[2], (S, M), jnp.float32) * s, 'W_in': jax.random.normal(ks[3], (2 * M, M), jnp.float32) * s, 'b_in': jnp.zeros((2 * M,), jnp.float32), 'W_xp': jax.random.normal(ks[4], (S, M), jnp.float32) * s, 'b_xp': jnp.zeros((S,), jnp.float32), 'W_out': jax.random.normal(ks[5], (M, M), jnp.float32) * s, 'b_out': jnp.zeros((M,), jnp.float32), 'gamma': jnp.ones((M,), jnp.float32), 'beta': jnp.zeros((M,), jnp.float32)}
    _L0_attn_in = _L0_attn_setup()

    def _L0_ffn_setup():
        import jax, jax.numpy as jnp
        import numpy as np
        H = 128
        I = 88
        E = 64
        TOP_K = 8
        NG = 8
        TOPK_GROUP = 4
        N_SHARED = 2
        ROUTED_SCALE = 2.5
        S_I = I * N_SHARED

        def _route(x, gate_w, gate_bias):
            T = x.shape[0]
            logits = x @ gate_w.T
            scores = jax.nn.sigmoid(logits)
            scores_for_choice = scores + gate_bias[None, :]
            grp = scores_for_choice.reshape(T, NG, E // NG)
            group_scores = jnp.sum(jax.lax.top_k(grp, 2)[0], axis=-1)
            _, gidx = jax.lax.top_k(group_scores, TOPK_GROUP)
            gmask = jnp.zeros((T, NG), dtype=scores.dtype).at[jnp.arange(T)[:, None], gidx].set(1.0)
            emask = jnp.repeat(gmask, E // NG, axis=1)
            masked = jnp.where(emask > 0, scores_for_choice, 0.0)
            _, topk_idx = jax.lax.top_k(masked, TOP_K)
            topk_w = jnp.take_along_axis(scores, topk_idx, axis=1)
            topk_w = topk_w / (jnp.sum(topk_w, axis=-1, keepdims=True) + 1e-20)
            topk_w = topk_w * ROUTED_SCALE
            rw = jnp.zeros((T, E), dtype=scores.dtype).at[jnp.arange(T)[:, None], topk_idx].add(topk_w)
            return rw

        def _mlp(x, gw, uw, dw):
            return jax.nn.silu(x @ gw.T) * (x @ uw.T) @ dw.T
        key = jax.random.key(seed)
        ks = jax.random.split(key, 10)
        sc = 0.02
        return {'hidden_states': jax.random.normal(ks[0], (1, 128, H), dtype=jnp.float32), 'gate_w': sc * jax.random.normal(ks[1], (E, H), dtype=jnp.float32), 'gate_bias': sc * jax.random.normal(ks[2], (E,), dtype=jnp.float32), 'Wg': sc * jax.random.normal(ks[3], (E, I, H), dtype=jnp.float32), 'Wu': sc * jax.random.normal(ks[4], (E, I, H), dtype=jnp.float32), 'Wd': sc * jax.random.normal(ks[5], (E, H, I), dtype=jnp.float32), 'Sg': sc * jax.random.normal(ks[6], (S_I, H), dtype=jnp.float32), 'Su': sc * jax.random.normal(ks[7], (S_I, H), dtype=jnp.float32), 'Sd': sc * jax.random.normal(ks[8], (H, S_I), dtype=jnp.float32)}
    _L0_ffn_in = _L0_ffn_setup()

    def _L1_attn_setup():
        import jax, jax.numpy as jnp
        import numpy as np
        DIM = 128
        HEADS = 16
        HEAD_DIM = DIM // HEADS
        B, N = (2, 256)
        SCALE = 1.0 / np.float32(np.sqrt(DIM))

        def _split_heads(t):
            b, n, _ = t.shape
            return jnp.moveaxis(t.reshape(b, n, HEADS, HEAD_DIM), 2, 0)
        key = jax.random.key(seed)
        ks = jax.random.split(key, 9)
        s = 0.02
        return {'x': jax.random.normal(ks[0], (B, N, DIM), dtype=jnp.float32), 'Wq': jax.random.normal(ks[1], (DIM, DIM), dtype=jnp.float32) * s, 'bq': jax.random.normal(ks[2], (DIM,), dtype=jnp.float32) * s, 'Wk': jax.random.normal(ks[3], (DIM, DIM), dtype=jnp.float32) * s, 'bk': jax.random.normal(ks[4], (DIM,), dtype=jnp.float32) * s, 'Wv': jax.random.normal(ks[5], (DIM, DIM), dtype=jnp.float32) * s, 'bv': jax.random.normal(ks[6], (DIM,), dtype=jnp.float32) * s, 'Wo': jax.random.normal(ks[7], (DIM, DIM), dtype=jnp.float32) * s, 'bo': jax.random.normal(ks[8], (DIM,), dtype=jnp.float32) * s}
    _L1_attn_in = _L1_attn_setup()

    def _L1_ffn_setup():
        import jax, jax.numpy as jnp
        import numpy as np
        import math
        D_IN = 128
        FEATURES = (512, 512, 128)
        BATCH, SEQ = (8, 256)

        def _conn_dense(kernel_bool, x):
            w = jnp.where(kernel_bool, jnp.float32(1.0), jnp.float32(-1.0))
            return x @ w
        key = jax.random.key(seed)
        kx, kk0, kk1, kk2 = jax.random.split(key, 4)
        x = jax.random.normal(kx, (BATCH, SEQ, D_IN), dtype=jnp.float32)
        k0 = jax.random.randint(kk0, (2 * D_IN, FEATURES[0]), 0, 2).astype(jnp.bool_)
        k1 = jax.random.randint(kk1, (FEATURES[0], FEATURES[1]), 0, 2).astype(jnp.bool_)
        k2 = jax.random.randint(kk2, (FEATURES[1], FEATURES[2]), 0, 2).astype(jnp.bool_)
        s0 = jnp.asarray(1.0 / math.sqrt(2 * D_IN), dtype=jnp.float32)
        s1 = jnp.asarray(1.0 / math.sqrt(FEATURES[0]), dtype=jnp.float32)
        s2 = jnp.asarray(1.0 / math.sqrt(FEATURES[1]), dtype=jnp.float32)
        return {'x': x, 'k0': k0, 'k1': k1, 'k2': k2, 's0': s0, 's1': s1, 's2': s2}
    _L1_ffn_in = _L1_ffn_setup()
    _d = {'L0_attn_x': _L0_attn_in['x'], 'L0_attn_A_log': _L0_attn_in['A_log'], 'L0_attn_Dmat': _L0_attn_in['Dmat'], 'L0_attn_W_in': _L0_attn_in['W_in'], 'L0_attn_b_in': _L0_attn_in['b_in'], 'L0_attn_W_xp': _L0_attn_in['W_xp'], 'L0_attn_b_xp': _L0_attn_in['b_xp'], 'L0_attn_W_out': _L0_attn_in['W_out'], 'L0_attn_b_out': _L0_attn_in['b_out'], 'L0_attn_gamma': _L0_attn_in['gamma'], 'L0_attn_beta': _L0_attn_in['beta'], 'L0_ffn_gate_w': _L0_ffn_in['gate_w'], 'L0_ffn_gate_bias': _L0_ffn_in['gate_bias'], 'L0_ffn_Wg': _L0_ffn_in['Wg'], 'L0_ffn_Wu': _L0_ffn_in['Wu'], 'L0_ffn_Wd': _L0_ffn_in['Wd'], 'L0_ffn_Sg': _L0_ffn_in['Sg'], 'L0_ffn_Su': _L0_ffn_in['Su'], 'L0_ffn_Sd': _L0_ffn_in['Sd'], 'L1_attn_Wq': _L1_attn_in['Wq'], 'L1_attn_bq': _L1_attn_in['bq'], 'L1_attn_Wk': _L1_attn_in['Wk'], 'L1_attn_bk': _L1_attn_in['bk'], 'L1_attn_Wv': _L1_attn_in['Wv'], 'L1_attn_bv': _L1_attn_in['bv'], 'L1_attn_Wo': _L1_attn_in['Wo'], 'L1_attn_bo': _L1_attn_in['bo'], 'L1_ffn_k0': _L1_ffn_in['k0'], 'L1_ffn_k1': _L1_ffn_in['k1'], 'L1_ffn_k2': _L1_ffn_in['k2'], 'L1_ffn_s0': _L1_ffn_in['s0'], 'L1_ffn_s1': _L1_ffn_in['s1'], 'L1_ffn_s2': _L1_ffn_in['s2']}
    _x0 = _d['L0_attn_x']
    _d['L0_attn_x'] = jax.random.normal(jax.random.fold_in(jax.random.key(seed), 1), (4, 512, 128), dtype=_x0.dtype)
    del _x0
    return _d

def reference(L0_attn_x, L0_attn_A_log, L0_attn_Dmat, L0_attn_W_in, L0_attn_b_in, L0_attn_W_xp, L0_attn_b_xp, L0_attn_W_out, L0_attn_b_out, L0_attn_gamma, L0_attn_beta, L0_ffn_gate_w, L0_ffn_gate_bias, L0_ffn_Wg, L0_ffn_Wu, L0_ffn_Wd, L0_ffn_Sg, L0_ffn_Su, L0_ffn_Sd, L1_attn_Wq, L1_attn_bq, L1_attn_Wk, L1_attn_bk, L1_attn_Wv, L1_attn_bv, L1_attn_Wo, L1_attn_bo, L1_ffn_k0, L1_ffn_k1, L1_ffn_k2, L1_ffn_s0, L1_ffn_s1, L1_ffn_s2):

    def _L0_attn_ref(x, A_log, Dmat, W_in, b_in, W_xp, b_xp, W_out, b_out, gamma, beta):
        import jax, jax.numpy as jnp
        import numpy as np
        D_MODEL = 128
        D_STATE = 64
        EPS = 1e-05
        B, L, M = x.shape
        S = A_log.shape[-1]
        mu = jnp.mean(x, axis=-1, keepdims=True)
        var = jnp.mean(jnp.square(x - mu), axis=-1, keepdims=True)
        x_norm = (x - mu) * jax.lax.rsqrt(var + EPS) * gamma + beta
        xz = jnp.einsum('blm,nm->bln', x_norm, W_in) + b_in
        x_p, z = jnp.split(xz, 2, axis=-1)
        x_p = jax.nn.silu(x_p)
        z = jax.nn.sigmoid(z)
        u = jnp.einsum('blm,sm->bls', x_p, W_xp) + b_xp
        a = jnp.exp(-jnp.exp(A_log[0, 0]))

        def step(h, inp):
            u_t, z_t = inp
            h = a * h + u_t
            out = h @ Dmat * z_t
            return (h, out)
        h0 = jnp.zeros((B, S), x.dtype)
        _, ys = jax.lax.scan(step, h0, (jnp.swapaxes(u, 0, 1), jnp.swapaxes(z, 0, 1)))
        y = jnp.einsum('lbm,nm->lbn', ys, W_out) + b_out
        y = y.reshape(B, L, M)
        return x + y

    def _L0_ffn_ref(hidden_states, gate_w, gate_bias, Wg, Wu, Wd, Sg, Su, Sd):
        import jax, jax.numpy as jnp
        import numpy as np
        H = 128
        I = 88
        E = 64
        TOP_K = 8
        NG = 8
        TOPK_GROUP = 4
        N_SHARED = 2
        ROUTED_SCALE = 2.5
        S_I = I * N_SHARED

        def _route(x, gate_w, gate_bias):
            T = x.shape[0]
            logits = x @ gate_w.T
            scores = jax.nn.sigmoid(logits)
            scores_for_choice = scores + gate_bias[None, :]
            grp = scores_for_choice.reshape(T, NG, E // NG)
            group_scores = jnp.sum(jax.lax.top_k(grp, 2)[0], axis=-1)
            _, gidx = jax.lax.top_k(group_scores, TOPK_GROUP)
            gmask = jnp.zeros((T, NG), dtype=scores.dtype).at[jnp.arange(T)[:, None], gidx].set(1.0)
            emask = jnp.repeat(gmask, E // NG, axis=1)
            masked = jnp.where(emask > 0, scores_for_choice, 0.0)
            _, topk_idx = jax.lax.top_k(masked, TOP_K)
            topk_w = jnp.take_along_axis(scores, topk_idx, axis=1)
            topk_w = topk_w / (jnp.sum(topk_w, axis=-1, keepdims=True) + 1e-20)
            topk_w = topk_w * ROUTED_SCALE
            rw = jnp.zeros((T, E), dtype=scores.dtype).at[jnp.arange(T)[:, None], topk_idx].add(topk_w)
            return rw

        def _mlp(x, gw, uw, dw):
            return jax.nn.silu(x @ gw.T) * (x @ uw.T) @ dw.T
        B, S, _ = hidden_states.shape
        x = hidden_states.reshape(B * S, H)
        rw = _route(x, gate_w, gate_bias)
        expert_out = jax.vmap(lambda gw_, uw_, dw_: _mlp(x, gw_, uw_, dw_))(Wg, Wu, Wd)
        routed = jnp.einsum('eth,te->th', expert_out, rw)
        shared = _mlp(x, Sg, Su, Sd)
        out = (routed + shared).reshape(B, S, H)
        return out

    def _L1_attn_ref(x, Wq, bq, Wk, bk, Wv, bv, Wo, bo):
        import jax, jax.numpy as jnp
        import numpy as np
        DIM = 128
        HEADS = 16
        HEAD_DIM = DIM // HEADS
        B, N = (2, 256)
        SCALE = 1.0 / np.float32(np.sqrt(DIM))

        def _split_heads(t):
            b, n, _ = t.shape
            return jnp.moveaxis(t.reshape(b, n, HEADS, HEAD_DIM), 2, 0)
        q = _split_heads(x @ Wq.T + bq)
        k = _split_heads(x @ Wk.T + bk)
        v = _split_heads(x @ Wv.T + bv)
        scores = jnp.einsum('hbnd,hbmd->hbnm', k, q) * SCALE
        attn = jax.nn.softmax(scores, axis=-1)
        out = jnp.einsum('hbnm,hbmd->hbnd', attn, v)
        out = jnp.moveaxis(out, 0, 2).reshape(x.shape[0], x.shape[1], DIM)
        return out @ Wo.T + bo

    def _L1_ffn_ref(x, k0, k1, k2, s0, s1, s2):
        import jax, jax.numpy as jnp
        import numpy as np
        import math
        D_IN = 128
        FEATURES = (512, 512, 128)
        BATCH, SEQ = (8, 256)

        def _conn_dense(kernel_bool, x):
            w = jnp.where(kernel_bool, jnp.float32(1.0), jnp.float32(-1.0))
            return x @ w
        h = jnp.concatenate([x, -x], axis=-1)
        h = s0 * _conn_dense(k0, h)
        h = jax.nn.relu(h) * 2
        h = s1 * _conn_dense(k1, h)
        h = jax.nn.relu(h) * 2
        h = s2 * _conn_dense(k2, h)
        return h
    x = L0_attn_x
    x = _layernorm(x + _L0_attn_ref(x, L0_attn_A_log, L0_attn_Dmat, L0_attn_W_in, L0_attn_b_in, L0_attn_W_xp, L0_attn_b_xp, L0_attn_W_out, L0_attn_b_out, L0_attn_gamma, L0_attn_beta), axis=-1)
    x = _layernorm(x + _L0_ffn_ref(x, L0_ffn_gate_w, L0_ffn_gate_bias, L0_ffn_Wg, L0_ffn_Wu, L0_ffn_Wd, L0_ffn_Sg, L0_ffn_Su, L0_ffn_Sd), axis=-1)
    x = _layernorm(x + _L1_attn_ref(x, L1_attn_Wq, L1_attn_bq, L1_attn_Wk, L1_attn_bk, L1_attn_Wv, L1_attn_bv, L1_attn_Wo, L1_attn_bo), axis=-1)
    x = _layernorm(x + _L1_ffn_ref(x, L1_ffn_k0, L1_ffn_k1, L1_ffn_k2, L1_ffn_s0, L1_ffn_s1, L1_ffn_s2), axis=-1)
    return x

_drawn_inputs = setup_inputs


def setup_inputs(seed=0):
    import zlib

    import numpy as np

    out = dict(_drawn_inputs(seed))
    spreads = {'L0_attn_b_in': (0.0, 0.8),
     'L0_attn_b_xp': (0.0, 0.8),
     'L0_attn_b_out': (0.0, 2.0),
     'L0_attn_gamma': (1.0, 0.6),
     'L0_attn_beta': (0.0, 0.8)}
    factors = {'L0_attn_A_log': 8.0,
     'L0_attn_Dmat': 8.0,
     'L0_attn_W_in': 8.0,
     'L0_attn_W_xp': 8.0,
     'L0_attn_W_out': 8.0,
     'L0_ffn_gate_w': 8.0,
     'L0_ffn_gate_bias': 8.0,
     'L0_ffn_Wg': 8.0,
     'L0_ffn_Wu': 8.0,
     'L0_ffn_Wd': 8.0,
     'L0_ffn_Sg': 8.0,
     'L0_ffn_Su': 8.0,
     'L0_ffn_Sd': 8.0,
     'L1_attn_Wq': 8.0,
     'L1_attn_bq': 200.0,
     'L1_attn_Wk': 8.0,
     'L1_attn_bk': 26.173,
     'L1_attn_Wv': 8.0,
     'L1_attn_bv': 8.0,
     'L1_attn_Wo': 8.0,
     'L1_attn_bo': 2.766}
    for name, (base, spread) in spreads.items():
        noise = np.random.default_rng([zlib.crc32(name.encode()), seed]).standard_normal(out[name].shape)
        drawn = base * np.exp(spread * noise) if base else spread * noise
        out[name] = jnp.asarray(drawn.astype(out[name].dtype))
    for name, factor in factors.items():
        out[name] = (out[name] * factor).astype(out[name].dtype)
    return out
```

```python
from contextlib import ExitStack

import concourse.bass as bass
from concourse import mybir

P = 128
ALU = mybir.AluOpType
ACT = mybir.ActivationFunctionType
F32 = mybir.dt.float32
BF16 = mybir.dt.bfloat16
U8 = mybir.dt.uint8
U32 = mybir.dt.uint32
I32 = mybir.dt.int32
AX_X = mybir.AxisListType.X
EPS = 1e-5
ROUTED_SCALE = 2.5
HEADS = 16
GROUPS = 8
GROUPS_KEPT = 4
TOP_K = 8
STAGE = 9


def build(nc, x, a_log, dmat, w_in, b_in, w_xp, b_xp, w_out, b_out, gamma, beta,
          gate_w, gate_bias, w_gu, w_d, w_sh, w_shd, w_qkv, b_qk, b_v, w_o, b_o, k0, k1, k2, s012, ident, out):
    B, L, M = x.shape
    T = B * L
    NT = T // P
    TB = L // P
    S = dmat.shape[0]
    E = gate_w.shape[1]
    EG = E // GROUPS
    I2 = w_gu.shape[2]
    I = I2 // 2
    KI = 96
    BODY = 16
    NB = -(-(T * TOP_K + E * (P - 1)) // (P * BODY)) * BODY
    NPAIR = NB // 2
    AHEAD = 8
    HD = M // HEADS
    HG = 4
    GB = HEADS // HG
    NGR = B * GB
    SCALE = float(M) ** -0.5
    NP = 3
    KD = 96
    KS = KD + NP
    F = k1.shape[0]
    FC = F // P

    with ExitStack() as ctx:
        def sb(name, shape, dt=F32):
            return ctx.enter_context(nc.sbuf_tensor(name, shape, dt))

        def sem(name):
            return ctx.enter_context(nc.semaphore(name))

        xt = sb("xt", [P, NT, M])
        xT = sb("xT", [P, T])
        tmp = sb("tmp", [P, NT, M])
        xb = sb("xb", [P, NT, M])
        big = sb("big", [P, 4, T])
        zT, xpT = big[:, 0].rearrange("p (b l) -> p b l", b=B), big[:, 1].rearrange("p (b l) -> p b l", b=B)
        uT = big[:, 2, 0:T // 2].rearrange("p (b l) -> p b l", b=B // 2)
        hT = big[:, 2, T // 2:T].rearrange("p (b l) -> p b l", b=B // 2)
        ysT = big[:, 3].rearrange("p (l b) -> p l b", b=B)
        st = sb("st", [P, NT, 6])
        mv = sb("mv", [P, NT, 2])
        rstd = sb("rstd", [P, NT])
        minus_half = sb("minus_half", [P, TB])
        idf = sb("idf", [P, P])
        idb = sb("idb", [P, P], BF16)
        w_in_s = sb("w_in_s", [P, 2 * M])
        w_xp_s = sb("w_xp_s", [P, S])
        dmat_s = sb("dmat_s", [P, M])
        w_out_s = sb("w_out_s", [P, M])
        gamma_s, beta_s = sb("gamma_s", [P, 1]), sb("beta_s", [P, 1])
        b_in_s = sb("b_in_s", [P, 2])
        b_xp_s, decay = sb("b_xp_s", [P, 1]), sb("decay", [P, 1])
        b_qk_s = sb("b_qk_s", [P, 2])
        rows = sb("rows", [P, 3, M])
        bias_row = sb("bias_row", [P, E])
        gate_s = sb("gate_s", [P, E])
        sc = sb("sc", [P, NT, E])
        ch = sb("ch", [P, NT, E])
        ra = sb("ra", [P, NT, E])
        rb = sb("rb", [P, NT, E])
        gs = sb("gs", [P, NT, GROUPS])
        g1, g2 = sb("g1", [P, NT, GROUPS, 4]), sb("g2", [P, NT, GROUPS, 4])
        g3, g4 = sb("g3", [P, NT, GROUPS, 2]), sb("g4", [P, NT, GROUPS, 2])
        top = sb("top", [P, NT, 8])
        cnt = sb("cnt", [P, NT])
        before = sb("before", [P, GROUPS, GROUPS])
        keep = sb("keep", [P, NT, E])
        places = sb("places", [P, 3, E * NT], BF16)
        selb, incb, exb = (places[:, i].rearrange("p (e t) -> p e t", t=NT) for i in range(3))
        keep2 = sb("keep2", [P, E, NT], BF16)
        tri, onesb = sb("tri", [P, P], BF16), sb("onesb", [P, P], BF16)
        ones_e = sb("ones_e", [P, E])
        nblk, endb, baserow = sb("nblk", [P, E]), sb("endb", [P, E]), sb("baserow", [P, E])
        thr = sb("thr", [P, NT])
        bnum = sb("bnum", [P, 2])
        ecmp = sb("ecmp", [P, 2, E])
        eidf, eid = sb("eidf", [P, 2]), sb("eid", [P, 2], I32)
        tab = sb("tab", [1, AHEAD + 2 * P], I32)
        dst = sb("dst", [P, NT, TOP_K])
        idx = sb("idx", [P, NT, TOP_K], U32)
        wk = sb("wk", [P, NT, TOP_K])
        sg = sb("sg", [P, 2, 2, I])
        hm = sb("hm", [P, 2, 2, KI])
        hmT = sb("hmT", [P, 2, 2, P])
        xbT = sb("xbT", [P, 2, 2, P])
        wsh_s = sb("wsh_s", [P, 2 * I2])
        wshd_s = sb("wshd_s", [P, 2, M])
        w_qkv_s = sb("w_qkv_s", [P, 3 * M])
        w_o_s = sb("w_o_s", [P, M])
        kb = sb("kb", [P, 2, F], U8)
        kb1 = sb("kb1", [P, FC, F], U8)
        kb2 = sb("kb2", [P, FC, M], U8)
        s_row = sb("s_row", [P, 3])
        arena = sb("arena", [P, E * (I2 + M)])
        wgu_s = arena[:, 0:E * I2].rearrange("p (e n) -> p e n", e=E)
        wd_s = arena[:, E * I2:E * (I2 + M)].rearrange("p (e n) -> p e n", e=E)
        SH = 2 * HEADS
        half = SH * L // 2
        qst = arena[:, 0:half].bitcast(BF16).rearrange("p (h n) -> p h n", h=SH)
        kst = arena[:, half:2 * half].bitcast(BF16).rearrange("p (h n) -> p h n", h=SH)
        assert 2 * half + F + FC * (F + M) <= E * (I2 + M)
        xin = big[:, 0].rearrange("p (q j m) -> p q j m", q=4, m=M)
        ob = big[:, 1].rearrange("p (q j m) -> p q j m", q=4, m=M)
        gb = big[:, 2:4].rearrange("p a (s k m) -> p (a s) k m", k=TOP_K, m=M)
        vt = big[:, 0].rearrange("p (i m c) -> p i m c", i=NGR, m=TB)
        ot = big[:, 1].rearrange("p (t m) -> p t m", t=NT)
        otg = big[:, 1].rearrange("p (b m g c) -> p b m g c", b=B, m=TB, g=GB)
        ering = big[:, 2:4].rearrange("p a (s n) -> p (a s) n", n=L)
        h1, h2 = big[:, 0].rearrange("p (c n) -> p c n", c=FC), big[:, 1].rearrange("p (c n) -> p c n", c=FC)
        kf = arena[:, 2 * half:2 * half + F + FC * F + FC * M]
        w0 = kf[:, 0:F]
        w1 = kf[:, F:F + FC * F].rearrange("p (c n) -> p c n", c=FC)
        w2 = kf[:, F + FC * F:].rearrange("p (c n) -> p c n", c=FC)
        qf, qr, oT = (t[:].rearrange("p t e -> p (t e)").rearrange("p (o n) -> p o n", o=2) for t in (sc, ra, ch))
        parts = places[:].rearrange("p a n -> p (a n)").rearrange("p (o c n) -> p o c n", o=2, c=NP)
        vs = keep[:].rearrange("p t e -> p (t e)").rearrange("p (k m h c) -> p k m h c", k=2, m=TB, h=HG)
        mx = sb("mx", [P, 2, HG * TB])
        mr = sb("mr", [P, 2, HG * TB])
        mp = sb("mp", [P, 2, P // (HG * TB), HG * TB], BF16)
        zeros = sb("zeros", [P, 4 * M])
        mT = sb("mT", [NP * HG * TB, 2, P], BF16)
        rc = sb("rc", [P, TB, HG])

        ps = ctx.enter_context(nc.psum_tensor("ps", [P, 8, 512], F32))
        xd = nc.dram_tensor("xd", (NB * P, M), F32, kind="Internal").ap()
        od = nc.dram_tensor("od", (NB * P, M), F32, kind="Internal").ap()
        scr = nc.dram_tensor("scr", (2, NP, P, B, L), BF16, kind="Internal").ap()

        s_x = sem("s_x")
        s_w, s_we, s_wa, s_wf = sem("s_w"), sem("s_we"), sem("s_wa"), sem("s_wf")
        s_idb, s_const, s_decay = sem("s_idb"), sem("s_const"), sem("s_decay")
        s_st, s_rstd, s_v, s_p, s_xn = sem("s_st"), sem("s_rstd"), sem("s_v"), sem("s_p"), sem("s_xn")
        s_tr, s_trs = sem("s_tr"), sem("s_trs")
        s_xz, s_xzs, s_u, s_h = sem("s_xz"), sem("s_xzs"), sem("s_u"), sem("s_h")
        s_y, s_ys, s_yo, s_xb = sem("s_y"), sem("s_ys"), sem("s_yo"), sem("s_xb")
        s_lg, s_lgs, s_rw = sem("s_lg"), sem("s_lgs"), sem("s_rw")
        s_zero, s_cum, s_pos, s_idx, s_eid, s_tab, s_sc = (sem(n) for n in ("s_zero", "s_cum", "s_pos", "s_idx", "s_eid", "s_tab", "s_sc"))
        ld, stq, g_in = ([sem(f"{n}{r}") for r in range(4)] for n in ("ld", "stq", "g_in"))
        xt_ready, x_copied, g_used, s_sh = sem("xt_ready"), sem("x_copied"), sem("g_used"), sem("s_sh")
        gu_ready, sg_ready, hm_ready = sem("gu_ready"), sem("sg_ready"), sem("hm_ready")
        th_ready, th_copied, d_ready, acc_done = sem("th_ready"), sem("th_copied"), sem("d_ready"), sem("acc_done")
        s_qk, s_qks, s_part, s_pw, s_stk = sem("s_qk"), sem("s_qks"), sem("s_part"), sem("s_pw"), sem("s_stk")
        s_pad, s_vv, s_vvs = sem("s_pad"), sem("s_vv"), sem("s_vvs")
        stack_ready = sem("stack_ready")
        s1_ready, s1_free, split_done = sem("s1_ready"), sem("s1_free"), sem("split_done")
        mT_ready, mT_copied, max_in = sem("mT_ready"), sem("mT_copied"), sem("max_in")
        s2_ready, exp_ready, pv_done = sem("s2_ready"), sem("exp_ready"), sem("pv_done")
        vs_ready, o_evac, o_turn, o_norm = sem("vs_ready"), sem("o_evac"), sem("o_turn"), sem("o_norm")
        rc_done = sem("rc_done")
        s_pr, s_kf, s_f, s_fs, s_out, s_r = sem("s_pr"), sem("s_kf"), sem("s_f"), sem("s_fs"), sem("s_out"), sem("s_r")
        s_fo = sem("s_fo")

        block = ctx.enter_context(nc.Block())
        tiled = "b (t p) m -> p (b t) m"
        NDR, NDQ = NP * NP * 2, NP

        def load_stack(sp, b):
            for o, stack in enumerate((qst, kst)):
                for j in range(NP * NP):
                    part = (j % NP, j // NP)[o]
                    sp.dma_start(stack[HD * j:HD * j + HD, HEADS * (b % 2):HEADS * (b % 2) + HEADS, :],
                                 scr[o, part, :, b, :].rearrange("(h d) n -> d h n", d=HD)).then_inc(s_stk, 16)

        def stacked(sp, b):
            sp.wait_ge(s_stk, 16 * 2 * NP * NP * (b + 1))
            sp.sem_inc(stack_ready, 1)

        @block.sync
        def _(sp):
            sp.dma_start(idf[:], ident).then_inc(s_w, 16)
            for q in range(B):
                sp.dma_start(xt[:, TB * q:TB * q + TB, :], x.rearrange(tiled, p=P)[:, TB * q:TB * q + TB, :]).then_inc(s_x, 16)
                sp.wait_ge(s_x, 16 * q + 16)
            for dst, src in ((w_in_s[:], w_in), (w_xp_s[:], w_xp), (dmat_s[0:S], dmat), (dmat_s[S:2 * S], dmat),
                             (w_out_s[:], w_out), (gamma_s[:], gamma), (beta_s[:], beta), (b_in_s[:], b_in),
                             (b_xp_s[0:S], b_xp), (b_xp_s[S:2 * S], b_xp), (decay[0:S], a_log), (decay[S:2 * S], a_log),
                             (gate_s[:], gate_w), (bias_row[:], gate_bias.broadcast_to([P, E])),
                             (rows[:, 0], b_out.broadcast_to([P, M]))):
                sp.dma_start(dst, src).then_inc(s_w, 16)
            sp.wait_ge(s_const, 1)
            sp.dma_start(xd.rearrange("(p b c) m -> p b (c m)", p=P, c=4),
                         zeros[:].unsqueeze(1).broadcast_to([P, NB // 4, 4 * M])).then_inc(s_zero, 16)
            sp.dma_start(wsh_s[:], w_sh).then_inc(s_we, 16)
            sp.dma_start(wshd_s[0:I], w_shd).then_inc(s_we, 16)
            sp.dma_start(wgu_s, w_gu).then_inc(s_we, 16)
            sp.dma_start(wd_s[0:I], w_d).then_inc(s_we, 16)
            for dst, src in ((rows[:, 1], b_v.broadcast_to([P, M])), (rows[:, 2], b_o.broadcast_to([P, M])),
                             (w_qkv_s[:], w_qkv), (w_o_s[:], w_o), (b_qk_s[:], b_qk), (s_row[:], s012.broadcast_to([P, 3])),
                             (kb[:], k0.rearrange("(a p) n -> p a n", p=P)), (kb1[:], k1.rearrange("(c p) n -> p c n", p=P)),
                             (kb2[:], k2.rearrange("(c p) n -> p c n", p=P))):
                sp.dma_start(dst, src).then_inc(s_wa, 16)
            if STAGE >= 2:
                sp.wait_ge(s_eid, 1)
                sp.dma_start(tab[0:1, AHEAD:AHEAD + P], eid[:, 0:1]).then_inc(s_tab, 16)
                sp.dma_start(tab[0:1, AHEAD + P:AHEAD + NB], eid[0:NB - P, 1:2]).then_inc(s_tab, 16)
                sp.wait_ge(s_sc, 16 * NT * TOP_K)
                xq = xd.rearrange("(q j p) m -> p q j m", j=4, p=P)
                oq = od.rearrange("(q j p) m -> p q j m", j=4, p=P)
                for r in range(4):
                    sp.dma_start(xin[:, r], xq[:, r]).then_inc(ld[r], 16)

                def quads(sp, q, last=False):
                    for r in range(4):
                        if not last:
                            sp.wait_ge(xt_ready, q * 2 + (2 * r + 2))
                            sp.dma_start(xin[:, r], xq[:, bass.ds(q + (r + 4), 1)].rearrange("p a j m -> p (a j) m")).then_inc(ld[r], 16)
                        sp.wait_ge(acc_done, q * 2 + (2 * r + 4))
                        sp.dma_start(oq[:, bass.ds(q + r, 1)].rearrange("p a j m -> p (a j) m"), ob[:, r]).then_inc(stq[r], 16)

                with sp.Fori(0, NB // BODY - 1) as j:
                    quads(sp, sp.snap(j * 4))
                quads(sp, NB // 4 - 4, last=True)
            if STAGE >= 3:
                for b in range(B):
                    for o in range(2):
                        sp.wait_ge(s_part, 2 * b + o + 1)
                        sp.dma_start(scr[o, :, :, b, :].rearrange("c p n -> p c n"), parts[:, o]).then_inc(s_pw, 16)
                        sp.wait_ge(s_pw, 16 * (2 * b + o + 1))
                    if b < 2:
                        if b == 0:
                            sp.wait_ge(s_pad, 1)
                        load_stack(sp, b)
                        stacked(sp, b)
                for i in range(NGR):
                    sp.wait_ge(mT_copied, i + 1)
                    hd = HG * (i % (2 * GB))
                    for c in range(NP):
                        sp.dma_start(kst[KD + c:KD + c + 1, hd:hd + HG, :].rearrange("p h n -> p (h n)"),
                                     mT[HG * TB * c:HG * TB * c + HG * TB, i % 2, :]).then_inc(max_in, 16)
                    sp.wait_ge(max_in, 16 * NP * (i + 1))
                    for b in range(2, B):
                        if i == GB * (b - 1):
                            sp.wait_ge(s2_ready, HG * TB * i)
                            load_stack(sp, b)
                        if i == GB * (b - 1) + 1:
                            stacked(sp, b)
            sp.wait_ge(s_out, 1)
            sp.dma_start(out.rearrange(tiled, p=P), xt[:]).then_inc(s_out, 16)
            sp.wait_ge(s_out, 17)
            sp.wait_ge(s_we, 64)
            sp.wait_ge(s_zero, 16)
            sp.wait_ge(s_wa, 16 * 9)

        @block.gpsimd
        def _(pool):
            pn = [0]

            def own(ins):
                pn[0] += 1
                ins.then_inc(s_p, 1)
                pool.wait_ge(s_p, pn[0])

            own(pool.memset(minus_half[:], -0.5))
            own(pool.memset(zeros[:], 0.0))
            own(pool.memset(mp[:], 0.0))
            own(pool.memset(hm[:], 0.0))
            own(pool.memset(hmT[:], 0.0))
            own(pool.memset(keep[:], 1.0))
            own(pool.memset(keep[:, :, 0:1], 0.0))
            own(pool.memset(keep2[:], 1.0))
            own(pool.memset(keep2[:, :, 0:1], 0.0))
            own(pool.memset(tri[:], 1.0))
            own(pool.affine_select(out=tri[:], in_=tri[:], pattern=[[1, P]], compare_op=ALU.is_ge, fill=0.0, base=-1,
                                   channel_multiplier=-1))
            own(pool.memset(onesb[:], 1.0))
            own(pool.memset(ones_e[:], 1.0))
            own(pool.memset(tab[:], 0))
            own(pool.iota(thr[:], [[P, NT]], base=0, channel_multiplier=0, allow_small_or_imprecise_dtypes=True))
            own(pool.iota(bnum[:], [[P, 2]], base=0, channel_multiplier=1, allow_small_or_imprecise_dtypes=True))
            own(pool.memset(before[:], 1.0))
            own(pool.affine_select(out=before[:], in_=before[:], pattern=[[1, GROUPS], [-1, GROUPS]], compare_op=ALU.is_ge,
                                   fill=0.0, base=-1, channel_multiplier=0))
            own(pool.memset(wd_s[64:KI], 0.0))
            own(pool.memset(wshd_s[64:KI], 0.0))
            pool.sem_inc(s_const, 1)

            def rstd_of(k):
                pool.wait_ge(s_st, k + 1)
                q = k % B
                r = rstd[:, TB * q:TB * q + TB]
                own(pool.tensor_scalar(r, mv[:, TB * q:TB * q + TB, 1], EPS, None, ALU.add))
                pool.tensor_tensor(r, r, minus_half[:], ALU.pow).then_inc(s_rstd, 1)

            for q in range(B):
                rstd_of(q)
            pool.wait_ge(s_w, 16 * 16)
            own(pool.tensor_tensor(xb[:], xt[:], xt[:], ALU.add))
            pool.tensor_tensor(xb[:], xb[:], rows[:, 0:1].broadcast_to([P, NT, M]), ALU.add).then_inc(s_xb, 1)
            for q in range(B, 2 * B):
                rstd_of(q)
            if STAGE < 2:
                return
            pool.wait_ge(s_idx, 1)
            pool.wait_ge(s_zero, 16)
            pool.wait_ge(s_xn, 2 * B)
            for t in range(NT):
                for k in range(TOP_K):
                    pool.indirect_dma_start(out=xd, out_offset=bass.IndirectOffsetOnAxis(ap=idx[:, t, k:k + 1], axis=0),
                                            in_=xt[:, t], in_offset=None).then_inc(s_sc, 16)
            for r in range(4):
                pool.wait_ge(stq[r], 16 * (NB // BODY))
            for t in range(NT):
                if t >= 4:
                    pool.wait_ge(g_used, t - 3)
                for k in range(TOP_K):
                    pool.indirect_dma_start(out=gb[:, t % 4, k], out_offset=None, in_=od,
                                            in_offset=bass.IndirectOffsetOnAxis(ap=idx[:, t, k:k + 1], axis=0)).then_inc(g_in[t % 4], 16)
            for q in range(2 * B, 3 * B):
                rstd_of(q)
            if STAGE >= 3:
                pool.wait_ge(s_xn, 3 * B)
                pool.wait_ge(s_wa, 16 * 9)
                own(pool.memset(qst[64:P], 0.0))
                own(pool.memset(kst[64:P], 0.0))
                own(pool.memset(qst[KD:P], 1.0))
                pool.sem_inc(s_pad, 1)
                own(pool.memset(vs[:], 0.0))
                own(pool.memset(vs[:, :, :, :, HD:HD + 1], 1.0))
                own(pool.tensor_tensor(xb[:], xt[:], rows[:, 2:3].broadcast_to([P, NT, M]), ALU.add))
                pool.sem_inc(s_xb, 1)

                def stage_values(i, k):
                    pool.wait_ge(pv_done, TB * i + 2 - TB) if not (isinstance(i, int) and i < 2) else None
                    pool.tensor_tensor(vs[:, k, :, :, 0:HD], vt[:, bass.ds(i, 1)].rearrange("p a m (h d) -> p (a m) h d", h=HG),
                                       zeros[:, 0:TB * HG * HD].rearrange("p (m h d) -> p m h d", m=TB, h=HG), ALU.add).then_inc(vs_ready, 1)

                def split_max(i, k):
                    pool.wait_ge(s1_free, 2 * HG * i + (2 * HG + 2))
                    if not (isinstance(i, int) and i < 2):
                        pool.wait_ge(mT_ready, i - 1)
                    nm, r = mx[:, k], mr[:, k]
                    pool.tensor_tensor(r, zeros[:, 0:HG * TB], nm, ALU.subtract).then_inc(s_r, 1)
                    pool.wait_ge(s_r, 5 * i + 1)
                    pool.tensor_tensor(mp[:, k, 0], r, zeros[:, 0:HG * TB], ALU.add).then_inc(s_r, 1)
                    pool.wait_ge(s_r, 5 * i + 2)
                    pool.tensor_tensor(r, r, mp[:, k, 0], ALU.subtract).then_inc(s_r, 1)
                    pool.wait_ge(s_r, 5 * i + 3)
                    pool.tensor_tensor(mp[:, k, 1], r, zeros[:, 0:HG * TB], ALU.add).then_inc(s_r, 1)
                    pool.wait_ge(s_r, 5 * i + 4)
                    pool.tensor_tensor(r, r, mp[:, k, 1], ALU.subtract).then_inc(s_r, 1)
                    pool.wait_ge(s_r, 5 * i + 5)
                    pool.tensor_tensor(mp[:, k, 2], r, zeros[:, 0:HG * TB], ALU.add).then_inc(split_done, 1)

                pool.wait_ge(s_vvs, B)
                stage_values(0, 0)
                split_max(0, 0)

                def pool_group(i, k):
                    if not isinstance(i, int) or i + 1 < NGR:
                        split_max(i + 1, 1 - k)
                        stage_values(i + 1, 1 - k)

                pool_group(0, 0)
                pool_group(1, 1)
                with pool.Fori(1, NGR // 2 - 1) as j:
                    i = pool.snap(j * 2)
                    pool_group(i, 0)
                    pool_group(i + 1, 1)
                pool_group(NGR - 2, 0)
                pool_group(NGR - 1, 1)
                for q in range(3 * B, (5 if STAGE > 3 else 4) * B):
                    rstd_of(q)

        @block.scalar
        def _(act):
            act.wait_ge(s_w, 16 * 16)
            act.activation(decay[:], decay[:], ACT.Exp).then_inc(s_decay, 1)
            act.wait_ge(s_decay, 1)
            act.activation(decay[:], decay[:], ACT.Exp, scale=-1.0).then_inc(s_decay, 1)
            act.activation(idb[:], idf[:], ACT.Copy).then_inc(s_idb, 1)

            def turned(k, dst, **how):
                act.wait_ge(s_tr, k + 1)
                act.activation(dst, ps[:, k % B, :], ACT.Identity, **how).then_inc(s_trs, 1)

            for b in range(B):
                turned(b, xT[:, L * b:L * b + L], scale=gamma_s[:], bias=beta_s[:])
            for b in range(B):
                for o, (dst, f) in enumerate(((xpT, ACT.Silu), (zT, ACT.Sigmoid))):
                    act.wait_ge(s_xz, 2 * b + o + 1)
                    act.activation(dst[:, b], ps[:, 4 + (2 * b + o) % 4, :], f, bias=b_in_s[:, o:o + 1]).then_inc(s_xzs, 1)
            for b in range(B):
                turned(B + b, xT[:, L * b:L * b + L])
            for a in range(2):
                act.wait_ge(s_lg, a + 1)
                act.activation(sc[:, NT // 2 * a:NT // 2 * (a + 1), :], ps[:, 4 + a, :].rearrange("p (t e) -> p t e", e=E),
                               ACT.Sigmoid).then_inc(s_lgs, 1)
            if STAGE < 2:
                return
            for t in range(NT + 2):
                if t < NT:
                    act.wait_ge(gu_ready, t + 1)
                    act.activation(sg[:, t % 2], ps[:, 2 + t % 2, 0:I2].rearrange("p (a i) -> p a i", a=2), ACT.Silu).then_inc(sg_ready, 1)
                if 1 <= t <= NT:
                    act.wait_ge(th_ready, t)
                    act.activation(hmT[0:KI, (t - 1) % 2], ps[0:KI, 4 + (t - 1) % 2, 0:2 * P].rearrange("p (a i) -> p a i", a=2), ACT.Copy).then_inc(th_copied, 1)

            def act_pair(s, u):
                if not isinstance(s, int) or 1 <= s <= NPAIR:
                    act.wait_ge(gu_ready, s + NT)
                    act.activation(sg[:, (u - 1) % 2], ps[:, 2 + (u - 1) % 2, 0:2 * I2].rearrange("p (a i) -> p a i", a=2)[:, :, 0:I],
                                   ACT.Silu).then_inc(sg_ready, 1)
                if not isinstance(s, int) or 2 <= s <= NPAIR + 1:
                    act.wait_ge(th_ready, s + (NT - 1))
                    act.activation(hmT[0:KI, u % 2], ps[0:KI, 4 + u % 2, 0:2 * P].rearrange("p (a i) -> p a i", a=2), ACT.Copy).then_inc(th_copied, 1)

            for u in range(8):
                act_pair(u, u)
            with act.Fori(1, NB // BODY) as j:
                s0 = act.snap(j * 8)
                for u in range(8):
                    act_pair(s0 + u, u)
            for u in range(3):
                act_pair(NPAIR + u, u)
            for b in range(B):
                turned(2 * B + b, xT[:, L * b:L * b + L])
            if STAGE < 3:
                return
            for b in range(B):
                for o in range(2):
                    act.wait_ge(s_qk, 2 * b + o + 1)
                    if b >= 1:
                        act.wait_ge(s_part, 2 * (b - 1) + o + 1)
                        act.wait_ge(s_pw, 16 * (2 * (b - 1) + o + 1))
                    act.activation(parts[:, o, 0], ps[:, 4 + o, :], ACT.Identity, bias=b_qk_s[:, o:o + 1])
                    act.activation(qf[:, o], ps[:, 4 + o, :], ACT.Identity, bias=b_qk_s[:, o:o + 1]).then_inc(s_qks, 1)

            def exps(i, mt):
                for h in range(HG):
                    act.wait_ge(s2_ready, HG * TB * i + (HG * mt + h + 1))
                    if h == 0:
                        act.wait_ge(pv_done, TB * i + (mt + 1))
                    act.activation(ering[:, HG * (mt % 2) + h], ps[:, 4 + h % 2, :], ACT.Exp, scale=SCALE).then_inc(exp_ready, 1)

            def act_group(i, k):
                for mt in range(1, TB):
                    exps(i, mt)
                if not isinstance(i, int) or i + 1 < NGR:
                    exps(i + 1, 0)
                act.wait_ge(pv_done, TB * i + (TB + 2))
                if not isinstance(i, int) or i >= 2:
                    act.wait_ge(o_turn, i - 1)
                act.activation(oT[:, k], ps[:, 6, :], ACT.Copy).then_inc(o_evac, 1)

            exps(0, 0)
            act_group(0, 0)
            act_group(1, 1)
            with act.Fori(1, NGR // 2 - 1) as j:
                i = act.snap(j * 2)
                act_group(i, 0)
                act_group(i + 1, 1)
            act_group(NGR - 2, 0)
            act_group(NGR - 1, 1)
            for b in range(B):
                turned(3 * B + b, xT[:, L * b:L * b + L])
            if STAGE < 4:
                return
            for b in range(B):
                turned(4 * B + b, xT[:, L * b:L * b + L])
            act.wait_ge(s_kf, 1)
            for b in range(B):
                for layer, dst in enumerate((h1, h2)):
                    for c in range(FC):
                        n = (2 * b + layer) * FC + c
                        act.wait_ge(s_f, n + 1)
                        act.activation(dst[:, c], ps[:, c, :], ACT.Relu, scale=s_row[:, layer:layer + 1]).then_inc(s_fs, 1)

        @block.vector
        def _(v):
            vn = [0]

            def own(ins):
                vn[0] += 1
                ins.then_inc(s_v, 1)
                v.wait_ge(s_v, vn[0])

            def stats(src, q):
                for t in range(TB * q, TB * q + TB):
                    ins = v.bn_stats(st[:, t], src[:, t])
                own(ins)
                for t in range(TB * q, TB * q + TB):
                    ins = v.bn_aggr(mv[:, t], st[:, t])
                ins.then_inc(s_st, 1)

            def normalise(dst, src, k):
                q = k % B
                v.wait_ge(s_rstd, k + 1)
                v.wait_ge(s_st, k + 1)
                for t in range(TB * q, TB * q + TB):
                    ins = v.tensor_scalar(dst[:, t], src[:, t], mv[:, t, 0:1], rstd[:, t:t + 1], ALU.subtract, ALU.mult)
                ins.then_inc(s_xn, 1)

            own(v.memset(cnt[:, 0:2], 0.0))
            v.sem_inc(acc_done, 2)
            v.sem_inc(s1_free, 2)
            v.sem_inc(exp_ready, 2)
            v.sem_inc(pv_done, 2)
            for q in range(B):
                v.wait_ge(s_x, 16 * q + 16)
                stats(xt, q)
            for q in range(B):
                normalise(tmp, xt, q)
            v.wait_ge(s_w, 16 * 16)
            v.wait_ge(s_decay, 2)
            for j in range(B // 2):
                v.wait_ge(s_u, 2 * j + 2)
                own(v.tensor_scalar(uT[:, j], ps[:, j, :], b_xp_s[:], None, ALU.add))
                v.tensor_tensor_scan(hT[:, j], decay[:].broadcast_to([P, L]), uT[:, j], 0.0, ALU.mult, ALU.add).then_inc(s_h, 1)
            for b in range(B):
                v.wait_ge(s_y, b + 1)
                v.wait_ge(s_xzs, 2 * b + 2)
                v.tensor_tensor(ysT[:, :, b], ps[:, 4 + b, :], zT[:, b], ALU.mult).then_inc(s_ys, 1)
            v.wait_ge(s_xb, 1)

            def add_and_norm(k0_, s_in, bank, res):
                for q in range(B):
                    v.wait_ge(s_in, q + 1)
                    own(v.tensor_tensor(tmp[:, TB * q:TB * q + TB], ps[:, bank + q].rearrange("p (t m) -> p t m", m=M),
                                        res[:, TB * q:TB * q + TB], ALU.add))
                    stats(tmp, q)
                for q in range(B):
                    normalise(xt, tmp, k0_ + q)

            add_and_norm(B, s_yo, 0, xb)

            v.wait_ge(s_const, 1)
            v.wait_ge(s_lgs, 2)
            own(v.tensor_tensor(ch[:], sc[:], bias_row[:].unsqueeze(1).broadcast_to([P, NT, E]), ALU.add))
            c4 = ch[:].rearrange("p t (g a) -> p t g a", a=EG)
            v.tensor_tensor(g1[:], c4[:, :, :, 0:4], c4[:, :, :, 4:8], ALU.max)
            own(v.tensor_tensor(g2[:], c4[:, :, :, 0:4], c4[:, :, :, 4:8], ALU.min))
            r4, q4 = ra[:, :, 0:2 * GROUPS].rearrange("p t (g a) -> p t g a", a=2), rb[:, :, 0:2 * GROUPS].rearrange("p t (g a) -> p t g a", a=2)
            v.tensor_tensor(g3[:], g1[:, :, :, 0:2], g1[:, :, :, 2:4], ALU.max)
            v.tensor_tensor(r4, g1[:, :, :, 0:2], g1[:, :, :, 2:4], ALU.min)
            own(v.tensor_tensor(q4, g2[:, :, :, 0:2], g2[:, :, :, 2:4], ALU.max))
            own(v.tensor_tensor(g4[:], r4, q4, ALU.max))
            first, second, third = ra[:, :, 32:40], ra[:, :, 40:48], ra[:, :, 48:56]
            v.tensor_tensor(first, g3[:, :, :, 0], g3[:, :, :, 1], ALU.max)
            v.tensor_tensor(second, g3[:, :, :, 0], g3[:, :, :, 1], ALU.min)
            own(v.tensor_tensor(third, g4[:, :, :, 0], g4[:, :, :, 1], ALU.max))
            own(v.tensor_tensor(second, second, third, ALU.max))
            own(v.tensor_tensor(gs[:], first, second, ALU.add))
            a4 = ra[:].rearrange("p t (g j) -> p t g j", j=GROUPS)
            b4 = rb[:].rearrange("p t (g j) -> p t g j", j=GROUPS)
            other = gs[:].unsqueeze(2).broadcast_to([P, NT, GROUPS, GROUPS])
            mine = gs[:].unsqueeze(3).broadcast_to([P, NT, GROUPS, GROUPS])
            v.tensor_tensor(a4, other, mine, ALU.is_gt)
            own(v.tensor_tensor(b4, other, mine, ALU.is_equal))
            own(v.tensor_tensor(b4, b4, before[:].unsqueeze(1).broadcast_to([P, NT, GROUPS, GROUPS]), ALU.mult))
            own(v.tensor_tensor(ra[:], ra[:], rb[:], ALU.add))
            own(v.tensor_reduce(gs[:], a4, AX_X, ALU.add))
            own(v.tensor_scalar(gs[:], gs[:], float(GROUPS_KEPT), None, ALU.is_lt))
            own(v.tensor_tensor(c4, c4, gs[:].unsqueeze(3).broadcast_to([P, NT, GROUPS, EG]), ALU.mult))
            for t in range(NT):
                ins = v.max(top[:, t], ch[:, t])
            own(ins)
            eighth = top[:, :, 7:8].broadcast_to([P, NT, E])
            v.tensor_tensor(ra[:], ch[:], eighth, ALU.is_gt)
            own(v.tensor_tensor(rb[:], ch[:], eighth, ALU.is_equal))
            own(v.tensor_reduce(cnt[:], ra[:], AX_X, ALU.add))
            own(v.tensor_scalar(cnt[:], cnt[:], -1.0, float(TOP_K), ALU.mult, ALU.add))
            own(v.tensor_tensor_scan(ch[:].rearrange("p t e -> p (t e)"), keep[:].rearrange("p t e -> p (t e)"),
                                     rb[:].rearrange("p t e -> p (t e)"), 0.0, ALU.mult, ALU.add))
            own(v.tensor_tensor(ch[:], ch[:], cnt[:].unsqueeze(2).broadcast_to([P, NT, E]), ALU.is_le))
            own(v.tensor_tensor(rb[:], rb[:], ch[:], ALU.mult))
            own(v.tensor_tensor(ra[:], ra[:], rb[:], ALU.add))
            own(v.tensor_copy(selb.rearrange("p e t -> p t e"), ra[:]))
            own(v.tensor_tensor_scan(incb.rearrange("p e t -> p (e t)"), keep2[:].rearrange("p e t -> p (e t)"),
                                     selb.rearrange("p e t -> p (e t)"), 0.0, ALU.mult, ALU.add))
            v.tensor_tensor(exb, incb, selb, ALU.subtract).then_inc(s_cum, 1)
            v.wait_ge(s_pos, 1)
            own(v.tensor_tensor(rb[:].rearrange("p t e -> p (t e)").rearrange("p (e j) -> p e j", j=NT),
                                ps[:, 2, 0:E].unsqueeze(2).broadcast_to([P, E, NT]), thr[:].unsqueeze(1).broadcast_to([P, E, NT]), ALU.is_gt))
            own(v.tensor_reduce(nblk[:], rb[:].rearrange("p t e -> p (t e)").rearrange("p (e j) -> p e j", j=NT), AX_X, ALU.add))
            own(v.tensor_tensor_scan(endb[:], ones_e[:], nblk[:], 0.0, ALU.mult, ALU.add))
            own(v.tensor_tensor(baserow[:], endb[:], nblk[:], ALU.subtract))
            own(v.tensor_scalar(baserow[:], baserow[:], float(P), 1.0, ALU.mult, ALU.add))
            own(v.tensor_tensor(ch[:].rearrange("p t e -> p e t"), ps[:, 0:2].rearrange("p a (e t) -> p (a e) t", t=NT),
                                baserow[:].unsqueeze(2).broadcast_to([P, E, NT]), ALU.add))
            own(v.tensor_tensor(ch[:], ch[:], ra[:], ALU.mult))
            for t in range(NT):
                ins = v.max(dst[:, t], ch[:, t])
            own(ins)
            v.tensor_scalar(idx[:], dst[:], -1.0, None, ALU.add).then_inc(s_idx, 1)
            for c in range(2):
                ins = v.tensor_scalar(ecmp[:, c], endb[:], bnum[:, c:c + 1], None, ALU.is_le)
            own(ins)
            own(v.tensor_reduce(eidf[:], ecmp[:], AX_X, ALU.add))
            v.tensor_scalar(eid[:], eidf[:], float(E - 1), None, ALU.min).then_inc(s_eid, 1)
            own(v.tensor_tensor(ra[:], ra[:], sc[:], ALU.mult))
            own(v.tensor_reduce(cnt[:], ra[:], AX_X, ALU.add))
            own(v.tensor_scalar(cnt[:], cnt[:], 1e-20, None, ALU.add))
            own(v.reciprocal(cnt[:], cnt[:]))
            own(v.tensor_scalar(cnt[:], cnt[:], ROUTED_SCALE, None, ALU.mult))
            own(v.tensor_tensor(rb[:], ra[:], cnt[:].unsqueeze(2).broadcast_to([P, NT, E]), ALU.mult))
            if STAGE < 2:
                v.wait_ge(s_xn, 2 * B)
                v.sem_inc(s_out, 1)
                return
            for t in range(NT + 2):
                if t < NT:
                    v.wait_ge(sg_ready, t + 1)
                    v.tensor_tensor(hm[:, t % 2, :, 0:I], sg[:, t % 2], ps[:, 2 + t % 2, I2:2 * I2].rearrange("p (a i) -> p a i", a=2),
                                    ALU.mult).then_inc(hm_ready, 1)
                if t >= 2:
                    v.wait_ge(d_ready, t - 1)
                    v.tensor_tensor(xb[:, t - 2], ps[:, 6 + t % 2, 0:M], xt[:, t - 2], ALU.add).then_inc(s_sh, 1)
            for k in range(TOP_K):
                own(v.tensor_tensor(ra[:], ch[:], dst[:, :, k:k + 1].broadcast_to([P, NT, E]), ALU.is_equal))
                own(v.tensor_tensor(ra[:], ra[:], rb[:], ALU.mult))
                own(v.tensor_reduce(wk[:, :, k], ra[:], AX_X, ALU.add))

            def dve_pair(s, u, earlier=0):
                static = isinstance(s, int)
                if not static or s < NPAIR:
                    v.wait_ge(xt_ready, s + 1)
                    v.tensor_copy(xbT[:, u % 2], ps[:, u % 2, 0:2 * P].rearrange("p (a m) -> p a m", a=2)).then_inc(x_copied, 1)
                if not static or 1 <= s <= NPAIR:
                    v.wait_ge(sg_ready, s + NT)
                    v.tensor_tensor(hm[:, (u - 1) % 2, :, 0:I], sg[:, (u - 1) % 2],
                                    ps[:, 2 + (u - 1) % 2, 0:2 * I2].rearrange("p (a i) -> p a i", a=2)[:, :, I:I2], ALU.mult).then_inc(hm_ready, 1)
                if not static or 3 <= s:
                    quad, part = (u - 3) // 2 % 4, (u - 3) % 2
                    if part == 0 and (not static or s >= 11):
                        v.wait_ge(stq[quad], 16 * ((s - 3) // 8) if static else earlier * 16 + (32 if u >= 3 else 16))
                    v.wait_ge(d_ready, s + (NT - 2))
                    v.tensor_copy(ob[:, quad, 2 * part:2 * part + 2], ps[:, 6 + (u - 3) % 2, 0:2 * M].rearrange("p (a m) -> p a m", a=2)).then_inc(acc_done, 1)

            for u in range(8):
                dve_pair(u, u)
            for u in range(8):
                dve_pair(8 + u, u)
            with v.Fori(0, NB // BODY - 2) as j:
                s0 = v.snap(j * 8 + 16)
                for u in range(8):
                    dve_pair(s0 + u, u, j)
            for u in range(3):
                dve_pair(NPAIR + u, u)
            for t in range(NT):
                v.wait_ge(g_in[t % 4], 16 * TOP_K * (t // 4 + 1))
                own(v.tensor_tensor(gb[:, t % 4], gb[:, t % 4], wk[:, t, :].unsqueeze(2).broadcast_to([P, TOP_K, M]), ALU.mult))
                own(v.tensor_reduce(tmp[:, t], gb[:, t % 4].rearrange("p k m -> p m k"), AX_X, ALU.add))
                v.sem_inc(g_used, 1)
                own(v.tensor_tensor(tmp[:, t], tmp[:, t], xb[:, t], ALU.add))
            for q in range(B):
                stats(tmp, q)
            for q in range(B):
                normalise(xt, tmp, 2 * B + q)
            if STAGE < 3:
                v.wait_ge(s_xn, 3 * B)
                v.sem_inc(s_out, 1)
                return
            v.wait_ge(s_wa, 16 * 9)
            for b in range(B):
                v.wait_ge(s_vv, b + 1)
                v.tensor_tensor(vt[:, GB * b:GB * b + GB].rearrange("p g m c -> p m g c"),
                                ps[:, 6].rearrange("p (m g c) -> p m g c", m=TB, g=GB),
                                rows[:, 1:2].rearrange("p a (g c) -> p a g c", g=GB).broadcast_to([P, TB, GB, HG * HD]),
                                ALU.add).then_inc(s_vvs, 1)
                for o in range(2):
                    v.wait_ge(s_qks, 2 * b + o + 1)
                    own(v.tensor_tensor(qr[:, o], qf[:, o], parts[:, o, 0], ALU.subtract))
                    own(v.tensor_copy(parts[:, o, 1], qr[:, o]))
                    v.tensor_tensor(parts[:, o, 2], qr[:, o], parts[:, o, 1], ALU.subtract).then_inc(s_part, 1)

            def row_max(i, k, h):
                if h == 0 and not (isinstance(i, int) and i < 2):
                    v.wait_ge(split_done, i - 1)
                for a in range(2):
                    v.wait_ge(s1_ready, 2 * HG * i + (2 * h + a + 1))
                    v.tensor_reduce(mx[:, k, TB * h + 2 * a:TB * h + 2 * a + 2], ps[:, 2 * a:2 * a + 2, :], AX_X,
                                    ALU.max).then_inc(s1_free, 1)

            def copy_max(i, k):
                v.wait_ge(mT_ready, i + 1)
                if not (isinstance(i, int) and i < 2):
                    v.wait_ge(max_in, 16 * NP * i - 16 * NP)
                v.tensor_copy(mT[:, k], ps[0:NP * HG * TB, 7, 0:P // 2].bitcast(BF16)).then_inc(mT_copied, 1)

            def norm_out(i, k):
                v.wait_ge(o_turn, i + 1)
                turnedv = ps[:, 7].rearrange("p (m h c) -> p m h c", m=TB, h=HG)
                v.reciprocal(rc[:], turnedv[:, :, :, HD]).then_inc(rc_done, 1)
                v.wait_ge(rc_done, i + 1)
                dst = otg[:, bass.ds(i // GB, 1), :, bass.ds(i % GB, 1), :].rearrange("p b m g (h c) -> p (b m) (g h) c", h=HG)
                v.tensor_tensor(dst, turnedv[:, :, :, 0:HD], rc[:].unsqueeze(3).broadcast_to([P, TB, HG, HD]),
                                ALU.mult).then_inc(o_norm, 1)

            own(v.tensor_tensor(w0, kb[:, 0], kb[:, 1], ALU.subtract))
            v.tensor_scalar(w0, w0, 2.0, None, ALU.mult)
            v.tensor_scalar(w1, kb1[:], 2.0, -1.0, ALU.mult, ALU.add)
            v.tensor_scalar(w2, kb2[:], 2.0, -1.0, ALU.mult, ALU.add)
            v.tensor_scalar(s_row[:, 0:2], s_row[:, 0:2], 2.0, None, ALU.mult).then_inc(s_kf, 1)

            def dve_group(i, k):
                ahead = not isinstance(i, int) or i + 2 < NGR
                after = not isinstance(i, int) or i + 1 < NGR
                for h in range(HG):
                    if ahead:
                        row_max(i + 2, k, h)
                    if h == 0 and after:
                        copy_max(i + 1, 1 - k)
                if not isinstance(i, int) or i >= 1:
                    norm_out(i - 1, 1 - k)

            for h in range(HG):
                row_max(0, 0, h)
            copy_max(0, 0)
            for h in range(HG):
                row_max(1, 1, h)
            dve_group(0, 0)
            dve_group(1, 1)
            with v.Fori(1, NGR // 2 - 1) as j:
                i = v.snap(j * 2)
                dve_group(i, 0)
                dve_group(i + 1, 1)
            dve_group(NGR - 2, 0)
            dve_group(NGR - 1, 1)
            norm_out(NGR - 1, 1)
            v.wait_ge(s_xb, 2)
            add_and_norm(3 * B, s_pr, 4, xb)
            if STAGE < 4:
                v.wait_ge(s_xn, 4 * B)
                v.sem_inc(s_out, 1)
                return
            for q in range(B):
                v.wait_ge(s_fo, q + 1)
                own(v.scalar_tensor_tensor(out=tmp[:, TB * q:TB * q + TB], in0=ps[:, 4 + q].rearrange("p (t m) -> p t m", m=M),
                                           scalar=s_row[:, 2:3], in1=xt[:, TB * q:TB * q + TB], op0=ALU.mult, op1=ALU.add))
                stats(tmp, q)
                normalise(xt, tmp, 4 * B + q)
            v.wait_ge(s_xn, 5 * B)
            v.sem_inc(s_out, 1)

        @block.tensor
        def _(pe):
            pe.wait_ge(s_w, 16)

            def turn(k, src):
                if k >= B:
                    pe.wait_ge(s_trs, k - B + 1)
                for t in range(TB):
                    ins = pe.transpose(ps[:, k % B, P * t:P * t + P], src(TB * (k % B) + t), idf[:])
                ins.then_inc(s_tr, 1)

            for b in range(B):
                pe.wait_ge(s_xn, b + 1)
                turn(b, lambda t: tmp[:, t])
            pe.wait_ge(s_w, 16 * 16)
            for b in range(B):
                pe.wait_ge(s_trs, b + 1)
                for o in range(2):
                    n = 2 * b + o
                    if n >= 4:
                        pe.wait_ge(s_xzs, n - 3)
                    pe.matmul(ps[:, 4 + n % 4, :], w_in_s[:, M * o:M * o + M], xT[:, L * b:L * b + L],
                              start=True, stop=True).then_inc(s_xz, 1)
            for b in range(B):
                pe.wait_ge(s_xzs, 2 * b + 1)
                h = S * (b % 2)
                pe.matmul(ps[h:h + S, b // 2, :], w_xp_s[:], xpT[:, b], start=True, stop=True).then_inc(s_u, 1)
            pe.wait_ge(s_xzs, 2 * B)
            for b in range(B):
                pe.wait_ge(s_h, b // 2 + 1)
                h = S * (b % 2)
                pe.matmul(ps[:, 4 + b, :], dmat_s[h:h + S], hT[h:h + S, b // 2], start=True, stop=True).then_inc(s_y, 1)
            pe.wait_ge(s_ys, B)
            for q in range(B):
                for t in range(TB):
                    l = (TB * q + t) * P // B
                    ins = pe.matmul(ps[:, q, P * t:P * t + P], ysT[:, l:l + P // B, :].rearrange("p l b -> p (l b)"), w_out_s[:],
                                    start=True, stop=True)
                ins.then_inc(s_yo, 1)
            for b in range(B):
                pe.wait_ge(s_xn, B + b + 1)
                turn(B + b, lambda t: xt[:, t])
            for t in range(NT):
                if t % TB == 0:
                    pe.wait_ge(s_trs, B + t // TB + 1)
                ins = pe.matmul(ps[:, 4 + t // 8, E * (t % 8):E * (t % 8) + E], xT[:, P * t:P * t + P], gate_s[:],
                                start=True, stop=True)
                if t % 8 == 7:
                    ins.then_inc(s_lg, 1)
            if STAGE < 2:
                return
            pe.wait_ge(s_cum, 1)
            pe.wait_ge(s_const, 1)
            flat_sel, flat_ex = selb.rearrange("p e t -> p (e t)"), exb.rearrange("p e t -> p (e t)")
            for a in range(2):
                pe.matmul(ps[:, a, :], tri[:], flat_sel[:, 512 * a:512 * a + 512], start=True, stop=False)
                pe.matmul(ps[:, a, :], onesb[:], flat_ex[:, 512 * a:512 * a + 512], start=False, stop=True)
            pe.matmul(ps[:, 2, 0:E], onesb[:], incb[:, :, NT - 1], start=True, stop=True).then_inc(s_pos, 1)
            pe.wait_ge(s_we, 64)
            pe.wait_ge(s_lgs, 2)
            pe.wait_ge(s_idx, 1)
            for t in range(NT + 2):
                if t < NT:
                    pe.matmul(ps[:, 2 + t % 2, 0:2 * I2], xT[:, P * t:P * t + P], wsh_s[:], start=True, stop=True).then_inc(gu_ready, 1)
                if 1 <= t <= NT:
                    pe.wait_ge(hm_ready, t)
                    for a in range(2):
                        ins = pe.transpose(ps[0:KI, 4 + (t - 1) % 2, P * a:P * a + P], hm[:, (t - 1) % 2, a], idf[:])
                    ins.then_inc(th_ready, 1)
                if t >= 2:
                    pe.wait_ge(th_copied, t - 1)
                    if t >= 4:
                        pe.wait_ge(s_sh, t - 3)
                    for a in range(2):
                        ins = pe.matmul(ps[:, 6 + t % 2, 0:M], hmT[0:KI, t % 2, a], wshd_s[0:KI, a], start=(a == 0), stop=(a == 1))
                    ins.then_inc(d_ready, 1)

            def pe_pair(s, u, expert):
                static = isinstance(s, int)
                if not static or s < NPAIR:
                    quad, part = u // 2, u % 2
                    if part == 0:
                        pe.wait_ge(ld[quad], 16 * (s // 8) + 16 if static else s // 8 * 16 + 16)
                    for a in range(2):
                        ins = pe.transpose(ps[:, u % 2, P * a:P * a + P], xin[:, quad, 2 * part + a], idf[:])
                    ins.then_inc(xt_ready, 1)
                if not static or 1 <= s <= NPAIR:
                    pe.wait_ge(x_copied, s + 0)
                    for a in range(2):
                        ins = pe.matmul(ps[:, 2 + (u - 1) % 2, I2 * a:I2 * a + I2], xbT[:, (u - 1) % 2, a],
                                        wgu_s[:, bass.ds(expert(2 * (u - 1) + a), 1), :].rearrange("p a n -> p (a n)"), start=True, stop=True)
                    ins.then_inc(gu_ready, 1)
                if not static or 2 <= s <= NPAIR + 1:
                    pe.wait_ge(hm_ready, s + (NT - 1))
                    for a in range(2):
                        ins = pe.transpose(ps[0:KI, 4 + u % 2, P * a:P * a + P], hm[:, u % 2, a], idf[:])
                    ins.then_inc(th_ready, 1)
                if not static or 3 <= s:
                    pe.wait_ge(th_copied, s + (NT - 2))
                    pe.wait_ge(acc_done, s - 2)
                    for a in range(2):
                        ins = pe.matmul(ps[:, 6 + (u - 3) % 2, M * a:M * a + M], hmT[0:KI, (u - 3) % 2, a],
                                        wd_s[0:KI, bass.ds(expert(2 * (u - 3) + a), 1), :].rearrange("p a n -> p (a n)"), start=True, stop=True)
                    ins.then_inc(d_ready, 1)

            def experts_of(first, blocks):
                _, got = nc.values_load_multi_w_load_instructions(
                    tab[0:1, bass.ds(first + (AHEAD + blocks[0]), len(blocks))], engines=[mybir.EngineType.PE],
                    min_val=0, max_val=E - 1, skip_runtime_bounds_check_because="the table holds minima with E - 1")
                return lambda b: got[b - blocks[0]]

            pe.wait_ge(s_tab, 32)
            pe.wait_ge(s_sh, NT)
            chosen = experts_of(0, range(-6, 14))
            for u in range(8):
                pe_pair(u, u, chosen)
            with pe.Fori(1, NB // BODY) as j:
                chosen = experts_of(j * BODY, range(-6, 14))
                s0 = pe.snap(j * 8)
                for u in range(8):
                    pe_pair(s0 + u, u, chosen)
            chosen = experts_of(NB, range(-6, 2))
            for u in range(3):
                pe_pair(NPAIR + u, u, chosen)
            for b in range(B):
                pe.wait_ge(s_xn, 2 * B + b + 1)
                turn(2 * B + b, lambda t: xt[:, t])
            if STAGE < 3:
                return
            pe.wait_ge(s_wa, 16 * 9)
            pe.wait_ge(s_idb, 1)
            for b in range(B):
                pe.wait_ge(s_trs, 2 * B + b + 1)
                for o in range(2):
                    if b >= 1:
                        pe.wait_ge(s_qks, 2 * (b - 1) + o + 1)
                    pe.matmul(ps[:, 4 + o, :], w_qkv_s[:, M * o:M * o + M], xT[:, L * b:L * b + L],
                              start=True, stop=True).then_inc(s_qk, 1)
                if b >= 1:
                    pe.wait_ge(s_vvs, b)
                for t in range(TB):
                    ins = pe.matmul(ps[:, 6, P * t:P * t + P], xT[:, L * b + P * t:L * b + P * t + P], w_qkv_s[:, 2 * M:3 * M],
                                    start=True, stop=True)
                ins.then_inc(s_vv, 1)

            def head(i, h):
                if isinstance(i, int):
                    return slice(HG * (i % (2 * GB)) + h, HG * (i % (2 * GB)) + h + 1)
                return bass.ds(i % (2 * GB) * HG + h, 1)

            def flat(ap):
                return ap.rearrange("p a n -> p (a n)")

            def max_scores(i, h, c):
                if c % 2 == 0:
                    pe.wait_ge(s1_free, 2 * HG * i + (2 * h + c // 2 + 1))
                ins = pe.matmul(ps[:, c, :], flat(kst[0:KD, head(i, h), P * c:P * c + P]), flat(qst[0:KD, head(i, h), :]),
                                start=True, stop=True)
                if c % 2:
                    ins.then_inc(s1_ready, 1)

            def scores(i, mt, h):
                if mt == 0 and h == 0:
                    pe.wait_ge(max_in, 16 * NP * i + 16 * NP)
                pe.wait_ge(exp_ready, HG * TB * i + (HG * mt + h + 1))
                pe.matmul(ps[:, 4 + h % 2, :], flat(qst[0:KS, head(i, h), P * mt:P * mt + P]), flat(kst[0:KS, head(i, h), :]),
                          start=True, stop=True).then_inc(s2_ready, 1)

            def values(i, k, mt):
                if mt == 0:
                    pe.wait_ge(vs_ready, i + 1)
                    if not isinstance(i, int) or i >= 1:
                        pe.wait_ge(o_evac, i)
                pe.wait_ge(exp_ready, HG * TB * i + (HG * (mt + 1) + 2))
                for h in range(HG):
                    ins = pe.matmul(ps[32 * h:32 * h + 32, 6, :], vs[:, k, mt, h], ering[:, HG * (mt % 2) + h],
                                    start=(mt == 0), stop=(mt == TB - 1))
                ins.then_inc(pv_done, 1)

            def turn_max(i, k):
                pe.wait_ge(split_done, i + 1)
                if not isinstance(i, int) or i >= 3:
                    pe.wait_ge(o_norm, i - 2)
                pe.transpose(ps[:, 7, 0:P // 2].bitcast(BF16), mp[:, k].rearrange("p c n -> p (c n)"), idb[:]).then_inc(mT_ready, 1)

            def turn_out(i, k):
                pe.wait_ge(o_evac, i + 1)
                if not isinstance(i, int) or i + 2 < NGR:
                    pe.wait_ge(mT_copied, i + 3)
                else:
                    pe.wait_ge(o_norm, i)
                for c in range(TB):
                    ins = pe.transpose(ps[:, 7, P * c:P * c + P], oT[:, k, P * c:P * c + P], idf[:])
                ins.then_inc(o_turn, 1)

            def pe_group(i, k):
                static = isinstance(i, int)
                ahead, after = not static or i + 2 < NGR, not static or i + 1 < NGR
                if ahead:
                    if static:
                        pe.wait_ge(stack_ready, (i + 2) // GB + 1)
                    else:
                        pe.wait_ge(stack_ready, (i + 2) // GB + 1)
                for mt in range(TB):
                    if mt == TB - 1 and after and (not static or i >= 1):
                        turn_out(i - 1, 1 - k)
                    for h in range(HG):
                        if h == HG - 1:
                            values(i, k, mt)
                            if mt == 0 and after:
                                turn_max(i + 1, 1 - k)
                        if mt < TB - 1:
                            scores(i, mt + 1, h)
                        elif after:
                            scores(i + 1, 0, h)
                        if ahead:
                            max_scores(i + 2, mt, h)

            pe.wait_ge(stack_ready, 1)
            pe.wait_ge(s_qks, 2 * B)
            pe.wait_ge(s_vvs, B)
            for h in range(HG):
                for c in range(TB):
                    max_scores(0, h, c)
            turn_max(0, 0)
            for h in range(HG):
                for c in range(TB):
                    max_scores(1, h, c)
            for h in range(HG):
                scores(0, 0, h)
            pe_group(0, 0)
            pe_group(1, 1)
            with pe.Fori(1, NGR // 2 - 1) as j:
                i = pe.snap(j * 2)
                pe_group(i, 0)
                pe_group(i + 1, 1)
            pe_group(NGR - 2, 0)
            pe_group(NGR - 1, 1)
            turn_out(NGR - 2, 0)
            turn_out(NGR - 1, 1)
            for b in range(B):
                pe.wait_ge(o_norm, GB * (b + 1))
                turn(3 * B + b, lambda t: ot[:, t])
            for b in range(B):
                pe.wait_ge(s_trs, 3 * B + b + 1)
                for t in range(TB):
                    ins = pe.matmul(ps[:, 4 + b, P * t:P * t + P], xT[:, L * b + P * t:L * b + P * t + P], w_o_s[:], start=True, stop=True)
                ins.then_inc(s_pr, 1)
            if STAGE < 4:
                return
            for b in range(B):
                pe.wait_ge(s_xn, 3 * B + b + 1)
                turn(4 * B + b, lambda t: xt[:, t])
            if STAGE < 4:
                return
            pe.wait_ge(s_kf, 1)
            pe.wait_ge(s_trs, 5 * B)
            for b in range(B):
                for layer in range(2):
                    for c in range(FC):
                        n = (2 * b + layer) * FC + c
                        if n >= FC:
                            pe.wait_ge(s_fs, n - FC + 1)
                        if layer == 1 and c == 0:
                            pe.wait_ge(s_fs, n)
                        for kk in range(FC if layer else 1):
                            w = w1[:, kk, P * c:P * c + P] if layer else w0[:, P * c:P * c + P]
                            ins = pe.matmul(ps[:, c, :], w, h1[:, kk] if layer else xT[:, L * b:L * b + L],
                                            start=(kk == 0), stop=(not layer or kk == FC - 1))
                        ins.then_inc(s_f, 1)
                pe.wait_ge(s_fs, (2 * b + 2) * FC)
                for t in range(TB):
                    for kk in range(FC):
                        ins = pe.matmul(ps[:, 4 + b, P * t:P * t + P], h2[:, kk, P * t:P * t + P], w2[:, kk],
                                        start=(kk == 0), stop=(kk == FC - 1))
                ins.then_inc(s_fo, 1)


def kernel(**inputs):
    import numpy as np
    import concourse.bacc as bacc
    from concourse import mybir as mb
    from concourse.bass_utils import run_bass_kernel_spmd

    a = {k: np.asarray(v) for k, v in inputs.items()}
    wg, wu, wd = a["L0_ffn_Wg"], a["L0_ffn_Wu"], a["L0_ffn_Wd"]
    i = wg.shape[1]
    arrays = {
        "x": a["L0_attn_x"], "a_log": a["L0_attn_A_log"].reshape(-1, 1), "dmat": a["L0_attn_Dmat"],
        "w_in": a["L0_attn_W_in"].T, "b_in": a["L0_attn_b_in"].reshape(2, P).T, "w_xp": a["L0_attn_W_xp"].T,
        "b_xp": a["L0_attn_b_xp"].reshape(-1, 1), "w_out": a["L0_attn_W_out"].T, "b_out": a["L0_attn_b_out"].reshape(1, P),
        "gamma": a["L0_attn_gamma"].reshape(P, 1), "beta": a["L0_attn_beta"].reshape(P, 1),
        "gate_w": a["L0_ffn_gate_w"].T, "gate_bias": a["L0_ffn_gate_bias"].reshape(1, -1), 
        "w_gu": np.concatenate([wg, wu], axis=1).transpose(2, 0, 1), "w_d": wd.transpose(2, 0, 1),
        "w_sh": np.concatenate([a["L0_ffn_Sg"], a["L0_ffn_Su"]]).T,
        "w_shd": a["L0_ffn_Sd"].reshape(P, 2, i).transpose(2, 1, 0),
        "w_qkv": np.concatenate([a["L1_attn_Wq"], a["L1_attn_Wk"], a["L1_attn_Wv"]]).T,
        "b_qk": np.stack([a["L1_attn_bq"], a["L1_attn_bk"]], axis=1), "b_v": a["L1_attn_bv"].reshape(1, P),
        "w_o": a["L1_attn_Wo"].T, "b_o": a["L1_attn_bo"].reshape(1, P),
        "k0": a["L1_ffn_k0"], "k1": a["L1_ffn_k1"], "k2": a["L1_ffn_k2"],
        "s012": np.stack([a["L1_ffn_s0"], a["L1_ffn_s1"], a["L1_ffn_s2"]]).reshape(1, 3),
        "ident": np.eye(P, dtype=np.float32),
    }
    arrays = {k: np.ascontiguousarray(v) for k, v in arrays.items()}
    nc = bacc.Bacc("TRN2", target_bir_lowering=False, num_devices=1)
    args = {k: nc.dram_tensor(k, v.shape, mb.dt.from_np(v.dtype), kind="ExternalInput").ap() for k, v in arrays.items()}
    out = nc.dram_tensor("out", a["L0_attn_x"].shape, mb.dt.float32, kind="ExternalOutput").ap()
    build(nc, **args, out=out)
    return run_bass_kernel_spmd(nc, [arrays], core_ids=[0]).results[0]["out"]
```

```python
from contextlib import ExitStack

import concourse.bass as bass
from concourse import mybir

P = 128
ALU = mybir.AluOpType
ACT = mybir.ActivationFunctionType
F32 = mybir.dt.float32
BF16 = mybir.dt.bfloat16
U8 = mybir.dt.uint8
U32 = mybir.dt.uint32
I32 = mybir.dt.int32
AX_X = mybir.AxisListType.X
EPS = 1e-5
ROUTED_SCALE = 2.5
HEADS = 16
GROUPS = 8
GROUPS_KEPT = 4
TOP_K = 8
STAGE = 9


def build(nc, x, a_log, dmat, w_in, b_in, w_xp, b_xp, w_out, b_out, gamma, beta,
          gate_w, gate_bias, w_gu, w_d, w_sh, w_shd, w_qkv, b_qk, b_v, w_o, b_o, k0, k1, k2, s012, ident, out):
    B, L, M = x.shape
    T = B * L
    NT = T // P
    TB = L // P
    S = dmat.shape[0]
    E = gate_w.shape[1]
    EG = E // GROUPS
    I2 = w_gu.shape[2]
    I = I2 // 2
    KI = 96
    HT = NT // 2
    BODY = 16
    NBH = -(-(T // 2 * TOP_K + E * (P - 1)) // (P * BODY)) * BODY
    BODIES = NBH // BODY
    NB = 2 * NBH
    NPAIR = NB // 2
    assert NBH <= P
    AHEAD = 8
    HD = M // HEADS
    HG = 4
    GB = HEADS // HG
    NGR = B * GB
    SCALE = float(M) ** -0.5
    TURN_IN, QK_IN, V_IN = {1: 2, 4: 3}, {2: 2, 5: 3}, {3: 2, 6: 3}
    HEAD_GROUPS = 8
    COMBINED = {-2: (0, 1), -1: (2, 3), 0: (4, 5), 2: (6, 7)}
    NP = 3
    KD = 96
    KS = KD + NP
    F = k1.shape[0]
    FC = F // P

    with ExitStack() as ctx:
        def sb(name, shape, dt=F32):
            return ctx.enter_context(nc.sbuf_tensor(name, shape, dt))

        def sem(name):
            return ctx.enter_context(nc.semaphore(name))

        xt = sb("xt", [P, NT, M])
        xT = sb("xT", [P, T])
        tmp = sb("tmp", [P, NT, M])
        xb = sb("xb", [P, NT, M])
        big = sb("big", [P, 4, T])
        zT, xpT = big[:, 0].rearrange("p (b l) -> p b l", b=B), big[:, 1].rearrange("p (b l) -> p b l", b=B)
        uT = big[:, 2, 0:T // 2].rearrange("p (b l) -> p b l", b=B // 2)
        hT = big[:, 2, T // 2:T].rearrange("p (b l) -> p b l", b=B // 2)
        ysT = big[:, 3].rearrange("p (l b) -> p l b", b=B)
        st = sb("st", [P, NT, 6])
        mv = sb("mv", [P, NT, 2])
        rstd = sb("rstd", [P, NT])
        minus_half = sb("minus_half", [P, TB])
        idf = sb("idf", [P, P])
        idb = sb("idb", [P, P], BF16)
        w_in_s = sb("w_in_s", [P, 2 * M])
        w_xp_s = sb("w_xp_s", [P, S])
        dmat_s = sb("dmat_s", [P, M])
        w_out_s = sb("w_out_s", [P, M])
        gamma_s, beta_s = sb("gamma_s", [P, 1]), sb("beta_s", [P, 1])
        b_in_s = sb("b_in_s", [P, 2])
        b_xp_s, decay = sb("b_xp_s", [P, 1]), sb("decay", [P, 1])
        b_qk_s = sb("b_qk_s", [P, 2])
        rows = sb("rows", [P, 3, M])
        bias_row = sb("bias_row", [P, E])
        gate_s = sb("gate_s", [P, E])
        sc = sb("sc", [P, NT, E])
        ch = sb("ch", [P, NT, E])
        ra = sb("ra", [P, NT, E])
        rb = sb("rb", [P, NT, E])
        gs = sb("gs", [P, NT, GROUPS])
        g1, g2 = sb("g1", [P, NT, GROUPS, 4]), sb("g2", [P, NT, GROUPS, 4])
        g3, g4 = sb("g3", [P, NT, GROUPS, 2]), sb("g4", [P, NT, GROUPS, 2])
        top = sb("top", [P, NT, 8])
        cnt = sb("cnt", [P, NT])
        before = sb("before", [P, GROUPS, GROUPS])
        keep = sb("keep", [P, NT, E])
        places = sb("places", [P, 3, E * NT], BF16)
        selb, incb, exb = (places[:, i].rearrange("p (f e t) -> p f e t", f=2, t=HT) for i in range(3))
        keep2 = sb("keep2", [P, E, HT], BF16)
        tri, onesb = sb("tri", [P, P], BF16), sb("onesb", [P, P], BF16)
        ones_e = sb("ones_e", [P, E])
        nblk, endb, baserow = sb("nblk", [P, E]), sb("endb", [P, E]), sb("baserow", [P, E])
        thr = sb("thr", [P, HT])
        bnum = sb("bnum", [P, 1])
        ecmp = sb("ecmp", [P, E])
        eidf, eid = sb("eidf", [P, 2]), sb("eid", [P, 2], I32)
        tab = sb("tab", [1, AHEAD + NB], I32)
        dst = sb("dst", [P, NT, TOP_K])
        idx = sb("idx", [P, NT, TOP_K], U32)
        wk = sb("wk", [P, NT, TOP_K])
        sg = sb("sg", [P, 2, 2, I])
        hm = sb("hm", [P, 2, 2, KI])
        hmT = sb("hmT", [P, 2, 2, P])
        xbT = sb("xbT", [P, 2, 2, P])
        wsh_s = sb("wsh_s", [P, 2 * I2])
        wshd_s = sb("wshd_s", [P, 2, M])
        w_qkv_s = sb("w_qkv_s", [P, 3 * M])
        w_o_s = sb("w_o_s", [P, M])
        kb = sb("kb", [P, 2, F], U8)
        kb1 = sb("kb1", [P, FC, F], U8)
        kb2 = sb("kb2", [P, FC, M], U8)
        s_row = sb("s_row", [P, 3])
        arena = sb("arena", [P, E * (I2 + M)])
        wgu_s = arena[:, 0:E * I2].rearrange("p (e n) -> p e n", e=E)
        wd_s = arena[:, E * I2:E * (I2 + M)].rearrange("p (e n) -> p e n", e=E)
        SH = 2 * HEADS
        half = SH * L // 2
        qst = arena[:, 0:half].bitcast(BF16).rearrange("p (h n) -> p h n", h=SH)
        kst = arena[:, half:2 * half].bitcast(BF16).rearrange("p (h n) -> p h n", h=SH)
        assert 2 * half + 3 * TOP_K * M <= E * (I2 + M)
        xin = big[:, 0].rearrange("p (q j m) -> p q j m", q=4, m=M)
        ob = big[:, 1].rearrange("p (q j m) -> p q j m", q=4, m=M)
        gb = big[:, 2:4].rearrange("p a (s k m) -> p (a s) k m", k=TOP_K, m=M)
        gb2 = arena[:, 2 * half:2 * half + 3 * TOP_K * M].rearrange("p (s k m) -> p s k m", k=TOP_K, m=M)
        vt = big[:, 0].rearrange("p (i m c) -> p i m c", i=NGR, m=TB)
        ot = big[:, 1].rearrange("p (t m) -> p t m", t=NT)
        otg = big[:, 1].rearrange("p (b m g c) -> p b m g c", b=B, m=TB, g=GB)
        ering = big[:, 2:4].rearrange("p a (s n) -> p (a s) n", n=L)
        kf = arena[:, 2 * half:2 * half + 3 * TOP_K * M].bitcast(BF16)
        w0 = kf[:, 0:F]
        w1 = kf[:, F:F + FC * F].rearrange("p (c n) -> p c n", c=FC)
        w2 = kf[:, F + FC * F:F + FC * F + FC * M].rearrange("p (c n) -> p c n", c=FC)
        mlp = arena[:, 0:2 * half].bitcast(BF16)
        assert 3 * NP * T <= 2 * half * 2 and FC * L == T
        xp = mlp[:, 0:NP * T].rearrange("p (c n) -> p c n", c=NP)
        h1, h2 = (mlp[:, NP * T * a:NP * T * (a + 1)].rearrange("p (c k n) -> p c k n", c=NP, k=FC) for a in (1, 2))
        hid, rest = (big[:, a].rearrange("p (c n) -> p c n", c=FC) for a in (0, 2))
        qf, qr, oT = (t[:].rearrange("p t e -> p (t e)").rearrange("p (o n) -> p o n", o=2) for t in (sc, ra, ch))
        parts = places[:].rearrange("p a n -> p (a n)").rearrange("p (o c n) -> p o c n", o=2, c=NP)
        vs = keep[:].rearrange("p t e -> p (t e)").rearrange("p (k m h c) -> p k m h c", k=2, m=TB, h=HG)
        mx = sb("mx", [P, 2, HG * TB])
        mr = sb("mr", [P, 2, HG * TB])
        mp = sb("mp", [P, 2, P // (HG * TB), HG * TB], BF16)
        zeros = sb("zeros", [P, 4 * M])
        mT = sb("mT", [NP * HG * TB, 2, P], BF16)
        rc = sb("rc", [P, TB, HG])

        def back_slot(t):
            if t < 4:
                return gb[:, t], g_in[t], 16 * TOP_K * (HT // 4 + 1)
            return gb2[:, (t - 4) % 3], g2_in[(t - 4) % 3], 16 * TOP_K * ((t - 4) // 3 + 1)

        ps = ctx.enter_context(nc.psum_tensor("ps", [P, 8, 512], F32))
        xd, od = ([nc.dram_tensor(f"{n}{f}", (NBH * P, M), F32, kind="Internal").ap() for f in range(2)] for n in ("xd", "od"))
        scr = nc.dram_tensor("scr", (2, B, HEADS, NP, HD, L), BF16, kind="Internal").ap()

        s_x = [sem(f"s_x{q}") for q in range(B)]
        s_w, s_we, s_wa, s_wf = sem("s_w"), sem("s_we"), sem("s_wa"), sem("s_wf")
        s_idb, s_const, s_decay = sem("s_idb"), sem("s_const"), sem("s_decay")
        s_st, s_rstd, s_v, s_p, s_xn = sem("s_st"), sem("s_rstd"), sem("s_v"), sem("s_p"), sem("s_xn")
        s_tr, s_trs = sem("s_tr"), sem("s_trs")
        s_xz, s_xzs, s_u, s_h = sem("s_xz"), sem("s_xzs"), sem("s_u"), sem("s_h")
        s_y, s_ys, s_yo, s_xb = sem("s_y"), sem("s_ys"), sem("s_yo"), sem("s_xb")
        s_lg, s_lgs, s_rw = sem("s_lg"), sem("s_lgs"), sem("s_rw")
        s_zero, s_cum, s_pos, s_idx, s_eid, s_tab = (sem(n) for n in ("s_zero", "s_cum", "s_pos", "s_idx", "s_eid", "s_tab"))
        ld, stq, g_in = ([sem(f"{n}{r}") for r in range(4)] for n in ("ld", "stq", "g_in"))
        s_sc, g2_in = ([sem(f"{n}{r}") for r in range(k)] for n, k in (("s_sc", 2), ("g2_in", 3)))
        rows_back, comb = sem("rows_back"), sem("comb")
        xt_ready, x_copied, s_sh = sem("xt_ready"), sem("x_copied"), sem("s_sh")
        gu_ready, sg_ready, hm_ready = sem("gu_ready"), sem("sg_ready"), sem("hm_ready")
        th_ready, th_copied, d_ready, acc_done = sem("th_ready"), sem("th_copied"), sem("d_ready"), sem("acc_done")
        s_qk, s_qks, s_part, s_pw = sem("s_qk"), sem("s_qks"), sem("s_part"), sem("s_pw")
        s_stk = [sem(f"s_stk{b}") for b in range(B)]
        s_pad, s_vv, s_vvs = sem("s_pad"), sem("s_vv"), sem("s_vvs")
        stack_ready = sem("stack_ready")
        s1_ready, s1_free, split_done = sem("s1_ready"), sem("s1_free"), sem("split_done")
        mT_ready, mT_copied, max_in = sem("mT_ready"), sem("mT_copied"), sem("max_in")
        s2_ready, exp_ready, pv_done = sem("s2_ready"), sem("exp_ready"), sem("pv_done")
        vs_ready, o_evac, o_turn, o_norm = sem("vs_ready"), sem("o_evac"), sem("o_turn"), sem("o_norm")
        rc_done, s_vs = sem("rc_done"), sem("s_vs")
        s_pr, s_kf, s_f, s_fs, s_out, s_r = sem("s_pr"), sem("s_kf"), sem("s_f"), sem("s_fs"), sem("s_out"), sem("s_r")
        s_fo, s_hid, s_rest, s_mid, s_xp = sem("s_fo"), sem("s_hid"), sem("s_rest"), sem("s_mid"), sem("s_xp")

        block = ctx.enter_context(nc.Block())
        tiled = "b (t p) m -> p (b t) m"
        NDR, NDQ = NP * NP * 2, NP

        STK = NP + NP * NP

        def write_parts(sp, b, os=(0, 1)):
            for o in os:
                sp.wait_ge(s_part, 2 * b + o + 1)
                for c in range(NP):
                    sp.dma_start(scr[o, b, :, c], parts[:, o, c]).then_inc(s_pw, 16)
                sp.wait_ge(s_pw, 16 * NP * (2 * b + o + 1))

        def load_stack(sp, b, first=0, heads=HEADS, os=(0, 1)):
            h0 = HEADS * (b % 2) + first
            hs, src = slice(h0, h0 + heads), slice(first, first + heads)
            if 0 in os:
                for c in range(NP):
                    sp.dma_start(qst[NP * HD * c:NP * HD * (c + 1), hs, :], scr[0, b, src].rearrange("h c d n -> (c d) h n")).then_inc(s_stk[b], 16)
            if 1 in os:
                for j in range(NP * NP):
                    sp.dma_start(kst[HD * j:HD * j + HD, hs, :], scr[1, b, src, j // NP].rearrange("h d n -> d h n")).then_inc(s_stk[b], 16)

        def stacked(sp, b, loads=1):
            sp.wait_ge(s_stk[b], 16 * STK * loads)
            sp.sem_inc(stack_ready, 1)

        def pad_stack(sp, h0, heads):
            for stack in (qst, kst):
                sp.dma_start(stack[NP * NP * HD:KD, h0:h0 + heads].rearrange("p (a h) n -> p a (h n)", h=2),
                             zeros[NP * NP * HD:KD].bitcast(BF16).unsqueeze(1).broadcast_to([KD - NP * NP * HD, heads // 2, 2 * L])).then_inc(s_pad, 16)
            sp.dma_start(qst[KD:KS, h0:h0 + heads].rearrange("p h (a n) -> p (h a) n", n=P),
                         onesb[KD:KS].unsqueeze(1).broadcast_to([NP, heads * L // P, P])).then_inc(s_pad, 16)

        @block.sync
        def _(sp):
            sp.dma_start(idf[:], ident).then_inc(s_w, 16)
            for q in range(B):
                sp.dma_start(xt[:, TB * q:TB * q + TB, :], x.rearrange(tiled, p=P)[:, TB * q:TB * q + TB, :]).then_inc(s_x[q], 16)
            for dst, src in ((w_in_s[:], w_in), (w_xp_s[:], w_xp), (dmat_s[0:S], dmat), (dmat_s[S:2 * S], dmat),
                             (w_out_s[:], w_out), (gamma_s[:], gamma), (beta_s[:], beta), (b_in_s[:], b_in),
                             (b_xp_s[0:S], b_xp), (b_xp_s[S:2 * S], b_xp), (decay[0:S], a_log), (decay[S:2 * S], a_log),
                             (gate_s[:], gate_w), (bias_row[:], gate_bias.broadcast_to([P, E])),
                             (rows[:, 0], b_out.broadcast_to([P, M]))):
                sp.dma_start(dst, src).then_inc(s_w, 16)
            sp.wait_ge(s_const, 1)
            for f in range(2):
                sp.dma_start(xd[f].rearrange("(p b c) m -> p b (c m)", p=P, c=4),
                             zeros[:].unsqueeze(1).broadcast_to([P, NBH // 4, 4 * M])).then_inc(s_zero, 16)
            sp.dma_start(wsh_s[:], w_sh).then_inc(s_we, 16)
            sp.dma_start(wshd_s[0:I], w_shd).then_inc(s_we, 16)
            sp.dma_start(wgu_s, w_gu).then_inc(s_we, 16)
            sp.dma_start(wd_s[0:I], w_d).then_inc(s_we, 16)
            for dst, src in ((rows[:, 1], b_v.broadcast_to([P, M])), (rows[:, 2], b_o.broadcast_to([P, M])),
                             (w_qkv_s[:], w_qkv), (w_o_s[:], w_o), (b_qk_s[:], b_qk), (s_row[:], s012.broadcast_to([P, 3])),
                             (kb[:], k0.rearrange("(a p) n -> p a n", p=P)), (kb1[:], k1.rearrange("(c p) n -> p c n", p=P)),
                             (kb2[:], k2.rearrange("(c p) n -> p c n", p=P))):
                sp.dma_start(dst, src).then_inc(s_wa, 16)
            if STAGE >= 2:
                for f in range(2):
                    sp.wait_ge(s_eid, f + 1)
                    sp.dma_start(tab[0:1, AHEAD + NBH * f:AHEAD + NBH * f + NBH], eid[0:NBH, f:f + 1]).then_inc(s_tab, 16)
                sp.wait_ge(s_sc[0], 16 * HT * TOP_K)
                xq, oq = ([a.rearrange("(q j p) m -> p q j m", j=4, p=P) for a in d] for d in (xd, od))
                QH = NBH // 4

                def quads(q, done, src, dst, store):
                    for r in range(4):
                        if src is not None:
                            sp.wait_ge(xt_ready, done * 2 + (2 * r + 2))
                            sp.dma_start(xin[:, r], src[:, bass.ds(q + r, 1)].rearrange("p a j m -> p (a j) m")).then_inc(ld[r], 16)
                        sp.wait_ge(acc_done, done * 2 + (2 * r + 4))
                        sp.dma_start(dst[:, bass.ds(store + r, 1)].rearrange("p a j m -> p (a j) m"), ob[:, r]).then_inc(stq[r], 16)

                for r in range(4):
                    sp.dma_start(xin[:, r], xq[0][:, r]).then_inc(ld[r], 16)
                with sp.Fori(0, BODIES - 1) as j:
                    q = sp.snap(j * 4)
                    quads(q + 4, q, xq[0], oq[0], q)
                sp.wait_ge(s_sc[1], 16 * HT * TOP_K)
                quads(0, QH - 4, xq[1], oq[0], QH - 4)
                with sp.Fori(0, BODIES - 1) as j:
                    q = sp.snap(j * 4)
                    quads(q + 4, q + QH, xq[1], oq[1], q)
                quads(0, 2 * QH - 4, None, oq[1], QH - 4)
            if STAGE >= 3:
                sp.wait_ge(d_ready, NT + NPAIR)
                pad_stack(sp, 0, HG)
                for o in range(2):
                    write_parts(sp, 0, (o,))
                    load_stack(sp, 0, 0, HG, (o,))
                sp.wait_ge(s_pad, 48)
                stacked(sp, 0)
                load_stack(sp, 0, HG, HEADS - HG)
                pad_stack(sp, HG, HEADS - HG)
                write_parts(sp, 1)
                sp.wait_ge(s_pad, 96)
                stacked(sp, 0, loads=2)
                load_stack(sp, 1)
                pad_stack(sp, HEADS, HEADS)
                sp.wait_ge(s_pad, 144)
                stacked(sp, 1)
                for i in range(NGR):
                    sp.wait_ge(mT_copied, i + 1)
                    hd = HG * (i % (2 * GB))
                    for c in range(NP):
                        sp.dma_start(kst[KD + c:KD + c + 1, hd:hd + HG, :].rearrange("p h n -> p (h n)"),
                                     mT[HG * TB * c:HG * TB * c + HG * TB, i % 2, :]).then_inc(max_in, 16)
                    sp.wait_ge(max_in, 16 * NP * (i + 1))
                    for b in range(2, B):
                        if QK_IN.get(i - 1) == b:
                            write_parts(sp, b)
                        if i == GB * (b - 1):
                            sp.wait_ge(s2_ready, HG * TB * i)
                            load_stack(sp, b)
                        if i == GB * (b - 1) + 1:
                            stacked(sp, b)
            for q in range(B):
                sp.wait_ge(s_xn, 4 * B + q + 1)
                sp.dma_start(out.rearrange(tiled, p=P)[:, TB * q:TB * q + TB, :], xt[:, TB * q:TB * q + TB, :]).then_inc(s_out, 16)
            sp.wait_ge(s_out, 16 * B)
            sp.wait_ge(s_we, 64)
            sp.wait_ge(s_zero, 32)
            sp.wait_ge(s_wa, 16 * 9)

        @block.gpsimd
        def _(pool):
            pn = [0]

            def own(ins):
                pn[0] += 1
                ins.then_inc(s_p, 1)
                pool.wait_ge(s_p, pn[0])

            def rstd_of(k):
                pool.wait_ge(s_st, k + 1)
                q = k % B
                r = rstd[:, TB * q:TB * q + TB]
                own(pool.tensor_scalar(r, mv[:, TB * q:TB * q + TB, 1], EPS, None, ALU.add))
                pool.tensor_tensor(r, r, minus_half[:], ALU.pow).then_inc(s_rstd, 1)

            own(pool.memset(minus_half[:], -0.5))
            own(pool.memset(zeros[:], 0.0))
            own(pool.memset(mp[:], 0.0))
            own(pool.memset(hm[:], 0.0))
            for q in range(B):
                rstd_of(q)
            own(pool.memset(hmT[:], 0.0))
            own(pool.memset(keep[:], 1.0))
            own(pool.memset(keep[:, :, 0:1], 0.0))
            own(pool.memset(keep2[:], 1.0))
            own(pool.memset(keep2[:, :, 0:1], 0.0))
            own(pool.memset(tri[:], 1.0))
            own(pool.affine_select(out=tri[:], in_=tri[:], pattern=[[1, P]], compare_op=ALU.is_ge, fill=0.0, base=-1,
                                   channel_multiplier=-1))
            own(pool.memset(onesb[:], 1.0))
            own(pool.memset(ones_e[:], 1.0))
            own(pool.memset(tab[:], 0))
            own(pool.iota(thr[:], [[P, HT]], base=0, channel_multiplier=0, allow_small_or_imprecise_dtypes=True))
            own(pool.iota(bnum[:], [[P, 1]], base=0, channel_multiplier=1, allow_small_or_imprecise_dtypes=True))
            own(pool.memset(before[:], 1.0))
            own(pool.affine_select(out=before[:], in_=before[:], pattern=[[1, GROUPS], [-1, GROUPS]], compare_op=ALU.is_ge,
                                   fill=0.0, base=-1, channel_multiplier=0))
            own(pool.memset(wd_s[64:KI], 0.0))
            own(pool.memset(wshd_s[64:KI], 0.0))
            pool.sem_inc(s_const, 1)

            pool.wait_ge(s_w, 16 * 16)
            own(pool.tensor_tensor(xb[:], xt[:], xt[:], ALU.add))
            pool.tensor_tensor(xb[:], xb[:], rows[:, 0:1].broadcast_to([P, NT, M]), ALU.add).then_inc(s_xb, 1)
            for q in range(B, 2 * B):
                rstd_of(q)
            if STAGE < 2:
                return
            pool.wait_ge(s_zero, 32)
            for f in range(2):
                pool.wait_ge(s_idx, f + 1)
                pool.wait_ge(s_xn, B + 2 * f + 2)
                for t in range(HT * f, HT * f + HT):
                    for k in range(TOP_K):
                        pool.indirect_dma_start(out=xd[f], out_offset=bass.IndirectOffsetOnAxis(ap=idx[:, t, k:k + 1], axis=0),
                                                in_=xt[:, t], in_offset=None).then_inc(s_sc[f], 16)

            own(pool.memset(vs, 0.0))
            own(pool.memset(vs[:, :, :, :, HD:HD + 1], 1.0))
            pool.sem_inc(s_vs, 1)

            def bring(f, t, slot, landed):
                for k in range(TOP_K):
                    pool.indirect_dma_start(out=slot[:, k], out_offset=None, in_=od[f],
                                            in_offset=bass.IndirectOffsetOnAxis(ap=idx[:, t, k:k + 1], axis=0)).then_inc(landed, 16)

            for r in range(4):
                pool.wait_ge(stq[r], 16 * BODIES)
            for t in range(HT):
                if t >= 4:
                    pool.wait_ge(comb, TOP_K * (t - 3))
                bring(0, t, gb[:, t % 4], g_in[t % 4])
                pool.wait_ge(g_in[t % 4], 16 * TOP_K * (t // 4 + 1))
                pool.sem_inc(rows_back, 1)
            rstd_of(2 * B)
            for r in range(4):
                pool.wait_ge(stq[r], 32 * BODIES)
            for t in range(HT):
                if t < 4:
                    pool.wait_ge(comb, TOP_K * (t + 5 if t < 2 else HT))
                if t >= 7:
                    last = [max(ts) for ts in COMBINED.values() if t - 3 in ts][0]
                    pool.wait_ge(comb, TOP_K * (HT + last + 1))
                bring(1, HT + t, *back_slot(t)[:2])
                if t == 1:
                    rstd_of(2 * B + 1)
                if t == 5:
                    rstd_of(2 * B + 2)
            if STAGE >= 3:
                def qk_parts(b):
                    for o in range(2):
                        pool.wait_ge(s_qks, 2 * b + o + 1)
                        own(pool.tensor_tensor(qr[:, o], qf[:, o], parts[:, o, 0], ALU.subtract))
                        own(pool.tensor_copy(parts[:, o, 1], qr[:, o]))
                        pool.tensor_tensor(parts[:, o, 2], qr[:, o], parts[:, o, 1], ALU.subtract).then_inc(s_part, 1)

                qk_parts(2)
                rstd_of(2 * B + 3)
                pool.wait_ge(s_wa, 16 * 9)
                pool.wait_ge(comb, TOP_K * NT)
                lower = xbT[:].rearrange("p u a m -> p (u a m)")
                upper = hmT[:].rearrange("p u a m -> p (u a m)")
                own(pool.tensor_scalar(upper, kb[:, 0], 2.0, None, ALU.mult))
                own(pool.tensor_scalar(lower, kb[:, 1], 2.0, None, ALU.mult))
                own(pool.tensor_tensor(w0, upper, lower, ALU.subtract))
                own(pool.tensor_scalar(w1, kb1[:], 2.0, -1.0, ALU.mult, ALU.add))
                own(pool.tensor_scalar(w2, kb2[:], 2.0, -1.0, ALU.mult, ALU.add))
                pool.tensor_scalar(s_row[:, 0:2], s_row[:, 0:2], 2.0, None, ALU.mult).then_inc(s_kf, 1)
                qk_parts(3)
                pool.wait_ge(s_xn, 3 * B)
                pool.tensor_tensor(xb[:], xt[:], rows[:, 2:3].broadcast_to([P, NT, M]), ALU.add).then_inc(s_xb, 1)
                for q in range(3 * B, (5 if STAGE > 3 else 4) * B):
                    rstd_of(q)

        @block.scalar
        def _(act):
            act.wait_ge(s_w, 16 * 16)
            act.activation(decay[:], decay[:], ACT.Exp).then_inc(s_decay, 1)
            act.wait_ge(s_decay, 1)
            act.activation(decay[:], decay[:], ACT.Exp, scale=-1.0).then_inc(s_decay, 1)
            act.activation(idb[:], idf[:], ACT.Copy).then_inc(s_idb, 1)

            def turned(k, dst, **how):
                act.wait_ge(s_tr, k + 1)
                act.activation(dst, ps[:, k % B, :], ACT.Identity, **how).then_inc(s_trs, 1)

            for b in range(B):
                turned(b, xT[:, L * b:L * b + L], scale=gamma_s[:], bias=beta_s[:])
            for o, (dst, f) in enumerate(((xpT, ACT.Silu), (zT, ACT.Sigmoid))):
                for b in range(B):
                    act.wait_ge(s_xz, B * o + b + 1)
                    act.activation(dst[:, b], ps[:, 4 + b, :], f, bias=b_in_s[:, o:o + 1]).then_inc(s_xzs, 1)
            for a in range(2):
                for b in range(2 * a, 2 * a + 2):
                    turned(B + b, xT[:, L * b:L * b + L])
                act.wait_ge(s_lg, a + 1)
                act.activation(sc[:, NT // 2 * a:NT // 2 * (a + 1), :], ps[:, 4 + a, :].rearrange("p (t e) -> p t e", e=E),
                               ACT.Sigmoid).then_inc(s_lgs, 1)
            if STAGE < 2:
                return
            for t in range(NT + 2):
                if t < NT:
                    act.wait_ge(gu_ready, t + 1)
                    act.activation(sg[:, t % 2], ps[:, 2 + t % 2, 0:I2].rearrange("p (a i) -> p a i", a=2), ACT.Silu).then_inc(sg_ready, 1)
                if 1 <= t <= NT:
                    act.wait_ge(th_ready, t)
                    act.activation(hmT[0:KI, (t - 1) % 2], ps[0:KI, 4 + (t - 1) % 2, 0:2 * P].rearrange("p (a i) -> p a i", a=2), ACT.Copy).then_inc(th_copied, 1)

            def act_pair(s, u):
                if not isinstance(s, int) or 1 <= s <= NPAIR:
                    act.wait_ge(gu_ready, s + NT)
                    act.activation(sg[:, (u - 1) % 2], ps[:, 2 + (u - 1) % 2, 0:2 * I2].rearrange("p (a i) -> p a i", a=2)[:, :, 0:I],
                                   ACT.Silu).then_inc(sg_ready, 1)
                if not isinstance(s, int) or 2 <= s <= NPAIR + 1:
                    act.wait_ge(th_ready, s + (NT - 1))
                    act.activation(hmT[0:KI, u % 2], ps[0:KI, 4 + u % 2, 0:2 * P].rearrange("p (a i) -> p a i", a=2), ACT.Copy).then_inc(th_copied, 1)

            for u in range(8):
                act_pair(u, u)
            with act.Fori(1, NB // BODY) as j:
                s0 = act.snap(j * 8)
                for u in range(8):
                    act_pair(s0 + u, u)
            for u in range(3):
                act_pair(NPAIR + u, u)
            if STAGE < 3:
                for b in range(B):
                    turned(2 * B + b, xT[:, L * b:L * b + L])
                return

            def turn_in(b, bank):
                act.wait_ge(s_tr, 2 * B + b + 1)
                act.activation(xT[:, L * b:L * b + L], ps[:, bank, :], ACT.Identity).then_inc(s_trs, 1)

            def qk_in(b, o, bank):
                act.wait_ge(s_qk, 2 * b + o + 1)
                if b >= 1:
                    act.wait_ge(s_part, 2 * (b - 1) + o + 1)
                    act.wait_ge(s_pw, 16 * NP * (2 * (b - 1) + o + 1))
                act.activation(parts[:, o, 0], ps[:, bank, :], ACT.Identity, bias=b_qk_s[:, o:o + 1])
                act.activation(qf[:, o], ps[:, bank, :], ACT.Identity, bias=b_qk_s[:, o:o + 1]).then_inc(s_qks, 1)

            act.wait_ge(s_wa, 16 * 9)
            for b in range(2):
                turn_in(b, b)
                for o in range(2):
                    qk_in(b, o, 4 + o)

            def stage_values(i, k):
                act.activation(vs[:, k, :, :, 0:HD], vt[:, bass.ds(i, 1)].rearrange("p a m (h d) -> p (a m) h d", h=HG),
                               ACT.Copy).then_inc(vs_ready, 1)

            def exps(i, mt):
                for h in range(HG):
                    act.wait_ge(s2_ready, HG * TB * i + (HG * mt + h + 1))
                    if h == 0:
                        act.wait_ge(pv_done, TB * i + (mt + 1))
                    act.activation(ering[:, HG * (mt % 2) + h], ps[:, 4 + h % 2, :], ACT.Exp, scale=SCALE).then_inc(exp_ready, 1)

            def act_group(i, k):
                for mt in range(1, TB):
                    exps(i, mt)
                    if mt == 1 and (not isinstance(i, int) or i + 1 < NGR):
                        stage_values(i + 1, 1 - k)
                    if isinstance(i, int) and mt == 2 and i in TURN_IN:
                        turn_in(TURN_IN[i], 7)
                    if isinstance(i, int) and mt >= 2 and i in QK_IN:
                        qk_in(QK_IN[i], mt - 2, 7)
                if not isinstance(i, int) or i + 1 < NGR:
                    exps(i + 1, 0)
                act.wait_ge(pv_done, TB * i + (TB + 2))
                if not isinstance(i, int) or i >= 2:
                    act.wait_ge(o_turn, i - 1)
                act.activation(oT[:, k], ps[:, 6, :], ACT.Copy).then_inc(o_evac, 1)

            act.wait_ge(s_vs, 1)
            act.wait_ge(s_vvs, 2)
            stage_values(0, 0)
            act.wait_ge(comb, TOP_K * (HT + 2))
            exps(0, 0)
            act.wait_ge(comb, TOP_K * (HT + 4))
            for i in range(HEAD_GROUPS):
                act_group(i, i % 2)
            act.wait_ge(s_vvs, B)
            with act.Fori(HEAD_GROUPS // 2, NGR // 2 - 1) as j:
                i = act.snap(j * 2)
                act_group(i, 0)
                act_group(i + 1, 1)
            act_group(NGR - 2, 0)
            act_group(NGR - 1, 1)
            for b in range(B):
                turned(3 * B + b, xT[:, L * b:L * b + L])

            def mlp_input(b):
                act.wait_ge(s_tr, 4 * B + b + 1)
                act.activation(xp[:, 0, L * b:L * b + L], ps[:, 4 + b, :], ACT.Copy)
                act.activation(xT[:, L * b:L * b + L], ps[:, 4 + b, :], ACT.Copy).then_inc(s_trs, 1)

            def middle(n, dst, c):
                act.wait_ge(s_rest, n + 1)
                act.activation(dst[:, 1, c], rest[:, c], ACT.Copy).then_inc(s_mid, 1)

            def hidden(b, layer):
                dst = (h1, h2)[layer]
                for c in range(FC):
                    n = (2 * b + layer) * FC + c
                    act.wait_ge(s_f, n + 1)
                    if n >= FC:
                        act.wait_ge(s_fs, n - FC + 1)
                    act.activation(dst[:, 0, c], ps[:, c, :], ACT.Relu, scale=s_row[:, layer:layer + 1])
                    act.activation(hid[:, c], ps[:, c, :], ACT.Relu, scale=s_row[:, layer:layer + 1]).then_inc(s_hid, 1)
                    if c >= 1:
                        middle(n - 1, dst, c - 1)
                middle(n, dst, c)

            act.wait_ge(s_kf, 1)
            mlp_input(0)
            mlp_input(1)
            hidden(0, 0)
            mlp_input(2)
            for b in range(B):
                hidden(b, 1)
                if b == 0:
                    mlp_input(3)
                if b + 1 < B:
                    hidden(b + 1, 0)

        @block.vector
        def _(v):
            vn = [0]

            def own(ins):
                vn[0] += 1
                ins.then_inc(s_v, 1)
                v.wait_ge(s_v, vn[0])

            def stats(src, q):
                for t in range(TB * q, TB * q + TB):
                    ins = v.bn_stats(st[:, t], src[:, t])
                own(ins)
                for t in range(TB * q, TB * q + TB):
                    ins = v.bn_aggr(mv[:, t], st[:, t])
                ins.then_inc(s_st, 1)

            def normalise(dst, src, k):
                q = k % B
                v.wait_ge(s_rstd, k + 1)
                v.wait_ge(s_st, k + 1)
                for t in range(TB * q, TB * q + TB):
                    ins = v.tensor_scalar(dst[:, t], src[:, t], mv[:, t, 0:1], rstd[:, t:t + 1], ALU.subtract, ALU.mult)
                ins.then_inc(s_xn, 1)

            own(v.memset(cnt[:, 0:2], 0.0))
            v.sem_inc(acc_done, 2)
            v.sem_inc(s1_free, 2)
            v.sem_inc(exp_ready, 2)
            v.sem_inc(pv_done, 2)
            for q in range(B):
                v.wait_ge(s_x[q], 16)
                stats(xt, q)
            for q in range(B):
                normalise(tmp, xt, q)
            v.wait_ge(s_w, 16 * 16)
            v.wait_ge(s_decay, 2)
            for j in range(B // 2):
                v.wait_ge(s_u, 2 * j + 2)
                own(v.tensor_scalar(uT[:, j], ps[:, j, :], b_xp_s[:], None, ALU.add))
                v.tensor_tensor_scan(hT[:, j], decay[:].broadcast_to([P, L]), uT[:, j], 0.0, ALU.mult, ALU.add).then_inc(s_h, 1)
            for b in range(B):
                v.wait_ge(s_y, b + 1)
                v.wait_ge(s_xzs, B + b + 1)
                v.tensor_tensor(ysT[:, :, b], ps[:, 4 + b, :], zT[:, b], ALU.mult).then_inc(s_ys, 1)
            v.wait_ge(s_xb, 1)

            def add_mixer(q):
                v.wait_ge(s_yo, q + 1)
                own(v.tensor_tensor(tmp[:, TB * q:TB * q + TB], ps[:, q].rearrange("p (t m) -> p t m", m=M),
                                    xb[:, TB * q:TB * q + TB], ALU.add))
                stats(tmp, q)

            add_mixer(0)
            add_mixer(1)
            normalise(xt, tmp, B)
            normalise(xt, tmp, B + 1)
            add_mixer(2)
            add_mixer(3)

            v.wait_ge(s_const, 1)

            def route(f):
                ts = slice(HT * f, HT * f + HT)
                fsc, fch, fra, frb, fkeep, fgs, fcnt = sc[:, ts], ch[:, ts], ra[:, ts], rb[:, ts], keep[:, ts], gs[:, ts], cnt[:, ts]
                v.wait_ge(s_lgs, f + 1)
                own(v.tensor_tensor(fch, fsc, bias_row[:].unsqueeze(1).broadcast_to([P, HT, E]), ALU.add))
                c4 = fch.rearrange("p t (g a) -> p t g a", a=EG)
                m1, m2, m3, m4 = g1[:, ts], g2[:, ts], g3[:, ts], g4[:, ts]
                v.tensor_tensor(m1, c4[:, :, :, 0:4], c4[:, :, :, 4:8], ALU.max)
                own(v.tensor_tensor(m2, c4[:, :, :, 0:4], c4[:, :, :, 4:8], ALU.min))
                r4, q4 = (a[:, :, 0:2 * GROUPS].rearrange("p t (g a) -> p t g a", a=2) for a in (fra, frb))
                v.tensor_tensor(m3, m1[:, :, :, 0:2], m1[:, :, :, 2:4], ALU.max)
                v.tensor_tensor(r4, m1[:, :, :, 0:2], m1[:, :, :, 2:4], ALU.min)
                own(v.tensor_tensor(q4, m2[:, :, :, 0:2], m2[:, :, :, 2:4], ALU.max))
                own(v.tensor_tensor(m4, r4, q4, ALU.max))
                first, second, third = fra[:, :, 32:40], fra[:, :, 40:48], fra[:, :, 48:56]
                v.tensor_tensor(first, m3[:, :, :, 0], m3[:, :, :, 1], ALU.max)
                v.tensor_tensor(second, m3[:, :, :, 0], m3[:, :, :, 1], ALU.min)
                own(v.tensor_tensor(third, m4[:, :, :, 0], m4[:, :, :, 1], ALU.max))
                own(v.tensor_tensor(second, second, third, ALU.max))
                own(v.tensor_tensor(fgs, first, second, ALU.add))
                a4 = fra.rearrange("p t (g j) -> p t g j", j=GROUPS)
                b4 = frb.rearrange("p t (g j) -> p t g j", j=GROUPS)
                other = fgs.unsqueeze(2).broadcast_to([P, HT, GROUPS, GROUPS])
                mine = fgs.unsqueeze(3).broadcast_to([P, HT, GROUPS, GROUPS])
                v.tensor_tensor(a4, other, mine, ALU.is_gt)
                own(v.tensor_tensor(b4, other, mine, ALU.is_equal))
                own(v.tensor_tensor(b4, b4, before[:].unsqueeze(1).broadcast_to([P, HT, GROUPS, GROUPS]), ALU.mult))
                own(v.tensor_tensor(fra, fra, frb, ALU.add))
                own(v.tensor_reduce(fgs, a4, AX_X, ALU.add))
                own(v.tensor_scalar(fgs, fgs, float(GROUPS_KEPT), None, ALU.is_lt))
                own(v.tensor_tensor(c4, c4, fgs.unsqueeze(3).broadcast_to([P, HT, GROUPS, EG]), ALU.mult))
                for t in range(HT * f, HT * f + HT):
                    ins = v.max(top[:, t], ch[:, t])
                own(ins)
                eighth = top[:, ts, 7:8].broadcast_to([P, HT, E])
                v.tensor_tensor(fra, fch, eighth, ALU.is_gt)
                own(v.tensor_tensor(frb, fch, eighth, ALU.is_equal))
                own(v.tensor_reduce(fcnt, fra, AX_X, ALU.add))
                own(v.tensor_scalar(fcnt, fcnt, -1.0, float(TOP_K), ALU.mult, ALU.add))
                own(v.tensor_tensor_scan(fch.rearrange("p t e -> p (t e)"), fkeep.rearrange("p t e -> p (t e)"),
                                         frb.rearrange("p t e -> p (t e)"), 0.0, ALU.mult, ALU.add))
                own(v.tensor_tensor(fch, fch, fcnt.unsqueeze(2).broadcast_to([P, HT, E]), ALU.is_le))
                own(v.tensor_tensor(frb, frb, fch, ALU.mult))
                own(v.tensor_tensor(fra, fra, frb, ALU.add))
                own(v.tensor_copy(selb[:, f].rearrange("p e t -> p t e"), fra))
                own(v.tensor_tensor_scan(incb[:, f].rearrange("p e t -> p (e t)"), keep2[:].rearrange("p e t -> p (e t)"),
                                         selb[:, f].rearrange("p e t -> p (e t)"), 0.0, ALU.mult, ALU.add))
                v.tensor_tensor(exb[:, f], incb[:, f], selb[:, f], ALU.subtract).then_inc(s_cum, 1)
                v.wait_ge(s_pos, f + 1)
                above = frb.rearrange("p t e -> p (t e)").rearrange("p (e j) -> p e j", j=HT)
                own(v.tensor_tensor(above, ps[:, 6 + f, 0:E].unsqueeze(2).broadcast_to([P, E, HT]),
                                    thr[:].unsqueeze(1).broadcast_to([P, E, HT]), ALU.is_gt))
                own(v.tensor_reduce(nblk[:], above, AX_X, ALU.add))
                own(v.tensor_tensor_scan(endb[:], ones_e[:], nblk[:], 0.0, ALU.mult, ALU.add))
                own(v.tensor_tensor(baserow[:], endb[:], nblk[:], ALU.subtract))
                own(v.tensor_scalar(baserow[:], baserow[:], float(P), 1.0, ALU.mult, ALU.add))
                own(v.tensor_tensor(fch.rearrange("p t e -> p e t"), ps[:, 4 + f].rearrange("p (e t) -> p e t", t=HT),
                                    baserow[:].unsqueeze(2).broadcast_to([P, E, HT]), ALU.add))
                own(v.tensor_tensor(fch, fch, fra, ALU.mult))
                for t in range(HT * f, HT * f + HT):
                    ins = v.max(dst[:, t], ch[:, t])
                own(ins)
                v.tensor_scalar(idx[:, ts], dst[:, ts], -1.0, None, ALU.add).then_inc(s_idx, 1)
                own(v.tensor_scalar(ecmp[:], endb[:], bnum[:], None, ALU.is_le))
                own(v.tensor_reduce(eidf[:, f:f + 1], ecmp[:], AX_X, ALU.add))
                own(v.tensor_scalar(eid[:, f:f + 1], eidf[:, f:f + 1], float(E - 1), None, ALU.min))
                v.sem_inc(s_eid, 1)

            route(0)
            normalise(xt, tmp, B + 2)
            normalise(xt, tmp, B + 3)
            route(1)
            own(v.tensor_tensor(ra[:], ra[:], sc[:], ALU.mult))
            own(v.tensor_reduce(cnt[:], ra[:], AX_X, ALU.add))
            own(v.tensor_scalar(cnt[:], cnt[:], 1e-20, None, ALU.add))
            own(v.reciprocal(cnt[:], cnt[:]))
            own(v.tensor_scalar(cnt[:], cnt[:], ROUTED_SCALE, None, ALU.mult))
            own(v.tensor_tensor(rb[:], ra[:], cnt[:].unsqueeze(2).broadcast_to([P, NT, E]), ALU.mult))
            if STAGE < 2:
                v.wait_ge(s_xn, 2 * B)
                v.sem_inc(s_out, 1)
                return
            for t in range(NT + 2):
                if t < NT:
                    v.wait_ge(sg_ready, t + 1)
                    v.tensor_tensor(hm[:, t % 2, :, 0:I], sg[:, t % 2], ps[:, 2 + t % 2, I2:2 * I2].rearrange("p (a i) -> p a i", a=2),
                                    ALU.mult).then_inc(hm_ready, 1)
                if t >= 2:
                    v.wait_ge(d_ready, t - 1)
                    v.tensor_tensor(xb[:, t - 2], ps[:, 6 + t % 2, 0:M], xt[:, t - 2], ALU.add).then_inc(s_sh, 1)
                if t % 2 == 0 and t // 2 < TOP_K:
                    k = t // 2
                    own(v.tensor_tensor(ra[:], ch[:], dst[:, :, k:k + 1].broadcast_to([P, NT, E]), ALU.is_equal))
                    own(v.tensor_tensor(ra[:], ra[:], rb[:], ALU.mult))
                    own(v.tensor_reduce(wk[:, :, k], ra[:], AX_X, ALU.add))

            def dve_pair(s, u, earlier=0):
                static = isinstance(s, int)
                if not static or s < NPAIR:
                    v.wait_ge(xt_ready, s + 1)
                    v.tensor_copy(xbT[:, u % 2], ps[:, u % 2, 0:2 * P].rearrange("p (a m) -> p a m", a=2)).then_inc(x_copied, 1)
                if not static or 1 <= s <= NPAIR:
                    v.wait_ge(sg_ready, s + NT)
                    v.tensor_tensor(hm[:, (u - 1) % 2, :, 0:I], sg[:, (u - 1) % 2],
                                    ps[:, 2 + (u - 1) % 2, 0:2 * I2].rearrange("p (a i) -> p a i", a=2)[:, :, I:I2], ALU.mult).then_inc(hm_ready, 1)
                if not static or 3 <= s:
                    quad, part = (u - 3) // 2 % 4, (u - 3) % 2
                    if part == 0 and (not static or s >= 11):
                        v.wait_ge(stq[quad], 16 * ((s - 3) // 8) if static else earlier * 16 + (32 if u >= 3 else 16))
                    v.wait_ge(d_ready, s + (NT - 2))
                    v.tensor_copy(ob[:, quad, 2 * part:2 * part + 2], ps[:, 6 + (u - 3) % 2, 0:2 * M].rearrange("p (a m) -> p a m", a=2)).then_inc(acc_done, 1)

            for u in range(8):
                dve_pair(u, u)
            for u in range(8):
                dve_pair(8 + u, u)
            def add_row(t, k):
                if k >= 1:
                    v.wait_ge(comb, t * TOP_K + k)
                ts = bass.ds(t, 1)
                v.scalar_tensor_tensor(out=tmp[:, ts], in0=gb[:, bass.ds(t % 4, 1), k], scalar=wk[:, ts, k], in1=(tmp if k else xb)[:, ts],
                                       op0=ALU.mult, op1=ALU.add).then_inc(comb, 1)

            with v.Fori(0, BODIES) as j:
                s0 = v.snap(j * 8 + 16)
                for u in range(8):
                    dve_pair(s0 + u, u, j)
            with v.Fori(0, BODIES - 2) as t:
                s0 = v.snap(t * 8 + (8 * BODIES + 16))
                v.wait_ge(rows_back, t + 1)
                for u in range(8):
                    dve_pair(s0 + u, u, t + BODIES)
                    add_row(t, u)
            stats(tmp, 0)
            for u in range(3):
                dve_pair(NPAIR + u, u)
            normalise(xt, tmp, 2 * B)

            def combine_first():
                for k in range(TOP_K):
                    for t in range(HT - 2, HT):
                        if k == 0:
                            v.wait_ge(rows_back, t + 1)
                        v.scalar_tensor_tensor(out=tmp[:, t], in0=gb[:, t % 4, k], scalar=wk[:, t, k:k + 1], in1=(tmp if k else xb)[:, t],
                                               op0=ALU.mult, op1=ALU.add).then_inc(comb, 1)
                    v.wait_ge(comb, TOP_K * (HT - 2) + 2 * k + 2)

            def combine(tiles, k):
                for n, t in enumerate(tiles):
                    slot, landed, count = back_slot(t)
                    if k == 0:
                        v.wait_ge(landed, count)
                    else:
                        v.wait_ge(comb, TOP_K * (HT + tiles[0]) + len(tiles) * (k - 1) + n + 1)
                    v.scalar_tensor_tensor(out=tmp[:, HT + t], in0=slot[:, k], scalar=wk[:, HT + t, k:k + 1],
                                           in1=(tmp if k else xb)[:, HT + t], op0=ALU.mult, op1=ALU.add).then_inc(comb, 1)
                if k == TOP_K - 1:
                    v.wait_ge(comb, TOP_K * (HT + tiles[-1] + 1))

            def qk_parts(b, o):
                v.wait_ge(s_qks, 2 * b + o + 1)
                own(v.tensor_tensor(qr[:, o], qf[:, o], parts[:, o, 0], ALU.subtract))
                own(v.tensor_copy(parts[:, o, 1], qr[:, o]))
                v.tensor_tensor(parts[:, o, 2], qr[:, o], parts[:, o, 1], ALU.subtract).then_inc(s_part, 1)

            def v_in(b, bank):
                v.wait_ge(s_vv, b + 1)
                v.tensor_tensor(vt[:, GB * b:GB * b + GB].rearrange("p g m c -> p m g c"),
                                ps[:, bank].rearrange("p (m g c) -> p m g c", m=TB, g=GB),
                                rows[:, 1:2].rearrange("p a (g c) -> p a g c", g=GB).broadcast_to([P, TB, GB, HG * HD]),
                                ALU.add).then_inc(s_vvs, 1)

            v.wait_ge(s_wa, 16 * 9)
            for o in range(2):
                qk_parts(0, o)
            combine_first()
            stats(tmp, 1)
            v_in(0, 6)
            normalise(xt, tmp, 2 * B + 1)
            for o in range(2):
                qk_parts(1, o)
            v_in(1, 6)
            for k in range(TOP_K):
                combine(COMBINED[-2], k)
            for r in range(4):
                v.wait_ge(stq[r], 32 * BODIES)

            def row_max(i, k, h, a):
                v.wait_ge(s1_ready, 2 * HG * i + (2 * h + a + 1))
                v.tensor_reduce(mx[:, k, TB * h + 2 * a:TB * h + 2 * a + 2], ps[:, 2 * a:2 * a + 2, :], AX_X,
                                ALU.max).then_inc(s1_free, 1)

            def copy_max(i, k):
                v.wait_ge(mT_ready, i + 1)
                if not (isinstance(i, int) and i < 2):
                    v.wait_ge(max_in, 16 * NP * i - 16 * NP)
                v.tensor_copy(mT[:, k], ps[0:NP * HG * TB, 7, 0:P // 2].bitcast(BF16)).then_inc(mT_copied, 1)

            def norm_out(i, k, step):
                turnedv = ps[:, 7].rearrange("p (m h c) -> p m h c", m=TB, h=HG)
                if step == 0:
                    v.wait_ge(o_turn, i + 1)
                    v.reciprocal(rc[:], turnedv[:, :, :, HD]).then_inc(rc_done, 1)
                    return
                v.wait_ge(rc_done, i + 1)
                dst = otg[:, bass.ds(i // GB, 1), :, bass.ds(i % GB, 1), :].rearrange("p b m g (h c) -> p (b m) (g h) c", h=HG)
                v.tensor_tensor(dst, turnedv[:, :, :, 0:HD], rc[:].unsqueeze(3).broadcast_to([P, TB, HG, HD]),
                                ALU.mult).then_inc(o_norm, 1)

            def split_max(i, k, step):
                nm, r = mx[:, k], mr[:, k]
                if step == 0:
                    v.wait_ge(s1_free, 2 * HG * i + (2 * HG + 2))
                    if not (isinstance(i, int) and i < 2):
                        v.wait_ge(mT_ready, i - 1)
                    v.scalar_tensor_tensor(out=mp[:, k, 0], in0=nm, scalar=-1.0, in1=zeros[:, 0:HG * TB], op0=ALU.mult, op1=ALU.add).then_inc(s_r, 1)
                elif step == 1:
                    v.wait_ge(s_r, 3 * i + 1)
                    v.scalar_tensor_tensor(out=r, in0=nm, scalar=-1.0, in1=mp[:, k, 0], op0=ALU.mult, op1=ALU.subtract).then_inc(s_r, 1)
                elif step == 2:
                    v.wait_ge(s_r, 3 * i + 2)
                    v.tensor_copy(mp[:, k, 1], r).then_inc(s_r, 1)
                else:
                    v.wait_ge(s_r, 3 * i + 3)
                    v.tensor_tensor(mp[:, k, 2], r, mp[:, k, 1], ALU.subtract).then_inc(split_done, 1)

            def dve_group(i, k):
                ahead = not isinstance(i, int) or i + 2 < NGR
                after = not isinstance(i, int) or i + 1 < NGR
                for h in range(HG):
                    for a in range(2):
                        if ahead:
                            row_max(i + 2, k, h, a)
                        if after and h == 0 and a == 1:
                            copy_max(i + 1, 1 - k)
                        if isinstance(i, int) and i in COMBINED:
                            combine(COMBINED[i], 2 * h + a)
                        if isinstance(i, int) and i in V_IN and h == 2 and a == 0:
                            v_in(V_IN[i], 7)
                out = not isinstance(i, int) or i >= 1
                for step in range(4):
                    if ahead:
                        split_max(i + 2, k, step)
                    if out and step < 2:
                        norm_out(i - 1, 1 - k, step)

            for h in range(HG):
                for a in range(2):
                    row_max(0, 0, h, a)
            for step in range(4):
                split_max(0, 0, step)
            for h in range(HG):
                for a in range(2):
                    row_max(1, 1, h, a)
                    combine(COMBINED[-1], 2 * h + a)
                if h == 0:
                    copy_max(0, 0)
            stats(tmp, 2)
            for step in range(4):
                split_max(1, 1, step)
            for i in range(HEAD_GROUPS):
                dve_group(i, i % 2)
                if i == 0:
                    normalise(xt, tmp, 2 * B + 2)
                elif i == 2:
                    stats(tmp, 3)
                elif i == 3:
                    normalise(xt, tmp, 2 * B + 3)
            with v.Fori(HEAD_GROUPS // 2, NGR // 2 - 1) as j:
                i = v.snap(j * 2)
                dve_group(i, 0)
                dve_group(i + 1, 1)
            dve_group(NGR - 2, 0)
            dve_group(NGR - 1, 1)
            for step in range(2):
                norm_out(NGR - 1, 1, step)
            v.wait_ge(s_xb, 2)

            def add_x(q):
                v.wait_ge(s_pr, q + 1)
                own(v.tensor_tensor(tmp[:, TB * q:TB * q + TB], ps[:, 4 + q].rearrange("p (t m) -> p t m", m=M),
                                    xb[:, TB * q:TB * q + TB], ALU.add))
                stats(tmp, q)

            def mlp_input(q):
                v.wait_ge(s_trs, 4 * B + q + 1)
                cols = slice(L * q, L * q + L)
                own(v.tensor_tensor(qr[:, q % 2], xT[:, cols], xp[:, 0, cols], ALU.subtract))
                own(v.tensor_copy(xp[:, 1, cols], qr[:, q % 2]))
                v.tensor_tensor(xp[:, 2, cols], qr[:, q % 2], xp[:, 1, cols], ALU.subtract).then_inc(s_xp, 1)

            def last_part(n, dst, c):
                v.wait_ge(s_mid, n + 1)
                v.tensor_tensor(dst[:, 2, c], rest[:, c], dst[:, 1, c], ALU.subtract).then_inc(s_fs, 1)

            def hidden(b, layer):
                dst = (h1, h2)[layer]
                for c in range(FC):
                    n = (2 * b + layer) * FC + c
                    v.wait_ge(s_hid, n + 1)
                    v.tensor_tensor(rest[:, c], hid[:, c], dst[:, 0, c], ALU.subtract).then_inc(s_rest, 1)
                    if c >= 1:
                        last_part(n - 1, dst, c - 1)
                last_part(n, dst, c)

            def add_mlp(q):
                v.wait_ge(s_fo, q + 1)
                own(v.scalar_tensor_tensor(out=tmp[:, TB * q:TB * q + TB], in0=ps[:, 4 + q].rearrange("p (t m) -> p t m", m=M),
                                           scalar=s_row[:, 2:3], in1=xt[:, TB * q:TB * q + TB], op0=ALU.mult, op1=ALU.add))
                stats(tmp, q)

            add_x(0)
            add_x(1)
            normalise(xt, tmp, 3 * B)
            add_x(2)
            normalise(xt, tmp, 3 * B + 1)
            mlp_input(0)
            add_x(3)
            normalise(xt, tmp, 3 * B + 2)
            mlp_input(1)
            hidden(0, 0)
            normalise(xt, tmp, 3 * B + 3)
            mlp_input(2)
            for b in range(B):
                hidden(b, 1)
                if b == 0:
                    mlp_input(3)
                else:
                    normalise(xt, tmp, 4 * B + b - 1)
                if b + 1 < B:
                    hidden(b + 1, 0)
                add_mlp(b)
            normalise(xt, tmp, 5 * B - 1)

        @block.tensor
        def _(pe):
            pe.wait_ge(s_w, 16)

            def turn(k, src):
                if k >= B:
                    pe.wait_ge(s_trs, k - B + 1)
                for t in range(TB):
                    ins = pe.transpose(ps[:, k % B, P * t:P * t + P], src(TB * (k % B) + t), idf[:])
                ins.then_inc(s_tr, 1)

            for b in range(B):
                pe.wait_ge(s_xn, b + 1)
                turn(b, lambda t: tmp[:, t])
            pe.wait_ge(s_w, 16 * 16)
            def to_xz(b, o):
                pe.matmul(ps[:, 4 + b, :], w_in_s[:, M * o:M * o + M], xT[:, L * b:L * b + L], start=True, stop=True).then_inc(s_xz, 1)

            for b in range(B):
                pe.wait_ge(s_trs, b + 1)
                to_xz(b, 0)
            for b in range(B):
                pe.wait_ge(s_xzs, b + 1)
                h = S * (b % 2)
                pe.matmul(ps[h:h + S, b // 2, :], w_xp_s[:], xpT[:, b], start=True, stop=True).then_inc(s_u, 1)
                to_xz(b, 1)
            for b in range(B):
                pe.wait_ge(s_xzs, B + b + 1)
                pe.wait_ge(s_h, b // 2 + 1)
                h = S * (b % 2)
                pe.matmul(ps[:, 4 + b, :], dmat_s[h:h + S], hT[h:h + S, b // 2], start=True, stop=True).then_inc(s_y, 1)
            pe.wait_ge(s_ys, B)
            for q in range(B):
                for t in range(TB):
                    l = (TB * q + t) * P // B
                    ins = pe.matmul(ps[:, q, P * t:P * t + P], ysT[:, l:l + P // B, :].rearrange("p l b -> p (l b)"), w_out_s[:],
                                    start=True, stop=True)
                ins.then_inc(s_yo, 1)
            for f in range(2):
                for b in range(2 * f, 2 * f + 2):
                    pe.wait_ge(s_xn, B + b + 1)
                    turn(B + b, lambda t: xt[:, t])
                for t in range(HT):
                    if t % TB == 0:
                        pe.wait_ge(s_trs, B + 2 * f + t // TB + 1)
                    ins = pe.matmul(ps[:, 4 + f, E * t:E * t + E], xT[:, P * (HT * f + t):P * (HT * f + t) + P], gate_s[:],
                                    start=True, stop=True)
                ins.then_inc(s_lg, 1)
                pe.wait_ge(s_const, 1)
                pe.wait_ge(s_cum, f + 1)
                pe.matmul(ps[:, 4 + f, :], tri[:], selb[:, f].rearrange("p e t -> p (e t)"), start=True, stop=False)
                pe.matmul(ps[:, 4 + f, :], onesb[:], exb[:, f].rearrange("p e t -> p (e t)"), start=False, stop=True)
                pe.matmul(ps[:, 6 + f, 0:E], onesb[:], incb[:, f, :, HT - 1], start=True, stop=True).then_inc(s_pos, 1)
            pe.wait_ge(s_we, 64)
            pe.wait_ge(s_lgs, 2)
            pe.wait_ge(s_idx, 2)
            for t in range(NT + 2):
                if t < NT:
                    pe.matmul(ps[:, 2 + t % 2, 0:2 * I2], xT[:, P * t:P * t + P], wsh_s[:], start=True, stop=True).then_inc(gu_ready, 1)
                if 1 <= t <= NT:
                    pe.wait_ge(hm_ready, t)
                    for a in range(2):
                        ins = pe.transpose(ps[0:KI, 4 + (t - 1) % 2, P * a:P * a + P], hm[:, (t - 1) % 2, a], idf[:])
                    ins.then_inc(th_ready, 1)
                if t >= 2:
                    pe.wait_ge(th_copied, t - 1)
                    if t >= 4:
                        pe.wait_ge(s_sh, t - 3)
                    for a in range(2):
                        ins = pe.matmul(ps[:, 6 + t % 2, 0:M], hmT[0:KI, t % 2, a], wshd_s[0:KI, a], start=(a == 0), stop=(a == 1))
                    ins.then_inc(d_ready, 1)

            def pe_pair(s, u, expert):
                static = isinstance(s, int)
                if not static or s < NPAIR:
                    quad, part = u // 2, u % 2
                    if part == 0:
                        pe.wait_ge(ld[quad], 16 * (s // 8) + 16 if static else s // 8 * 16 + 16)
                    for a in range(2):
                        ins = pe.transpose(ps[:, u % 2, P * a:P * a + P], xin[:, quad, 2 * part + a], idf[:])
                    ins.then_inc(xt_ready, 1)
                if not static or 1 <= s <= NPAIR:
                    pe.wait_ge(x_copied, s + 0)
                    for a in range(2):
                        ins = pe.matmul(ps[:, 2 + (u - 1) % 2, I2 * a:I2 * a + I2], xbT[:, (u - 1) % 2, a],
                                        wgu_s[:, bass.ds(expert(2 * (u - 1) + a), 1), :].rearrange("p a n -> p (a n)"), start=True, stop=True)
                    ins.then_inc(gu_ready, 1)
                if not static or 2 <= s <= NPAIR + 1:
                    pe.wait_ge(hm_ready, s + (NT - 1))
                    for a in range(2):
                        ins = pe.transpose(ps[0:KI, 4 + u % 2, P * a:P * a + P], hm[:, u % 2, a], idf[:])
                    ins.then_inc(th_ready, 1)
                if not static or 3 <= s:
                    pe.wait_ge(th_copied, s + (NT - 2))
                    pe.wait_ge(acc_done, s - 2)
                    for a in range(2):
                        ins = pe.matmul(ps[:, 6 + (u - 3) % 2, M * a:M * a + M], hmT[0:KI, (u - 3) % 2, a],
                                        wd_s[0:KI, bass.ds(expert(2 * (u - 3) + a), 1), :].rearrange("p a n -> p (a n)"), start=True, stop=True)
                    ins.then_inc(d_ready, 1)

            def experts_of(first, blocks):
                _, got = nc.values_load_multi_w_load_instructions(
                    tab[0:1, bass.ds(first + (AHEAD + blocks[0]), len(blocks))], engines=[mybir.EngineType.PE],
                    min_val=0, max_val=E - 1, skip_runtime_bounds_check_because="the table holds minima with E - 1")
                return lambda b: got[b - blocks[0]]

            pe.wait_ge(s_tab, 32)
            pe.wait_ge(s_sh, NT)
            chosen = experts_of(0, range(-6, 14))
            for u in range(8):
                pe_pair(u, u, chosen)
            with pe.Fori(1, NB // BODY) as j:
                chosen = experts_of(j * BODY, range(-6, 14))
                s0 = pe.snap(j * 8)
                for u in range(8):
                    pe_pair(s0 + u, u, chosen)
            chosen = experts_of(NB, range(-6, 0))
            for u in range(3):
                pe_pair(NPAIR + u, u, chosen)
            if STAGE < 3:
                for b in range(B):
                    pe.wait_ge(s_xn, 2 * B + b + 1)
                    turn(2 * B + b, lambda t: xt[:, t])
                return
            pe.wait_ge(s_wa, 16 * 9)
            pe.wait_ge(s_idb, 1)

            def turn_in(b, bank):
                pe.wait_ge(s_xn, 2 * B + b + 1)
                for t in range(TB):
                    ins = pe.transpose(ps[:, bank, P * t:P * t + P], xt[:, TB * b + t], idf[:])
                ins.then_inc(s_tr, 1)

            def q_or_k(b, o, bank):
                pe.wait_ge(s_trs, 2 * B + b + 1)
                if b >= 1:
                    pe.wait_ge(s_qks, 2 * b + (o if bank == 7 else 0))
                pe.matmul(ps[:, bank, :], w_qkv_s[:, M * o:M * o + M], xT[:, L * b:L * b + L], start=True, stop=True).then_inc(s_qk, 1)

            def v_in(b, bank):
                if b >= 1:
                    pe.wait_ge(s_vvs, b)
                for t in range(TB):
                    ins = pe.matmul(ps[:, bank, P * t:P * t + P], xT[:, L * b + P * t:L * b + P * t + P], w_qkv_s[:, 2 * M:3 * M],
                                    start=True, stop=True)
                ins.then_inc(s_vv, 1)

            for b in range(2):
                turn_in(b, b)
                for o in range(2):
                    q_or_k(b, o, 4 + o)
                v_in(b, 6)

            def head(i, h):
                if isinstance(i, int):
                    return slice(HG * (i % (2 * GB)) + h, HG * (i % (2 * GB)) + h + 1)
                return bass.ds(i % (2 * GB) * HG + h, 1)

            def flat(ap):
                return ap.rearrange("p a n -> p (a n)")

            def max_scores(i, h, c):
                if c % 2 == 0:
                    pe.wait_ge(s1_free, 2 * HG * i + (2 * h + c // 2 + 1))
                ins = pe.matmul(ps[:, c, :], flat(kst[0:KD, head(i, h), P * c:P * c + P]), flat(qst[0:KD, head(i, h), :]),
                                start=True, stop=True)
                if c % 2:
                    ins.then_inc(s1_ready, 1)

            def scores(i, mt, h):
                if mt == 0 and h == 0:
                    pe.wait_ge(max_in, 16 * NP * i + 16 * NP)
                pe.wait_ge(exp_ready, HG * TB * i + (HG * mt + h + 1))
                pe.matmul(ps[:, 4 + h % 2, :], flat(qst[0:KS, head(i, h), P * mt:P * mt + P]), flat(kst[0:KS, head(i, h), :]),
                          start=True, stop=True).then_inc(s2_ready, 1)

            def values(i, k, mt):
                if mt == 0:
                    pe.wait_ge(vs_ready, i + 1)
                    if not isinstance(i, int) or i >= 1:
                        pe.wait_ge(o_evac, i)
                pe.wait_ge(exp_ready, HG * TB * i + (HG * (mt + 1) + 2))
                for h in range(HG):
                    ins = pe.matmul(ps[32 * h:32 * h + 32, 6, :], vs[:, k, mt, h], ering[:, HG * (mt % 2) + h],
                                    start=(mt == 0), stop=(mt == TB - 1))
                ins.then_inc(pv_done, 1)

            def turn_max(i, k):
                pe.wait_ge(split_done, i + 1)
                if not isinstance(i, int) or i >= 3:
                    pe.wait_ge(o_norm, i - 2)
                pe.transpose(ps[:, 7, 0:P // 2].bitcast(BF16), mp[:, k].rearrange("p c n -> p (c n)"), idb[:]).then_inc(mT_ready, 1)

            def turn_out(i, k):
                pe.wait_ge(o_evac, i + 1)
                if isinstance(i, int):
                    bank_back(i + 1)
                if not isinstance(i, int) or i + 2 < NGR:
                    pe.wait_ge(mT_copied, i + 3)
                else:
                    pe.wait_ge(o_norm, i)
                for c in range(TB):
                    ins = pe.transpose(ps[:, 7, P * c:P * c + P], oT[:, k, P * c:P * c + P], idf[:])
                ins.then_inc(o_turn, 1)

            def pe_group(i, k):
                static = isinstance(i, int)
                ahead, after = not static or i + 2 < NGR, not static or i + 1 < NGR
                if ahead:
                    pe.wait_ge(stack_ready, (i + 2) // GB + 2)
                for mt in range(TB):
                    for what, h in (("s", 0), ("s", 1), ("m", 0), ("m", 1), ("m", 2), ("s", 2), ("m", 3), ("s", 3)):
                        if what == "m":
                            if ahead:
                                max_scores(i + 2, mt, h)
                            continue
                        if mt == 0 and h == 3 and after:
                            turn_max(i + 1, 1 - k)
                        if mt == 1 and h == 3 and static and i < HEAD_GROUPS:
                            later_sequence(i, 0)
                        if mt == 2 and h == 2 and static and i < HEAD_GROUPS:
                            later_sequence(i, 1)
                        if mt == 3 and h == 2 and after and (not static or i >= 1):
                            turn_out(i - 1, 1 - k)
                        if mt < TB - 1:
                            scores(i, mt + 1, h)
                        elif after:
                            scores(i + 1, 0, h)
                    values(i, k, mt)

            def later_sequence(i, step):
                if step == 0 and (i in TURN_IN or i in QK_IN or i in V_IN):
                    pe.wait_ge(mT_copied, i + 2)
                if step == 0 and i in TURN_IN:
                    turn_in(TURN_IN[i], 7)
                if i in QK_IN:
                    q_or_k(QK_IN[i], step, 7)
                if step == 0 and i in V_IN:
                    v_in(V_IN[i], 7)

            def bank_back(i):
                if i in TURN_IN:
                    pe.wait_ge(s_trs, 2 * B + TURN_IN[i] + 1)
                if i in QK_IN:
                    pe.wait_ge(s_qks, 2 * QK_IN[i] + 2)
                if i in V_IN:
                    pe.wait_ge(s_vvs, V_IN[i] + 1)

            pe.wait_ge(stack_ready, 1)
            pe.wait_ge(s_qks, 4)
            pe.wait_ge(s_vvs, 2)
            for h in range(HG):
                for c in range(TB):
                    max_scores(0, h, c)
            turn_max(0, 0)
            pe.wait_ge(stack_ready, 2)
            for h in range(HG):
                for c in range(TB):
                    max_scores(1, h, c)
            for h in range(HG):
                scores(0, 0, h)
            for i in range(HEAD_GROUPS):
                pe_group(i, i % 2)
            with pe.Fori(HEAD_GROUPS // 2, NGR // 2 - 1) as j:
                i = pe.snap(j * 2)
                pe_group(i, 0)
                pe_group(i + 1, 1)
            pe_group(NGR - 2, 0)
            pe_group(NGR - 1, 1)
            turn_out(NGR - 2, 0)
            turn_out(NGR - 1, 1)
            def out_in(b):
                pe.wait_ge(o_norm, GB * (b + 1))
                turn(3 * B + b, lambda t: ot[:, t])

            def project(b):
                pe.wait_ge(s_trs, 3 * B + b + 1)
                for t in range(TB):
                    ins = pe.matmul(ps[:, 4 + b, P * t:P * t + P], xT[:, L * b + P * t:L * b + P * t + P], w_o_s[:], start=True, stop=True)
                ins.then_inc(s_pr, 1)

            for b in range(B - 1):
                out_in(b)
            for b in range(B - 1):
                project(b)
            out_in(B - 1)
            project(B - 1)

            def mlp_input(b):
                pe.wait_ge(s_xn, 3 * B + b + 1)
                for t in range(TB):
                    ins = pe.transpose(ps[:, 4 + b, P * t:P * t + P], xt[:, TB * b + t], idf[:])
                ins.then_inc(s_tr, 1)

            def hidden(b, layer):
                for c in range(FC):
                    n = (2 * b + layer) * FC + c
                    if n >= FC:
                        pe.wait_ge(s_hid, n - FC + 1)
                    if layer == 0 and c == 0:
                        pe.wait_ge(s_xp, b + 1)
                    for kk in range(FC if layer else 1):
                        if layer == 1 and c == 0:
                            pe.wait_ge(s_fs, 2 * b * FC + kk + 1)
                        w = w1[:, kk, P * c:P * c + P] if layer else w0[:, P * c:P * c + P]
                        for part in range(NP):
                            ins = pe.matmul(ps[:, c, :], w, h1[:, part, kk] if layer else xp[:, part, L * b:L * b + L],
                                            start=(kk == 0 and part == 0), stop=(part == NP - 1 and (not layer or kk == FC - 1)))
                    ins.then_inc(s_f, 1)

            def mlp_output(b):
                for kk in range(FC):
                    pe.wait_ge(s_fs, (2 * b + 1) * FC + kk + 1)
                for t in range(TB):
                    for kk in range(FC):
                        for part in range(NP):
                            ins = pe.matmul(ps[:, 4 + b, P * t:P * t + P], h2[:, part, kk, P * t:P * t + P], w2[:, kk],
                                            start=(kk == 0 and part == 0), stop=(kk == FC - 1 and part == NP - 1))
                ins.then_inc(s_fo, 1)

            pe.wait_ge(s_kf, 1)
            mlp_input(0)
            mlp_input(1)
            hidden(0, 0)
            mlp_input(2)
            for b in range(B):
                hidden(b, 1)
                if b == 0:
                    mlp_input(3)
                if b + 1 < B:
                    hidden(b + 1, 0)
                mlp_output(b)


def kernel(**inputs):
    import numpy as np
    import concourse.bacc as bacc
    from concourse import mybir as mb
    from concourse.bass_utils import run_bass_kernel_spmd

    a = {k: np.asarray(v) for k, v in inputs.items()}
    wg, wu, wd = a["L0_ffn_Wg"], a["L0_ffn_Wu"], a["L0_ffn_Wd"]
    i = wg.shape[1]
    arrays = {
        "x": a["L0_attn_x"], "a_log": a["L0_attn_A_log"].reshape(-1, 1), "dmat": a["L0_attn_Dmat"],
        "w_in": a["L0_attn_W_in"].T, "b_in": a["L0_attn_b_in"].reshape(2, P).T, "w_xp": a["L0_attn_W_xp"].T,
        "b_xp": a["L0_attn_b_xp"].reshape(-1, 1), "w_out": a["L0_attn_W_out"].T, "b_out": a["L0_attn_b_out"].reshape(1, P),
        "gamma": a["L0_attn_gamma"].reshape(P, 1), "beta": a["L0_attn_beta"].reshape(P, 1),
        "gate_w": a["L0_ffn_gate_w"].T, "gate_bias": a["L0_ffn_gate_bias"].reshape(1, -1), 
        "w_gu": np.concatenate([wg, wu], axis=1).transpose(2, 0, 1), "w_d": wd.transpose(2, 0, 1),
        "w_sh": np.concatenate([a["L0_ffn_Sg"], a["L0_ffn_Su"]]).T,
        "w_shd": a["L0_ffn_Sd"].reshape(P, 2, i).transpose(2, 1, 0),
        "w_qkv": np.concatenate([a["L1_attn_Wq"], a["L1_attn_Wk"], a["L1_attn_Wv"]]).T,
        "b_qk": np.stack([a["L1_attn_bq"], a["L1_attn_bk"]], axis=1), "b_v": a["L1_attn_bv"].reshape(1, P),
        "w_o": a["L1_attn_Wo"].T, "b_o": a["L1_attn_bo"].reshape(1, P),
        "k0": a["L1_ffn_k0"], "k1": a["L1_ffn_k1"], "k2": a["L1_ffn_k2"],
        "s012": np.stack([a["L1_ffn_s0"], a["L1_ffn_s1"], a["L1_ffn_s2"]]).reshape(1, 3),
        "ident": np.eye(P, dtype=np.float32),
    }
    arrays = {k: np.ascontiguousarray(v) for k, v in arrays.items()}
    nc = bacc.Bacc("TRN2", target_bir_lowering=False, num_devices=1)
    args = {k: nc.dram_tensor(k, v.shape, mb.dt.from_np(v.dtype), kind="ExternalInput").ap() for k, v in arrays.items()}
    out = nc.dram_tensor("out", a["L0_attn_x"].shape, mb.dt.float32, kind="ExternalOutput").ap()
    build(nc, **args, out=out)
    return run_bass_kernel_spmd(nc, [arrays], core_ids=[0]).results[0]["out"]
```

```python
from contextlib import ExitStack

import concourse.bass as bass
from concourse import mybir

P = 128
ALU = mybir.AluOpType
ACT = mybir.ActivationFunctionType
F32 = mybir.dt.float32
BF16 = mybir.dt.bfloat16
U8 = mybir.dt.uint8
U32 = mybir.dt.uint32
I32 = mybir.dt.int32
AX_X = mybir.AxisListType.X
EPS = 1e-5
ROUTED_SCALE = 2.5
HEADS = 16
GROUPS = 8
GROUPS_KEPT = 4
TOP_K = 8


def build(nc, x, a_log, dmat, w_in, b_in, w_xp, b_xp, w_out, b_out, gamma, beta,
          gate_w, gate_bias, w_gu, w_d, w_sh, w_shd, w_qkv, b_qk, b_v, w_o, b_o, k0, k1, k2, s012, ident, out):
    B, L, M = x.shape
    T = B * L
    NT = T // P
    TB = L // P
    S = dmat.shape[0]
    E = gate_w.shape[1]
    EG = E // GROUPS
    I2 = w_gu.shape[2]
    I = I2 // 2
    KI = 96
    TILES = (NT * 3 // 8, NT - NT * 3 // 8)
    FIRST = (0, TILES[0])
    BODY = 16
    BLOCKS = [-(-(n * P * TOP_K + E * (P - 1)) // (P * BODY)) * BODY for n in TILES]
    BODIES = [n // BODY for n in BLOCKS]
    NB = sum(BLOCKS)
    NPAIR = NB // 2
    COLS = [-(-n // P) for n in BLOCKS]
    HT = NT // 2
    AHEAD = 8
    HD = M // HEADS
    HG = 4
    GB = HEADS // HG
    NGR = B * GB
    SCALE = float(M) ** -0.5
    TURN_IN, QK_IN, V_IN = {2: 2, 5: 3}, {3: 2, 6: 3}, {4: 2, 7: 3}
    HEAD_GROUPS = 8
    COMBINED = {-2: (6, 7), -1: (8, 9), 0: (10, 11), 1: (12,), 2: (13,), 3: (14, 15)}
    NP = 3
    KD = 96
    KS = KD + NP
    F = k1.shape[0]
    FC = F // P

    with ExitStack() as ctx:
        def sb(name, shape, dt=F32):
            return ctx.enter_context(nc.sbuf_tensor(name, shape, dt))

        def sem(name):
            return ctx.enter_context(nc.semaphore(name))

        xt = sb("xt", [P, NT, M])
        xT = sb("xT", [P, T])
        tmp = sb("tmp", [P, NT, M])
        xb = sb("xb", [P, NT, M])
        big = sb("big", [P, 4, T])
        zT, xpT = big[:, 0].rearrange("p (b l) -> p b l", b=B), big[:, 1].rearrange("p (b l) -> p b l", b=B)
        uT = big[:, 2, 0:T // 2].rearrange("p (b l) -> p b l", b=B // 2)
        hT = big[:, 2, T // 2:T].rearrange("p (b l) -> p b l", b=B // 2)
        ysT = big[:, 3].rearrange("p (l b) -> p l b", b=B)
        st = sb("st", [P, NT, 6])
        mv = sb("mv", [P, NT, 2])
        rstd = sb("rstd", [P, NT])
        minus_half = sb("minus_half", [P, TB])
        idf = sb("idf", [P, P])
        idb = sb("idb", [P, P], BF16)
        w_in_s = sb("w_in_s", [P, 2 * M])
        w_xp_s = sb("w_xp_s", [P, S])
        dmat_s = sb("dmat_s", [P, M])
        w_out_s = sb("w_out_s", [P, M])
        gamma_s, beta_s = sb("gamma_s", [P, 1]), sb("beta_s", [P, 1])
        b_in_s = sb("b_in_s", [P, 2])
        b_xp_s, decay = sb("b_xp_s", [P, 1]), sb("decay", [P, 1])
        b_qk_s = sb("b_qk_s", [P, 2])
        rows = sb("rows", [P, 3, M])
        bias_row = sb("bias_row", [P, E])
        gate_s = sb("gate_s", [P, E])
        sc = sb("sc", [P, NT, E])
        ch = sb("ch", [P, NT, E])
        ra = sb("ra", [P, NT, E])
        rb = sb("rb", [P, NT, E])
        gs = sb("gs", [P, NT, GROUPS])
        g1, g2 = sb("g1", [P, NT, GROUPS, 4]), sb("g2", [P, NT, GROUPS, 4])
        g3, g4 = sb("g3", [P, NT, GROUPS, 2]), sb("g4", [P, NT, GROUPS, 2])
        top = sb("top", [P, NT, 8])
        cnt = sb("cnt", [P, NT])
        before = sb("before", [P, GROUPS, GROUPS])
        keep = sb("keep", [P, NT, E])
        places = sb("places", [P, 3, E * NT], BF16)
        selb, incb, exb = ([places[:, i, E * FIRST[f]:E * (FIRST[f] + TILES[f])].rearrange("p (e t) -> p e t", t=TILES[f])
                            for f in range(2)] for i in range(3))
        keep2 = [sb(f"keep2{f}", [P, E, TILES[f]], BF16) for f in range(2)]
        tri, onesb = sb("tri", [P, P], BF16), sb("onesb", [P, P], BF16)
        ones_e = sb("ones_e", [P, E])
        nblk, endb, baserow = sb("nblk", [P, E]), sb("endb", [P, E]), sb("baserow", [P, E])
        thr = sb("thr", [P, TILES[1]])
        bnum = sb("bnum", [P, 2])
        ecmp = sb("ecmp", [P, E])
        eidf, eid = sb("eidf", [P, sum(COLS)]), sb("eid", [P, sum(COLS)], I32)
        tab = sb("tab", [1, AHEAD + NB], I32)
        dst = sb("dst", [P, NT, TOP_K])
        idx = sb("idx", [P, NT, TOP_K], U32)
        wk = sb("wk", [P, NT, TOP_K])
        wsum = sb("wsum", [P, TOP_K])
        picked = g1[:].rearrange("p t g a -> p (t g a)").rearrange("p (k e) -> p k e", e=E)
        sg = sb("sg", [P, 2, 2, I])
        hm = sb("hm", [P, 2, 2, KI])
        hmT = sb("hmT", [P, 2, 2, P])
        xbT = sb("xbT", [P, 2, 2, P])
        wsh_s = sb("wsh_s", [P, 2 * I2])
        wshd_s = sb("wshd_s", [P, 2, M])
        w_qkv_s = sb("w_qkv_s", [P, 3 * M])
        w_o_s = sb("w_o_s", [P, M])
        kb = sb("kb", [P, 2, F], U8)
        kb1 = sb("kb1", [P, FC, F], U8)
        kb2 = sb("kb2", [P, FC, M], U8)
        s_row = sb("s_row", [P, 3])
        arena = sb("arena", [P, E * (I2 + M)])
        wgu_s = arena[:, 0:E * I2].rearrange("p (e n) -> p e n", e=E)
        wd_s = arena[:, E * I2:E * (I2 + M)].rearrange("p (e n) -> p e n", e=E)
        SH = 2 * HEADS
        half = SH * L // 2
        qst = arena[:, 0:half].bitcast(BF16).rearrange("p (h n) -> p h n", h=SH)
        kst = arena[:, half:2 * half].bitcast(BF16).rearrange("p (h n) -> p h n", h=SH)
        assert 2 * half + 3 * TOP_K * M <= E * (I2 + M)
        xin = big[:, 0].rearrange("p (q j m) -> p q j m", q=4, m=M)
        ob = big[:, 1].rearrange("p (q j m) -> p q j m", q=4, m=M)
        gb = big[:, 2:4].rearrange("p a (s k m) -> p (a s) k m", k=TOP_K, m=M)
        gb2 = arena[:, 2 * half:2 * half + 3 * TOP_K * M].rearrange("p (s k m) -> p s k m", k=TOP_K, m=M)
        vt = big[:, 0].rearrange("p (i m c) -> p i m c", i=NGR, m=TB)
        ot = big[:, 1].rearrange("p (t m) -> p t m", t=NT)
        otg = big[:, 1].rearrange("p (b m g c) -> p b m g c", b=B, m=TB, g=GB)
        ering = big[:, 2:4].rearrange("p a (s n) -> p (a s) n", n=L)
        kf = arena[:, 2 * half:2 * half + 3 * TOP_K * M].bitcast(BF16)
        w0 = kf[:, 0:F]
        w1 = kf[:, F:F + FC * F].rearrange("p (c n) -> p c n", c=FC)
        w2 = kf[:, F + FC * F:F + FC * F + FC * M].rearrange("p (c n) -> p c n", c=FC)
        mlp = arena[:, 0:2 * half].bitcast(BF16)
        assert 3 * NP * T <= 2 * half * 2 and FC * L == T
        xp = mlp[:, 0:NP * T].rearrange("p (c n) -> p c n", c=NP)
        h1, h2 = (mlp[:, NP * T * a:NP * T * (a + 1)].rearrange("p (c k n) -> p c k n", c=NP, k=FC) for a in (1, 2))
        hid, rest = (big[:, a].rearrange("p (c n) -> p c n", c=FC) for a in (0, 2))
        qf, qr, oT = (t[:].rearrange("p t e -> p (t e)").rearrange("p (o n) -> p o n", o=2) for t in (sc, ra, ch))
        parts = places[:].rearrange("p a n -> p (a n)").rearrange("p (o c n) -> p o c n", o=2, c=NP)
        vs = keep[:].rearrange("p t e -> p (t e)").rearrange("p (k m h c) -> p k m h c", k=2, m=TB, h=HG)
        mx = sb("mx", [P, 2, HG * TB])
        mr = sb("mr", [P, 2, HG * TB])
        mp = sb("mp", [P, 2, P // (HG * TB), HG * TB], BF16)
        zeros = sb("zeros", [P, 4 * M])
        mT = sb("mT", [NP * HG * TB, 2, P], BF16)
        rc = sb("rc", [P, TB, HG])

        def banks_of(f):
            banks = -(-E * TILES[f] // 512)
            return [slice(E // banks * c, E // banks * (c + 1)) for c in range(banks)]

        def back_slot(t):
            n = t - FIRST[1]
            if n < 4:
                return gb[:, n], g_in[n], 16 * TOP_K * (len(range(n, TILES[0], 4)) + 1)
            return gb2[:, (n - 4) % 3], g2_in[(n - 4) % 3], 16 * TOP_K * ((n - 4) // 3 + 1)

        ps = ctx.enter_context(nc.psum_tensor("ps", [P, 8, 512], F32))
        xd, od = ([nc.dram_tensor(f"{n}{f}", (BLOCKS[f] * P, M), F32, kind="Internal").ap() for f in range(2)] for n in ("xd", "od"))
        scr = nc.dram_tensor("scr", (2, B, NP, HD, HEADS, L), BF16, kind="Internal").ap()

        s_idf = sem("s_idf")
        s_x = [sem(f"s_x{q}") for q in range(B)]
        s_w, s_we, s_wa = sem("s_w"), sem("s_we"), sem("s_wa")
        s_idb, s_const, s_decay = sem("s_idb"), sem("s_const"), sem("s_decay")
        s_st, s_rstd, s_v, s_p, s_xn = sem("s_st"), sem("s_rstd"), sem("s_v"), sem("s_p"), sem("s_xn")
        s_tr, s_trs = sem("s_tr"), sem("s_trs")
        s_xz, s_xzs, s_u, s_h = sem("s_xz"), sem("s_xzs"), sem("s_u"), sem("s_h")
        s_y, s_ys, s_yo, s_xb = sem("s_y"), sem("s_ys"), sem("s_yo"), sem("s_xb")
        s_lg, s_lgs = sem("s_lg"), sem("s_lgs")
        s_zero = [sem(f"s_zero{f}") for f in range(2)]
        s_zeros, s_cum, s_pos, s_idx, s_eid, s_tab = (sem(n) for n in ("s_zeros", "s_cum", "s_pos", "s_idx", "s_eid", "s_tab"))
        ld, stq, g_in = ([sem(f"{n}{r}") for r in range(4)] for n in ("ld", "stq", "g_in"))
        s_sc, g2_in = ([sem(f"{n}{r}") for r in range(k)] for n, k in (("s_sc", 2), ("g2_in", 3)))
        rows_back, comb, s_wk = sem("rows_back"), sem("comb"), sem("s_wk")
        xt_ready, x_copied, s_sh = sem("xt_ready"), sem("x_copied"), sem("s_sh")
        gu_ready, sg_ready, hm_ready = sem("gu_ready"), sem("sg_ready"), sem("hm_ready")
        th_ready, th_copied, d_ready, acc_done = sem("th_ready"), sem("th_copied"), sem("d_ready"), sem("acc_done")
        s_qk, s_qks, s_part = sem("s_qk"), sem("s_qks"), sem("s_part")
        s_pw = [sem(f"s_pw{o}") for o in range(2)]
        s_stk = [sem(f"s_stk{b}") for b in range(B)]
        s_pad, s_vv, s_vvs = sem("s_pad"), sem("s_vv"), sem("s_vvs")
        stack_ready = sem("stack_ready")
        s1_ready, s1_free, split_done = sem("s1_ready"), sem("s1_free"), sem("split_done")
        mT_ready, mT_copied, max_in = sem("mT_ready"), sem("mT_copied"), sem("max_in")
        s2_ready, exp_ready, pv_done = sem("s2_ready"), sem("exp_ready"), sem("pv_done")
        vs_ready, o_evac, o_turn, o_norm = sem("vs_ready"), sem("o_evac"), sem("o_turn"), sem("o_norm")
        rc_done, s_vs = sem("rc_done"), sem("s_vs")
        s_pr, s_kf, s_f, s_fs, s_out, s_r = sem("s_pr"), sem("s_kf"), sem("s_f"), sem("s_fs"), sem("s_out"), sem("s_r")
        s_fo, s_hid, s_rest, s_mid, s_xp = sem("s_fo"), sem("s_hid"), sem("s_rest"), sem("s_mid"), sem("s_xp")

        block = ctx.enter_context(nc.Block())
        tiled = "b (t p) m -> p (b t) m"
        STK = 1 + NP

        def write_parts(sp, b):
            for o in range(2):
                sp.wait_ge(s_part, 2 * b + o + 1)
                for c in range(NP):
                    sp.dma_start(scr[o, b, c].rearrange("d h n -> h d n"), parts[:, o, c]).then_inc(s_pw[o], 16)

        def load_stack(sp, b, first=0, heads=HEADS):
            h0 = HEADS * (b % 2) + first
            hs, src = slice(h0, h0 + heads), slice(first, first + heads)
            sp.wait_ge(s_pw[0], 16 * NP * (b + 1))
            sp.dma_start(qst[0:NP * NP * HD, hs, :].rearrange("p h n -> p (h n)"),
                         scr[0, b, :, :, src].rearrange("c d h n -> (c d) (h n)").unsqueeze(0).broadcast_to([NP, NP * HD, heads * L])).then_inc(s_stk[b], 16)
            sp.wait_ge(s_pw[1], 16 * NP * (b + 1))
            for c in range(NP):
                sp.dma_start(kst[NP * HD * c:NP * HD * (c + 1), hs, :].rearrange("p h n -> p (h n)"),
                             scr[1, b, c, :, src].rearrange("d h n -> d (h n)").unsqueeze(0).broadcast_to([NP, HD, heads * L])).then_inc(s_stk[b], 16)

        def stacked(sp, b, loads=1):
            sp.wait_ge(s_stk[b], 16 * STK * loads)
            sp.sem_inc(stack_ready, 1)

        def pad_stack(sp, h0, heads):
            for stack in (qst, kst):
                sp.dma_start(stack[NP * NP * HD:KD, h0:h0 + heads].rearrange("p (a h) n -> p a (h n)", h=2),
                             zeros[NP * NP * HD:KD].bitcast(BF16).unsqueeze(1).broadcast_to([KD - NP * NP * HD, heads // 2, 2 * L])).then_inc(s_pad, 16)
            sp.dma_start(qst[KD:KS, h0:h0 + heads].rearrange("p h (a n) -> p (h a) n", n=P),
                         onesb[KD:KS].unsqueeze(1).broadcast_to([NP, heads * L // P, P])).then_inc(s_pad, 16)

        @block.sync
        def _(sp):
            sp.dma_start(idf[:], ident).then_inc(s_idf, 16)
            for q in range(B):
                sp.dma_start(xt[:, TB * q:TB * q + TB, :], x.rearrange(tiled, p=P)[:, TB * q:TB * q + TB, :]).then_inc(s_x[q], 16)
            for dst, src in ((w_in_s[:], w_in), (w_xp_s[:], w_xp), (dmat_s[0:S], dmat), (dmat_s[S:2 * S], dmat),
                             (w_out_s[:], w_out), (gamma_s[:], gamma), (beta_s[:], beta), (b_in_s[:], b_in),
                             (b_xp_s[0:S], b_xp), (b_xp_s[S:2 * S], b_xp), (decay[0:S], a_log), (decay[S:2 * S], a_log),
                             (gate_s[:], gate_w), (bias_row[:], gate_bias.broadcast_to([P, E])),
                             (rows[:, 0], b_out.broadcast_to([P, M]))):
                sp.dma_start(dst, src).then_inc(s_w, 16)

            def clear_rows(f):
                sp.dma_start(xd[f].rearrange("(p b c) m -> p b (c m)", p=P, c=4),
                             zeros[:].unsqueeze(1).broadcast_to([P, BLOCKS[f] // 4, 4 * M])).then_inc(s_zero[f], 16)

            sp.wait_ge(s_zeros, 1)
            clear_rows(0)
            sp.dma_start(wsh_s[:], w_sh).then_inc(s_we, 16)
            sp.dma_start(wshd_s[0:I], w_shd).then_inc(s_we, 16)
            sp.dma_start(wgu_s, w_gu).then_inc(s_we, 16)
            sp.dma_start(wd_s[0:I], w_d).then_inc(s_we, 16)
            sp.dma_start(wshd_s[I:KI].rearrange("p a m -> p (a m)"), zeros[I:KI, 0:2 * M]).then_inc(s_we, 16)
            sp.dma_start(arena[I:KI, E * I2:E * (I2 + M)].rearrange("p (a n) -> p a n", n=4 * M),
                         zeros[I:KI].unsqueeze(1).broadcast_to([KI - I, E // 4, 4 * M])).then_inc(s_we, 16)
            clear_rows(1)
            for dst, src in ((rows[:, 1], b_v.broadcast_to([P, M])), (rows[:, 2], b_o.broadcast_to([P, M])),
                             (w_qkv_s[:], w_qkv), (w_o_s[:], w_o), (b_qk_s[:], b_qk), (s_row[:], s012.broadcast_to([P, 3])),
                             (kb[:], k0.rearrange("(a p) n -> p a n", p=P)), (kb1[:], k1.rearrange("(c p) n -> p c n", p=P)),
                             (kb2[:], k2.rearrange("(c p) n -> p c n", p=P))):
                sp.dma_start(dst, src).then_inc(s_wa, 16)
            for f in range(2):
                sp.wait_ge(s_eid, f + 1)
                for c in range(COLS[f]):
                    at, n = AHEAD + f * BLOCKS[0] + P * c, min(P, BLOCKS[f] - P * c)
                    sp.dma_start(tab[0:1, at:at + n], eid[0:n, f * COLS[0] + c:f * COLS[0] + c + 1]).then_inc(s_tab, 16)
            sp.wait_ge(s_sc[0], 16 * TILES[0] * TOP_K)
            xq, oq = ([a.rearrange("(q j p) m -> p q j m", j=4, p=P) for a in d] for d in (xd, od))
            QUADS = [n // 4 for n in BLOCKS]

            def quads(q, done, src, dst, store):
                for r in range(4):
                    if src is not None:
                        sp.wait_ge(xt_ready, done * 2 + (2 * r + 2))
                        sp.dma_start(xin[:, r], src[:, bass.ds(q + r, 1)].rearrange("p a j m -> p (a j) m")).then_inc(ld[r], 16)
                    sp.wait_ge(acc_done, done * 2 + (2 * r + 4))
                    sp.dma_start(dst[:, bass.ds(store + r, 1)].rearrange("p a j m -> p (a j) m"), ob[:, r]).then_inc(stq[r], 16)

            for r in range(4):
                sp.dma_start(xin[:, r], xq[0][:, r]).then_inc(ld[r], 16)
            with sp.Fori(0, BODIES[0] - 1) as j:
                q = sp.snap(j * 4)
                quads(q + 4, q, xq[0], oq[0], q)
            sp.wait_ge(s_sc[1], 16 * TILES[1] * TOP_K)
            quads(0, QUADS[0] - 4, xq[1], oq[0], QUADS[0] - 4)
            with sp.Fori(0, BODIES[1] - 1) as j:
                q = sp.snap(j * 4)
                quads(q + 4, q + QUADS[0], xq[1], oq[1], q)
            quads(0, QUADS[0] + QUADS[1] - 4, None, oq[1], QUADS[1] - 4)
            sp.wait_ge(d_ready, NT + NPAIR)
            pad_stack(sp, 0, HG)
            write_parts(sp, 0)
            load_stack(sp, 0, 0, HG)
            sp.wait_ge(s_pad, 48)
            stacked(sp, 0)
            load_stack(sp, 0, HG, HEADS - HG)
            pad_stack(sp, HG, HEADS - HG)
            sp.wait_ge(s_pad, 96)
            stacked(sp, 0, loads=2)
            for i in range(NGR):
                sp.wait_ge(mT_copied, i + 1)
                hd = HG * (i % (2 * GB))
                sp.dma_start(kst[KD:KS, hd:hd + HG, :].rearrange("p h n -> p (h n)"), mT[:, i % 2, :]).then_inc(max_in, 16)
                sp.wait_ge(max_in, 16 * (i + 1))
                if i == 0:
                    write_parts(sp, 1)
                    load_stack(sp, 1)
                    pad_stack(sp, HEADS, HEADS)
                if i == 1:
                    sp.wait_ge(s_pad, 144)
                    stacked(sp, 1)
                for b in range(2, B):
                    if QK_IN.get(i - 1) == b:
                        write_parts(sp, b)
                    if i == GB * (b - 1):
                        sp.wait_ge(s2_ready, HG * TB * i)
                        load_stack(sp, b)
                    if i == GB * (b - 1) + 1:
                        stacked(sp, b)
            for q in range(B):
                sp.wait_ge(s_xn, 4 * B + q + 1)
                sp.dma_start(out.rearrange(tiled, p=P)[:, TB * q:TB * q + TB, :], xt[:, TB * q:TB * q + TB, :]).then_inc(s_out, 16)
            sp.wait_ge(s_out, 16 * B)
            sp.wait_ge(s_we, 16 * 6)
            sp.wait_ge(s_wa, 16 * 9)

        @block.gpsimd
        def _(pool):
            pn = [0]

            def own(ins):
                pn[0] += 1
                ins.then_inc(s_p, 1)
                pool.wait_ge(s_p, pn[0])

            def rstd_of(k):
                pool.wait_ge(s_st, k + 1)
                q = k % B
                r = rstd[:, TB * q:TB * q + TB]
                own(pool.tensor_scalar(r, mv[:, TB * q:TB * q + TB, 1], EPS, None, ALU.add))
                pool.tensor_tensor(r, r, minus_half[:], ALU.pow).then_inc(s_rstd, 1)

            own(pool.memset(minus_half[:], -0.5))
            own(pool.memset(zeros[:], 0.0))
            pool.sem_inc(s_zeros, 1)
            own(pool.memset(mp[:], 0.0))
            own(pool.memset(hm[:], 0.0))
            for q in range(B):
                rstd_of(q)
            own(pool.tensor_tensor(xb[:], xt[:], xt[:], ALU.add))
            pool.wait_ge(s_w, 16 * 15)
            pool.tensor_tensor(xb[:], xb[:], rows[:, 0:1].broadcast_to([P, NT, M]), ALU.add).then_inc(s_xb, 1)
            own(pool.memset(hmT[:], 0.0))
            own(pool.memset(keep[:], 1.0))
            own(pool.memset(keep[:, :, 0:1], 0.0))
            for f in range(2):
                own(pool.memset(keep2[f][:], 1.0))
                own(pool.memset(keep2[f][:, :, 0:1], 0.0))
            own(pool.memset(tri[:], 1.0))
            own(pool.affine_select(out=tri[:], in_=tri[:], pattern=[[1, P]], compare_op=ALU.is_ge, fill=0.0, base=-1,
                                   channel_multiplier=-1))
            own(pool.memset(onesb[:], 1.0))
            own(pool.memset(ones_e[:], 1.0))
            own(pool.memset(tab[:], 0))
            own(pool.iota(thr[:], [[P, TILES[1]]], base=0, channel_multiplier=0, allow_small_or_imprecise_dtypes=True))
            own(pool.iota(bnum[:], [[P, 2]], base=0, channel_multiplier=1, allow_small_or_imprecise_dtypes=True))
            own(pool.memset(before[:], 1.0))
            own(pool.affine_select(out=before[:], in_=before[:], pattern=[[1, GROUPS], [-1, GROUPS]], compare_op=ALU.is_ge,
                                   fill=0.0, base=-1, channel_multiplier=0))
            pool.sem_inc(s_const, 1)

            for q in range(B, 2 * B):
                rstd_of(q)
            for f in range(2):
                pool.wait_ge(s_zero[f], 16)
                pool.wait_ge(s_idx, f + 1)
                pool.wait_ge(s_xn, B + 2 * f + 2)
                for t in range(FIRST[f], FIRST[f] + TILES[f]):
                    for k in range(TOP_K):
                        pool.indirect_dma_start(out=xd[f], out_offset=bass.IndirectOffsetOnAxis(ap=idx[:, t, k:k + 1], axis=0),
                                                in_=xt[:, t], in_offset=None).then_inc(s_sc[f], 16)

            own(pool.memset(vs, 0.0))
            own(pool.memset(vs[:, :, :, :, HD:HD + 1], 1.0))
            pool.sem_inc(s_vs, 1)

            def bring(f, t, slot, landed):
                for k in range(TOP_K):
                    pool.indirect_dma_start(out=slot[:, k], out_offset=None, in_=od[f],
                                            in_offset=bass.IndirectOffsetOnAxis(ap=idx[:, t, k:k + 1], axis=0)).then_inc(landed, 16)

            for r in range(4):
                pool.wait_ge(stq[r], 16 * BODIES[0])
            for t in range(TILES[0]):
                if t >= 4:
                    pool.wait_ge(comb, TOP_K * (t - 3))
                bring(0, t, gb[:, t % 4], g_in[t % 4])
                pool.wait_ge(g_in[t % 4], 16 * TOP_K * (t // 4 + 1))
                pool.sem_inc(rows_back, 1)
            rstd_of(2 * B)
            for r in range(4):
                pool.wait_ge(stq[r], 16 * sum(BODIES))
            for t in range(FIRST[1], NT):
                n = t - FIRST[1]
                if n < 4:
                    pool.wait_ge(comb, TOP_K * (max(range(n, TILES[0], 4)) + 1))
                if n >= 7:
                    last = [max(ts) for ts in COMBINED.values() if t - 3 in ts][0]
                    pool.wait_ge(comb, TOP_K * (last + 1))
                bring(1, t, *back_slot(t)[:2])
                if n == 3:
                    rstd_of(2 * B + 1)
                if n == 6:
                    rstd_of(2 * B + 2)
            def qk_parts(b):
                for o in range(2):
                    pool.wait_ge(s_qks, 2 * b + o + 1)
                    own(pool.tensor_tensor(qr[:, o], qf[:, o], parts[:, o, 0], ALU.subtract))
                    own(pool.tensor_copy(parts[:, o, 1], qr[:, o]))
                    pool.tensor_tensor(parts[:, o, 2], qr[:, o], parts[:, o, 1], ALU.subtract).then_inc(s_part, 1)

            qk_parts(2)
            rstd_of(2 * B + 3)
            pool.wait_ge(s_wa, 16 * 9)
            pool.wait_ge(comb, TOP_K * NT)
            lower = xbT[:].rearrange("p u a m -> p (u a m)")
            upper = hmT[:].rearrange("p u a m -> p (u a m)")
            own(pool.tensor_scalar(upper, kb[:, 0], 2.0, None, ALU.mult))
            own(pool.tensor_scalar(lower, kb[:, 1], 2.0, None, ALU.mult))
            own(pool.tensor_tensor(w0, upper, lower, ALU.subtract))
            own(pool.tensor_scalar(w1, kb1[:], 2.0, -1.0, ALU.mult, ALU.add))
            own(pool.tensor_scalar(w2, kb2[:], 2.0, -1.0, ALU.mult, ALU.add))
            pool.tensor_scalar(s_row[:, 0:2], s_row[:, 0:2], 2.0, None, ALU.mult).then_inc(s_kf, 1)
            qk_parts(3)
            pool.wait_ge(s_xn, 3 * B)
            pool.tensor_tensor(xb[:], xt[:], rows[:, 2:3].broadcast_to([P, NT, M]), ALU.add).then_inc(s_xb, 1)
            for q in range(3 * B, 5 * B):
                rstd_of(q)

        @block.scalar
        def _(act):
            act.wait_ge(s_w, 16 * 15)
            act.activation(decay[:], decay[:], ACT.Exp).then_inc(s_decay, 1)
            act.wait_ge(s_decay, 1)
            act.activation(decay[:], decay[:], ACT.Exp, scale=-1.0).then_inc(s_decay, 1)
            act.wait_ge(s_idf, 16)
            act.activation(idb[:], idf[:], ACT.Copy).then_inc(s_idb, 1)

            def turned(k, dst, **how):
                act.wait_ge(s_tr, k + 1)
                act.activation(dst, ps[:, k % B, :], ACT.Identity, **how).then_inc(s_trs, 1)

            for b in range(B):
                turned(b, xT[:, L * b:L * b + L], scale=gamma_s[:], bias=beta_s[:])
            for o, (dst, f) in enumerate(((xpT, ACT.Silu), (zT, ACT.Sigmoid))):
                for b in range(B):
                    act.wait_ge(s_xz, B * o + b + 1)
                    act.activation(dst[:, b], ps[:, 4 + b, :], f, bias=b_in_s[:, o:o + 1]).then_inc(s_xzs, 1)
            for a in range(2):
                for b in range(2 * a, 2 * a + 2):
                    turned(B + b, xT[:, L * b:L * b + L])
                act.wait_ge(s_lg, a + 1)
                act.activation(sc[:, NT // 2 * a:NT // 2 * (a + 1), :], ps[:, 4 + a, :].rearrange("p (t e) -> p t e", e=E),
                               ACT.Sigmoid).then_inc(s_lgs, 1)
            for t in range(NT + 2):
                if t < NT:
                    act.wait_ge(gu_ready, t + 1)
                    act.activation(sg[:, t % 2], ps[:, 2 + t % 2, 0:I2].rearrange("p (a i) -> p a i", a=2), ACT.Silu).then_inc(sg_ready, 1)
                if 1 <= t <= NT:
                    act.wait_ge(th_ready, t)
                    act.activation(hmT[0:KI, (t - 1) % 2], ps[0:KI, 4 + (t - 1) % 2, 0:2 * P].rearrange("p (a i) -> p a i", a=2), ACT.Copy).then_inc(th_copied, 1)

            def act_pair(s, u, earlier=0):
                static = isinstance(s, int)
                if not static or 1 <= s <= NPAIR:
                    act.wait_ge(gu_ready, s + NT)
                    act.activation(sg[:, (u - 1) % 2], ps[:, 2 + (u - 1) % 2, 0:2 * I2].rearrange("p (a i) -> p a i", a=2)[:, :, 0:I],
                                   ACT.Silu).then_inc(sg_ready, 1)
                if not static or 2 <= s <= NPAIR + 1:
                    act.wait_ge(th_ready, s + (NT - 1))
                    act.activation(hmT[0:KI, u % 2], ps[0:KI, 4 + u % 2, 0:2 * P].rearrange("p (a i) -> p a i", a=2), ACT.Copy).then_inc(th_copied, 1)
                if not static or 3 <= s:
                    quad, part = (u - 3) // 2 % 4, (u - 3) % 2
                    if part == 0 and (not static or s >= 11):
                        act.wait_ge(stq[quad], 16 * ((s - 3) // 8) if static else earlier * 16 + (32 if u >= 3 else 16))
                    act.wait_ge(d_ready, s + (NT - 2))
                    act.activation(ob[:, quad, 2 * part:2 * part + 2], ps[:, 6 + (u - 3) % 2, 0:2 * M].rearrange("p (a m) -> p a m", a=2),
                                   ACT.Copy).then_inc(acc_done, 1)

            for s0 in (0, 8):
                for u in range(8):
                    act_pair(s0 + u, u)
            with act.Fori(0, sum(BODIES) - 2) as j:
                s0 = act.snap(j * 8 + 16)
                for u in range(8):
                    act_pair(s0 + u, u, j)
            for u in range(3):
                act_pair(NPAIR + u, u)

            def turn_in(b, bank):
                act.wait_ge(s_tr, 2 * B + b + 1)
                act.activation(xT[:, L * b:L * b + L], ps[:, bank, :], ACT.Identity).then_inc(s_trs, 1)

            def qk_in(b, o, bank):
                act.wait_ge(s_qk, 2 * b + o + 1)
                if b >= 1:
                    act.wait_ge(s_part, 2 * (b - 1) + o + 1)
                    act.wait_ge(s_pw[o], 16 * NP * b)
                act.activation(parts[:, o, 0], ps[:, bank, :], ACT.Identity, bias=b_qk_s[:, o:o + 1])
                act.activation(qf[:, o], ps[:, bank, :], ACT.Identity, bias=b_qk_s[:, o:o + 1]).then_inc(s_qks, 1)

            act.wait_ge(s_wa, 16 * 9)
            for b in range(2):
                turn_in(b, 4 * b)
                for o in range(2):
                    qk_in(b, o, 4 + o)

            def stage_values(i, k):
                act.activation(vs[:, k, :, :, 0:HD], vt[:, bass.ds(i, 1)].rearrange("p a m (h d) -> p (a m) h d", h=HG),
                               ACT.Copy).then_inc(vs_ready, 1)

            def exps(i, mt):
                for h in range(HG):
                    act.wait_ge(s2_ready, HG * TB * i + (HG * mt + h + 1))
                    if h == 0:
                        act.wait_ge(pv_done, TB * i + (mt + 1))
                    act.activation(ering[:, HG * (mt % 2) + h], ps[:, 4 + h % 2, :], ACT.Exp, scale=SCALE).then_inc(exp_ready, 1)

            def act_group(i, k):
                for mt in range(1, TB):
                    exps(i, mt)
                    if mt == 1 and (not isinstance(i, int) or i + 1 < NGR):
                        stage_values(i + 1, 1 - k)
                    if isinstance(i, int) and mt == 2 and i in TURN_IN:
                        turn_in(TURN_IN[i], 7)
                    if isinstance(i, int) and mt >= 2 and i in QK_IN:
                        qk_in(QK_IN[i], mt - 2, 7)
                if not isinstance(i, int) or i + 1 < NGR:
                    exps(i + 1, 0)
                act.wait_ge(pv_done, TB * i + (TB + 2))
                if not isinstance(i, int) or i >= 2:
                    act.wait_ge(o_turn, i - 1)
                act.activation(oT[:, k], ps[:, 6, :], ACT.Copy).then_inc(o_evac, 1)

            act.wait_ge(s_vs, 1)
            act.wait_ge(s_vvs, 2)
            stage_values(0, 0)
            act.wait_ge(comb, TOP_K * (FIRST[1] + 2))
            exps(0, 0)
            act.wait_ge(comb, TOP_K * (FIRST[1] + 4))
            for i in range(HEAD_GROUPS):
                act_group(i, i % 2)
            act.wait_ge(s_vvs, B)
            with act.Fori(HEAD_GROUPS // 2, NGR // 2 - 1) as j:
                i = act.snap(j * 2)
                act_group(i, 0)
                act_group(i + 1, 1)
            act_group(NGR - 2, 0)
            act_group(NGR - 1, 1)
            for b in range(B):
                turned(3 * B + b, xT[:, L * b:L * b + L])

            def mlp_input(b):
                act.wait_ge(s_tr, 4 * B + b + 1)
                act.activation(xp[:, 0, L * b:L * b + L], ps[:, 4 + b, :], ACT.Copy)
                act.activation(xT[:, L * b:L * b + L], ps[:, 4 + b, :], ACT.Copy).then_inc(s_trs, 1)

            def middle(n, dst, c):
                act.wait_ge(s_rest, n + 1)
                act.activation(dst[:, 1, c], rest[:, c], ACT.Copy).then_inc(s_mid, 1)

            def hidden(b, layer):
                dst = (h1, h2)[layer]
                for c in range(FC):
                    n = (2 * b + layer) * FC + c
                    act.wait_ge(s_f, n + 1)
                    if n >= FC:
                        act.wait_ge(s_fs, n - FC + 1)
                    act.activation(dst[:, 0, c], ps[:, c, :], ACT.Relu, scale=s_row[:, layer:layer + 1])
                    act.activation(hid[:, c], ps[:, c, :], ACT.Relu, scale=s_row[:, layer:layer + 1]).then_inc(s_hid, 1)
                    if c >= 1:
                        middle(n - 1, dst, c - 1)
                middle(n, dst, c)

            act.wait_ge(s_kf, 1)
            mlp_input(0)
            mlp_input(1)
            hidden(0, 0)
            mlp_input(2)
            for b in range(B):
                hidden(b, 1)
                if b == 0:
                    mlp_input(3)
                if b + 1 < B:
                    hidden(b + 1, 0)

        @block.vector
        def _(v):
            vn = [0]

            def own(ins):
                vn[0] += 1
                ins.then_inc(s_v, 1)
                v.wait_ge(s_v, vn[0])

            def stats(src, q):
                for t in range(TB * q, TB * q + TB):
                    ins = v.bn_stats(st[:, t], src[:, t])
                own(ins)
                for t in range(TB * q, TB * q + TB):
                    ins = v.bn_aggr(mv[:, t], st[:, t])
                ins.then_inc(s_st, 1)

            def normalise(dst, src, k):
                q = k % B
                v.wait_ge(s_rstd, k + 1)
                v.wait_ge(s_st, k + 1)
                for t in range(TB * q, TB * q + TB):
                    ins = v.tensor_scalar(dst[:, t], src[:, t], mv[:, t, 0:1], rstd[:, t:t + 1], ALU.subtract, ALU.mult)
                ins.then_inc(s_xn, 1)

            own(v.memset(cnt[:, 0:2], 0.0))
            v.sem_inc(acc_done, 2)
            v.sem_inc(s1_free, 2)
            v.sem_inc(exp_ready, 2)
            v.sem_inc(pv_done, 2)
            for q in range(B):
                v.wait_ge(s_x[q], 16)
                stats(xt, q)
            for q in range(B):
                normalise(tmp, xt, q)
            v.wait_ge(s_w, 16 * 15)
            v.wait_ge(s_decay, 2)
            for j in range(B // 2):
                v.wait_ge(s_u, 2 * j + 2)
                own(v.tensor_scalar(uT[:, j], ps[:, j, :], b_xp_s[:], None, ALU.add))
                v.tensor_tensor_scan(hT[:, j], decay[:].broadcast_to([P, L]), uT[:, j], 0.0, ALU.mult, ALU.add).then_inc(s_h, 1)
            for b in range(B):
                v.wait_ge(s_y, b + 1)
                v.wait_ge(s_xzs, B + b + 1)
                v.tensor_tensor(ysT[:, :, b], ps[:, 4 + b, :], zT[:, b], ALU.mult).then_inc(s_ys, 1)
            v.wait_ge(s_xb, 1)

            def add_mixer(q):
                v.wait_ge(s_yo, q + 1)
                own(v.tensor_tensor(tmp[:, TB * q:TB * q + TB], ps[:, q].rearrange("p (t m) -> p t m", m=M),
                                    xb[:, TB * q:TB * q + TB], ALU.add))
                stats(tmp, q)

            add_mixer(0)
            add_mixer(1)
            normalise(xt, tmp, B)
            normalise(xt, tmp, B + 1)
            add_mixer(2)
            add_mixer(3)

            v.wait_ge(s_const, 1)

            def shared(t):
                if t < NT:
                    v.wait_ge(sg_ready, t + 1)
                    v.tensor_tensor(hm[:, t % 2, :, 0:I], sg[:, t % 2], ps[:, 2 + t % 2, I2:2 * I2].rearrange("p (a i) -> p a i", a=2),
                                    ALU.mult).then_inc(hm_ready, 1)
                if t >= 2:
                    v.wait_ge(d_ready, t - 1)
                    v.tensor_tensor(xb[:, t - 2], ps[:, 6 + t % 2, 0:M], xt[:, t - 2], ALU.add).then_inc(s_sh, 1)

            def route(f):
                def beside(*steps):
                    if f == 1:
                        for t in steps:
                            shared(t)

                n = TILES[f]
                ts = slice(FIRST[f], FIRST[f] + n)
                fsc, fch, fra, frb, fkeep, fgs, fcnt = sc[:, ts], ch[:, ts], ra[:, ts], rb[:, ts], keep[:, ts], gs[:, ts], cnt[:, ts]
                v.wait_ge(s_lgs, f + 1)
                own(v.tensor_tensor(fch, fsc, bias_row[:].unsqueeze(1).broadcast_to([P, n, E]), ALU.add))
                c4 = fch.rearrange("p t (g a) -> p t g a", a=EG)
                m1, m2, m3, m4 = g1[:, ts], g2[:, ts], g3[:, ts], g4[:, ts]
                v.tensor_tensor(m1, c4[:, :, :, 0:4], c4[:, :, :, 4:8], ALU.max)
                own(v.tensor_tensor(m2, c4[:, :, :, 0:4], c4[:, :, :, 4:8], ALU.min))
                beside(0)
                r4, q4 = (a[:, :, 0:2 * GROUPS].rearrange("p t (g a) -> p t g a", a=2) for a in (fra, frb))
                v.tensor_tensor(m3, m1[:, :, :, 0:2], m1[:, :, :, 2:4], ALU.max)
                v.tensor_tensor(r4, m1[:, :, :, 0:2], m1[:, :, :, 2:4], ALU.min)
                own(v.tensor_tensor(q4, m2[:, :, :, 0:2], m2[:, :, :, 2:4], ALU.max))
                own(v.tensor_tensor(m4, r4, q4, ALU.max))
                beside(1)
                first, second, third = fra[:, :, 32:40], fra[:, :, 40:48], fra[:, :, 48:56]
                v.tensor_tensor(first, m3[:, :, :, 0], m3[:, :, :, 1], ALU.max)
                v.tensor_tensor(second, m3[:, :, :, 0], m3[:, :, :, 1], ALU.min)
                own(v.tensor_tensor(third, m4[:, :, :, 0], m4[:, :, :, 1], ALU.max))
                beside(2)
                own(v.tensor_tensor(second, second, third, ALU.max))
                own(v.tensor_tensor(fgs, first, second, ALU.add))
                a4 = fra.rearrange("p t (g j) -> p t g j", j=GROUPS)
                b4 = frb.rearrange("p t (g j) -> p t g j", j=GROUPS)
                other = fgs.unsqueeze(2).broadcast_to([P, n, GROUPS, GROUPS])
                mine = fgs.unsqueeze(3).broadcast_to([P, n, GROUPS, GROUPS])
                v.tensor_tensor(a4, other, mine, ALU.is_gt)
                beside(3)
                own(v.tensor_tensor(b4, other, mine, ALU.is_equal))
                beside(4)
                own(v.tensor_tensor(b4, b4, before[:].unsqueeze(1).broadcast_to([P, n, GROUPS, GROUPS]), ALU.mult))
                beside(5)
                own(v.tensor_tensor(fra, fra, frb, ALU.add))
                beside(6)
                own(v.tensor_reduce(fgs, a4, AX_X, ALU.add))
                own(v.tensor_scalar(fgs, fgs, float(GROUPS_KEPT), None, ALU.is_lt))
                own(v.tensor_tensor(c4, c4, fgs.unsqueeze(3).broadcast_to([P, n, GROUPS, EG]), ALU.mult))
                beside(7)
                for t in range(FIRST[f], FIRST[f] + n):
                    ins = v.max(top[:, t], ch[:, t])
                own(ins)
                beside(8)
                eighth = top[:, ts, 7:8].broadcast_to([P, n, E])
                v.tensor_tensor(fra, fch, eighth, ALU.is_gt)
                beside(9)
                own(v.tensor_tensor(frb, fch, eighth, ALU.is_equal))
                beside(10)
                own(v.tensor_reduce(fcnt, fra, AX_X, ALU.add))
                beside(11)
                own(v.tensor_scalar(fcnt, fcnt, -1.0, float(TOP_K), ALU.mult, ALU.add))
                own(v.tensor_tensor_scan(fch.rearrange("p t e -> p (t e)"), fkeep.rearrange("p t e -> p (t e)"),
                                         frb.rearrange("p t e -> p (t e)"), 0.0, ALU.mult, ALU.add))
                beside(12)
                own(v.tensor_tensor(fch, fch, fcnt.unsqueeze(2).broadcast_to([P, n, E]), ALU.is_le))
                beside(13)
                own(v.tensor_tensor(frb, frb, fch, ALU.mult))
                beside(14)
                own(v.tensor_tensor(fra, fra, frb, ALU.add))
                beside(15)
                own(v.tensor_copy(selb[f].rearrange("p e t -> p t e"), fra))
                beside(16)
                own(v.tensor_tensor_scan(incb[f].rearrange("p e t -> p (e t)"), keep2[f][:].rearrange("p e t -> p (e t)"),
                                         selb[f].rearrange("p e t -> p (e t)"), 0.0, ALU.mult, ALU.add))
                v.tensor_tensor(exb[f], incb[f], selb[f], ALU.subtract).then_inc(s_cum, 1)
                beside(17)
                if f == 0:
                    normalise(xt, tmp, B + 2)
                v.wait_ge(s_pos, f + 1)
                above = frb.rearrange("p t e -> p (t e)").rearrange("p (e j) -> p e j", j=n)
                own(v.tensor_tensor(above, ps[:, 6 + f, 0:E].unsqueeze(2).broadcast_to([P, E, n]),
                                    thr[:, 0:n].unsqueeze(1).broadcast_to([P, E, n]), ALU.is_gt))
                own(v.tensor_reduce(nblk[:], above, AX_X, ALU.add))
                own(v.tensor_tensor_scan(endb[:], ones_e[:], nblk[:], 0.0, ALU.mult, ALU.add))
                own(v.tensor_tensor(baserow[:], endb[:], nblk[:], ALU.subtract))
                own(v.tensor_scalar(baserow[:], baserow[:], float(P), 1.0, ALU.mult, ALU.add))
                banks = banks_of(f)
                for c, es in enumerate(banks):
                    width = es.stop - es.start
                    ins = v.tensor_tensor(fch[:, :, es].rearrange("p t e -> p e t"),
                                          ps[:, 4 + f + c, 0:width * n].rearrange("p (e t) -> p e t", t=n),
                                          baserow[:, es].unsqueeze(2).broadcast_to([P, width, n]), ALU.add)
                own(ins)
                own(v.tensor_tensor(fch, fch, fra, ALU.mult))
                for t in range(FIRST[f], FIRST[f] + n):
                    ins = v.max(dst[:, t], ch[:, t])
                own(ins)
                v.tensor_scalar(idx[:, ts], dst[:, ts], -1.0, None, ALU.add).then_inc(s_idx, 1)
                if f == 0:
                    normalise(xt, tmp, B + 3)
                for c in range(COLS[f]):
                    col = slice(f * COLS[0] + c, f * COLS[0] + c + 1)
                    own(v.tensor_scalar(ecmp[:], endb[:], bnum[:, c:c + 1], None, ALU.is_le))
                    own(v.tensor_reduce(eidf[:, col], ecmp[:], AX_X, ALU.add))
                    own(v.tensor_scalar(eid[:, col], eidf[:, col], float(E - 1), None, ALU.min))
                v.sem_inc(s_eid, 1)

            route(0)
            route(1)
            own(v.tensor_tensor(ra[:], ra[:], sc[:], ALU.mult))
            own(v.tensor_reduce(cnt[:], ra[:], AX_X, ALU.add))
            own(v.tensor_scalar(cnt[:], cnt[:], 1e-20, None, ALU.add))
            own(v.reciprocal(cnt[:], cnt[:]))
            own(v.tensor_scalar(cnt[:], cnt[:], ROUTED_SCALE, None, ALU.mult))
            own(v.tensor_tensor(rb[:], ra[:], cnt[:].unsqueeze(2).broadcast_to([P, NT, E]), ALU.mult))

            def weights_of(t, step):
                ts = bass.ds(t, 1)
                if step == 0:
                    v.tensor_tensor(picked, ch[:, ts].broadcast_to([P, TOP_K, E]),
                                    dst[:, ts].rearrange("p t k -> p (t k)").unsqueeze(2).broadcast_to([P, TOP_K, E]), ALU.is_equal).then_inc(s_wk, 1)
                    return
                v.wait_ge(s_wk, t * 4 + step)
                if step == 1:
                    v.tensor_tensor(picked, picked, rb[:, ts].broadcast_to([P, TOP_K, E]), ALU.mult).then_inc(s_wk, 1)
                elif step == 2:
                    v.tensor_reduce(wsum[:], picked, AX_X, ALU.add).then_inc(s_wk, 1)
                else:
                    v.tensor_copy(wk[:, ts].rearrange("p t k -> p (t k)"), wsum[:]).then_inc(s_wk, 1)

            def dve_pair(s, u):
                static = isinstance(s, int)
                if not static or s < NPAIR:
                    v.wait_ge(xt_ready, s + 1)
                    v.tensor_copy(xbT[:, u % 2], ps[:, u % 2, 0:2 * P].rearrange("p (a m) -> p a m", a=2)).then_inc(x_copied, 1)
                if not static or 1 <= s <= NPAIR:
                    v.wait_ge(sg_ready, s + NT)
                    v.tensor_tensor(hm[:, (u - 1) % 2, :, 0:I], sg[:, (u - 1) % 2],
                                    ps[:, 2 + (u - 1) % 2, 0:2 * I2].rearrange("p (a i) -> p a i", a=2)[:, :, I:I2], ALU.mult).then_inc(hm_ready, 1)

            def dve_body(t, s0, back=None):
                for u in range(8):
                    dve_pair(s0 + u, u)
                    if back is not None:
                        add_row(back, u)
                    if u % 2:
                        weights_of(t, u // 2)

            def add_row(t, k):
                if k >= 1:
                    v.wait_ge(comb, t * TOP_K + k)
                ts = bass.ds(t, 1)
                v.scalar_tensor_tensor(out=tmp[:, ts], in0=gb[:, bass.ds(t % 4, 1), k], scalar=wk[:, ts, k], in1=(tmp if k else xb)[:, ts],
                                       op0=ALU.mult, op1=ALU.add).then_inc(comb, 1)

            assert sum(BODIES) == NT
            for t in range(2):
                dve_body(t, 8 * t)
            with v.Fori(0, BODIES[0]) as j:
                dve_body(j + 2, v.snap(j * 8 + 16))
            with v.Fori(0, TILES[0]) as t:
                s0 = v.snap(t * 8 + (8 * BODIES[0] + 16))
                v.wait_ge(rows_back, t + 1)
                dve_body(t + (BODIES[0] + 2), s0, t)
            for t in range(BODIES[0] + 2 + TILES[0], NT):
                dve_body(t, 8 * t)
            stats(tmp, 0)
            dve_pair(NPAIR, 0)
            normalise(xt, tmp, 2 * B)

            def combine(tiles, k):
                for n, t in enumerate(tiles):
                    slot, landed, count = back_slot(t)
                    if k == 0:
                        v.wait_ge(landed, count)
                    else:
                        v.wait_ge(comb, TOP_K * tiles[0] + len(tiles) * (k - 1) + n + 1)
                    v.scalar_tensor_tensor(out=tmp[:, t], in0=slot[:, k], scalar=wk[:, t, k:k + 1],
                                           in1=(tmp if k else xb)[:, t], op0=ALU.mult, op1=ALU.add).then_inc(comb, 1)
                if k == TOP_K - 1:
                    v.wait_ge(comb, TOP_K * (tiles[-1] + 1))

            def qk_parts(b, o):
                v.wait_ge(s_qks, 2 * b + o + 1)
                own(v.tensor_tensor(qr[:, o], qf[:, o], parts[:, o, 0], ALU.subtract))
                own(v.tensor_copy(parts[:, o, 1], qr[:, o]))
                v.tensor_tensor(parts[:, o, 2], qr[:, o], parts[:, o, 1], ALU.subtract).then_inc(s_part, 1)

            def v_in(b, bank):
                v.wait_ge(s_vv, b + 1)
                v.tensor_tensor(vt[:, GB * b:GB * b + GB].rearrange("p g m c -> p m g c"),
                                ps[:, bank].rearrange("p (m g c) -> p m g c", m=TB, g=GB),
                                rows[:, 1:2].rearrange("p a (g c) -> p a g c", g=GB).broadcast_to([P, TB, GB, HG * HD]),
                                ALU.add).then_inc(s_vvs, 1)

            v.wait_ge(s_wa, 16 * 9)
            for o in range(2):
                qk_parts(0, o)
            v_in(0, 6)
            for r in range(4):
                v.wait_ge(stq[r], 16 * sum(BODIES))

            def row_max(i, k, h, a):
                v.wait_ge(s1_ready, 2 * HG * i + (2 * h + a + 1))
                v.tensor_reduce(mx[:, k, TB * h + 2 * a:TB * h + 2 * a + 2], ps[:, 2 * a:2 * a + 2, :], AX_X,
                                ALU.max).then_inc(s1_free, 1)

            def copy_max(i, k):
                v.wait_ge(mT_ready, i + 1)
                if not (isinstance(i, int) and i < 2):
                    v.wait_ge(max_in, 16 * i - 16)
                v.tensor_copy(mT[:, k], ps[0:NP * HG * TB, 7, 0:P // 2].bitcast(BF16)).then_inc(mT_copied, 1)

            def norm_out(i, k, step):
                turnedv = ps[:, 7].rearrange("p (m h c) -> p m h c", m=TB, h=HG)
                if step == 0:
                    v.wait_ge(o_turn, i + 1)
                    v.reciprocal(rc[:], turnedv[:, :, :, HD]).then_inc(rc_done, 1)
                    return
                v.wait_ge(rc_done, i + 1)
                dst = otg[:, bass.ds(i // GB, 1), :, bass.ds(i % GB, 1), :].rearrange("p b m g (h c) -> p (b m) (g h) c", h=HG)
                v.tensor_tensor(dst, turnedv[:, :, :, 0:HD], rc[:].unsqueeze(3).broadcast_to([P, TB, HG, HD]),
                                ALU.mult).then_inc(o_norm, 1)

            def split_max(i, k, step):
                nm, r = mx[:, k], mr[:, k]
                if step == 0:
                    v.wait_ge(s1_free, 2 * HG * i + (2 * HG + 2))
                    if not (isinstance(i, int) and i < 2):
                        v.wait_ge(mT_ready, i - 1)
                    v.scalar_tensor_tensor(out=mp[:, k, 0], in0=nm, scalar=-1.0, in1=zeros[:, 0:HG * TB], op0=ALU.mult, op1=ALU.add).then_inc(s_r, 1)
                elif step == 1:
                    v.wait_ge(s_r, 3 * i + 1)
                    v.scalar_tensor_tensor(out=r, in0=nm, scalar=-1.0, in1=mp[:, k, 0], op0=ALU.mult, op1=ALU.subtract).then_inc(s_r, 1)
                elif step == 2:
                    v.wait_ge(s_r, 3 * i + 2)
                    v.tensor_copy(mp[:, k, 1], r).then_inc(s_r, 1)
                else:
                    v.wait_ge(s_r, 3 * i + 3)
                    v.tensor_tensor(mp[:, k, 2], r, mp[:, k, 1], ALU.subtract).then_inc(split_done, 1)

            def dve_group(i, k):
                ahead = not isinstance(i, int) or i + 2 < NGR
                after = not isinstance(i, int) or i + 1 < NGR
                for h in range(HG):
                    for a in range(2):
                        if ahead:
                            row_max(i + 2, k, h, a)
                        if after and h == 0 and a == 1:
                            copy_max(i + 1, 1 - k)
                        if isinstance(i, int) and i in COMBINED:
                            combine(COMBINED[i], 2 * h + a)
                        if isinstance(i, int) and i in V_IN and h == 2 and a == 0:
                            v_in(V_IN[i], 7)
                out = not isinstance(i, int) or i >= 1
                for step in range(4):
                    if ahead:
                        split_max(i + 2, k, step)
                    if out and step < 2:
                        norm_out(i - 1, 1 - k, step)

            for h in range(HG):
                for a in range(2):
                    row_max(0, 0, h, a)
            for step in range(4):
                split_max(0, 0, step)
            v.wait_ge(s_wk, 4 * NT)
            for k in range(TOP_K):
                combine(COMBINED[-2], k)
            stats(tmp, 1)
            for h in range(HG):
                for a in range(2):
                    row_max(1, 1, h, a)
                    if h >= 2:
                        combine(COMBINED[-1], 4 * h + 2 * a - 8)
                        combine(COMBINED[-1], 4 * h + 2 * a - 7)
                if h == 0:
                    copy_max(0, 0)
                if h == 1:
                    normalise(xt, tmp, 2 * B + 1)
            for o in range(2):
                qk_parts(1, o)
            v_in(1, 6)
            for step in range(4):
                split_max(1, 1, step)
            for i in range(HEAD_GROUPS):
                dve_group(i, i % 2)
                if i == 0:
                    stats(tmp, 2)
                elif i == 1:
                    normalise(xt, tmp, 2 * B + 2)
                elif i == 3:
                    stats(tmp, 3)
                elif i == 4:
                    normalise(xt, tmp, 2 * B + 3)
            with v.Fori(HEAD_GROUPS // 2, NGR // 2 - 1) as j:
                i = v.snap(j * 2)
                dve_group(i, 0)
                dve_group(i + 1, 1)
            dve_group(NGR - 2, 0)
            dve_group(NGR - 1, 1)
            for step in range(2):
                norm_out(NGR - 1, 1, step)
            v.wait_ge(s_xb, 2)

            def add_x(q):
                v.wait_ge(s_pr, q + 1)
                own(v.tensor_tensor(tmp[:, TB * q:TB * q + TB], ps[:, 4 + q].rearrange("p (t m) -> p t m", m=M),
                                    xb[:, TB * q:TB * q + TB], ALU.add))
                stats(tmp, q)

            def mlp_input(q):
                v.wait_ge(s_trs, 4 * B + q + 1)
                cols = slice(L * q, L * q + L)
                own(v.tensor_tensor(qr[:, q % 2], xT[:, cols], xp[:, 0, cols], ALU.subtract))
                own(v.tensor_copy(xp[:, 1, cols], qr[:, q % 2]))
                v.tensor_tensor(xp[:, 2, cols], qr[:, q % 2], xp[:, 1, cols], ALU.subtract).then_inc(s_xp, 1)

            def last_part(n, dst, c):
                v.wait_ge(s_mid, n + 1)
                v.tensor_tensor(dst[:, 2, c], rest[:, c], dst[:, 1, c], ALU.subtract).then_inc(s_fs, 1)

            def hidden(b, layer):
                dst = (h1, h2)[layer]
                for c in range(FC):
                    n = (2 * b + layer) * FC + c
                    v.wait_ge(s_hid, n + 1)
                    v.tensor_tensor(rest[:, c], hid[:, c], dst[:, 0, c], ALU.subtract).then_inc(s_rest, 1)
                    if c >= 1:
                        last_part(n - 1, dst, c - 1)
                last_part(n, dst, c)

            def add_mlp(q):
                v.wait_ge(s_fo, q + 1)
                made = ps[:, 4:4 + TB, 0:M] if q == B - 1 else ps[:, 4 + q].rearrange("p (t m) -> p t m", m=M)
                own(v.scalar_tensor_tensor(out=tmp[:, TB * q:TB * q + TB], in0=made,
                                           scalar=s_row[:, 2:3], in1=xt[:, TB * q:TB * q + TB], op0=ALU.mult, op1=ALU.add))
                stats(tmp, q)

            add_x(0)
            add_x(1)
            normalise(xt, tmp, 3 * B)
            add_x(2)
            normalise(xt, tmp, 3 * B + 1)
            mlp_input(0)
            add_x(3)
            normalise(xt, tmp, 3 * B + 2)
            mlp_input(1)
            hidden(0, 0)
            normalise(xt, tmp, 3 * B + 3)
            mlp_input(2)
            for b in range(B):
                hidden(b, 1)
                if b == 0:
                    mlp_input(3)
                else:
                    normalise(xt, tmp, 4 * B + b - 1)
                if b + 1 < B:
                    hidden(b + 1, 0)
                add_mlp(b)
            normalise(xt, tmp, 5 * B - 1)

        @block.tensor
        def _(pe):
            pe.wait_ge(s_idf, 16)

            def turn(k, src):
                if k >= B:
                    pe.wait_ge(s_trs, k - B + 1)
                for t in range(TB):
                    ins = pe.transpose(ps[:, k % B, P * t:P * t + P], src(TB * (k % B) + t), idf[:])
                ins.then_inc(s_tr, 1)

            for b in range(B):
                pe.wait_ge(s_xn, b + 1)
                turn(b, lambda t: tmp[:, t])
            pe.wait_ge(s_w, 16 * 15)

            def to_xz(b, o):
                pe.matmul(ps[:, 4 + b, :], w_in_s[:, M * o:M * o + M], xT[:, L * b:L * b + L], start=True, stop=True).then_inc(s_xz, 1)

            for b in range(B):
                pe.wait_ge(s_trs, b + 1)
                to_xz(b, 0)
            for b in range(B):
                pe.wait_ge(s_xzs, b + 1)
                h = S * (b % 2)
                pe.matmul(ps[h:h + S, b // 2, :], w_xp_s[:], xpT[:, b], start=True, stop=True).then_inc(s_u, 1)
                to_xz(b, 1)
            for b in range(B):
                pe.wait_ge(s_xzs, B + b + 1)
                pe.wait_ge(s_h, b // 2 + 1)
                h = S * (b % 2)
                pe.matmul(ps[:, 4 + b, :], dmat_s[h:h + S], hT[h:h + S, b // 2], start=True, stop=True).then_inc(s_y, 1)
            pe.wait_ge(s_ys, B)
            for q in range(B):
                for t in range(TB):
                    l = (TB * q + t) * P // B
                    ins = pe.matmul(ps[:, q, P * t:P * t + P], ysT[:, l:l + P // B, :].rearrange("p l b -> p (l b)"), w_out_s[:],
                                    start=True, stop=True)
                ins.then_inc(s_yo, 1)
            def shared_expert():
                pe.wait_ge(s_we, 16 * 6)
                pe.wait_ge(s_lgs, 2)
                pe.wait_ge(s_idx, 1)
                for t in range(NT + 2):
                    if t < NT:
                        pe.matmul(ps[:, 2 + t % 2, 0:2 * I2], xT[:, P * t:P * t + P], wsh_s[:], start=True, stop=True).then_inc(gu_ready, 1)
                    if 1 <= t <= NT:
                        pe.wait_ge(hm_ready, t)
                        for a in range(2):
                            ins = pe.transpose(ps[0:KI, 4 + (t - 1) % 2, P * a:P * a + P], hm[:, (t - 1) % 2, a], idf[:])
                        ins.then_inc(th_ready, 1)
                    if t >= 2:
                        pe.wait_ge(th_copied, t - 1)
                        if t >= 4:
                            pe.wait_ge(s_sh, t - 3)
                        for a in range(2):
                            ins = pe.matmul(ps[:, 6 + t % 2, 0:M], hmT[0:KI, t % 2, a], wshd_s[0:KI, a], start=(a == 0), stop=(a == 1))
                        ins.then_inc(d_ready, 1)
                pe.wait_ge(s_sh, NT)

            for f in range(2):
                for b in range(2 * f, 2 * f + 2):
                    pe.wait_ge(s_xn, B + b + 1)
                    turn(B + b, lambda t: xt[:, t])
                for t in range(HT):
                    if t % TB == 0:
                        pe.wait_ge(s_trs, B + 2 * f + t // TB + 1)
                    ins = pe.matmul(ps[:, 4 + f, E * t:E * t + E], xT[:, P * (HT * f + t):P * (HT * f + t) + P], gate_s[:],
                                    start=True, stop=True)
                ins.then_inc(s_lg, 1)
                if f == 1:
                    shared_expert()
                pe.wait_ge(s_const, 1)
                pe.wait_ge(s_cum, f + 1)
                for c, es in enumerate(banks_of(f)):
                    cols = slice(es.start * TILES[f], es.stop * TILES[f])
                    bank = ps[:, 4 + f + c, 0:cols.stop - cols.start]
                    pe.matmul(bank, tri[:], selb[f].rearrange("p e t -> p (e t)")[:, cols], start=True, stop=False)
                    pe.matmul(bank, onesb[:], exb[f].rearrange("p e t -> p (e t)")[:, cols], start=False, stop=True)
                pe.matmul(ps[:, 6 + f, 0:E], onesb[:], incb[f][:, :, TILES[f] - 1], start=True, stop=True).then_inc(s_pos, 1)

            def pe_pair(s, u, expert):
                static = isinstance(s, int)
                if not static or s < NPAIR:
                    quad, part = u // 2, u % 2
                    if part == 0:
                        pe.wait_ge(ld[quad], 16 * (s // 8) + 16 if static else s // 8 * 16 + 16)
                    for a in range(2):
                        ins = pe.transpose(ps[:, u % 2, P * a:P * a + P], xin[:, quad, 2 * part + a], idf[:])
                    ins.then_inc(xt_ready, 1)
                if not static or 1 <= s <= NPAIR:
                    pe.wait_ge(x_copied, s)
                    for a in range(2):
                        ins = pe.matmul(ps[:, 2 + (u - 1) % 2, I2 * a:I2 * a + I2], xbT[:, (u - 1) % 2, a],
                                        wgu_s[:, bass.ds(expert(2 * (u - 1) + a), 1), :].rearrange("p a n -> p (a n)"), start=True, stop=True)
                    ins.then_inc(gu_ready, 1)
                if not static or 2 <= s <= NPAIR + 1:
                    pe.wait_ge(hm_ready, s + (NT - 1))
                    for a in range(2):
                        ins = pe.transpose(ps[0:KI, 4 + u % 2, P * a:P * a + P], hm[:, u % 2, a], idf[:])
                    ins.then_inc(th_ready, 1)
                if not static or 3 <= s:
                    pe.wait_ge(th_copied, s + (NT - 2))
                    pe.wait_ge(acc_done, s - 2)
                    for a in range(2):
                        ins = pe.matmul(ps[:, 6 + (u - 3) % 2, M * a:M * a + M], hmT[0:KI, (u - 3) % 2, a],
                                        wd_s[0:KI, bass.ds(expert(2 * (u - 3) + a), 1), :].rearrange("p a n -> p (a n)"), start=True, stop=True)
                    ins.then_inc(d_ready, 1)

            def experts_of(first, blocks):
                _, got = nc.values_load_multi_w_load_instructions(
                    tab[0:1, bass.ds(first + (AHEAD + blocks[0]), len(blocks))], engines=[mybir.EngineType.PE],
                    min_val=0, max_val=E - 1, skip_runtime_bounds_check_because="the table holds minima with E - 1")
                return lambda b: got[b - blocks[0]]

            pe.wait_ge(s_tab, 16 * sum(COLS))
            pe.wait_ge(s_idx, 2)
            chosen = experts_of(0, range(-6, 14))
            for u in range(8):
                pe_pair(u, u, chosen)
            with pe.Fori(1, NB // BODY) as j:
                chosen = experts_of(j * BODY, range(-6, 14))
                s0 = pe.snap(j * 8)
                for u in range(8):
                    pe_pair(s0 + u, u, chosen)
            chosen = experts_of(NB, range(-6, 0))
            for u in range(3):
                pe_pair(NPAIR + u, u, chosen)

            pe.wait_ge(s_wa, 16 * 9)
            pe.wait_ge(s_idb, 1)

            def turn_in(b, bank):
                pe.wait_ge(s_xn, 2 * B + b + 1)
                for t in range(TB):
                    ins = pe.transpose(ps[:, bank, P * t:P * t + P], xt[:, TB * b + t], idf[:])
                ins.then_inc(s_tr, 1)

            def q_or_k(b, o, bank):
                pe.wait_ge(s_trs, 2 * B + b + 1)
                if b >= 1:
                    pe.wait_ge(s_qks, 2 * b + (o if bank == 7 else 0))
                pe.matmul(ps[:, bank, :], w_qkv_s[:, M * o:M * o + M], xT[:, L * b:L * b + L], start=True, stop=True).then_inc(s_qk, 1)

            def v_in(b, bank):
                if b >= 1:
                    pe.wait_ge(s_vvs, b)
                for t in range(TB):
                    ins = pe.matmul(ps[:, bank, P * t:P * t + P], xT[:, L * b + P * t:L * b + P * t + P], w_qkv_s[:, 2 * M:3 * M],
                                    start=True, stop=True)
                ins.then_inc(s_vv, 1)

            def qkv_in(b):
                for o in range(2):
                    q_or_k(b, o, 4 + o)
                v_in(b, 6)

            turn_in(0, 0)
            qkv_in(0)

            def head(i, h):
                if isinstance(i, int):
                    return slice(HG * (i % (2 * GB)) + h, HG * (i % (2 * GB)) + h + 1)
                return bass.ds(i % (2 * GB) * HG + h, 1)

            def flat(ap):
                return ap.rearrange("p a n -> p (a n)")

            def max_scores(i, h, c):
                if c % 2 == 0:
                    pe.wait_ge(s1_free, 2 * HG * i + (2 * h + c // 2 + 1))
                ins = pe.matmul(ps[:, c, :], flat(kst[0:KD, head(i, h), P * c:P * c + P]), flat(qst[0:KD, head(i, h), :]),
                                start=True, stop=True)
                if c % 2:
                    ins.then_inc(s1_ready, 1)

            def scores(i, mt, h):
                if mt == 0 and h == 0:
                    pe.wait_ge(max_in, 16 * i + 16)
                pe.wait_ge(exp_ready, HG * TB * i + (HG * mt + h + 1))
                pe.matmul(ps[:, 4 + h % 2, :], flat(qst[0:KS, head(i, h), P * mt:P * mt + P]), flat(kst[0:KS, head(i, h), :]),
                          start=True, stop=True).then_inc(s2_ready, 1)

            def values(i, k, mt):
                if mt == 0:
                    pe.wait_ge(vs_ready, i + 1)
                    if not isinstance(i, int) or i >= 1:
                        pe.wait_ge(o_evac, i)
                pe.wait_ge(exp_ready, HG * TB * i + (HG * (mt + 1) + 2))
                for h in range(HG):
                    ins = pe.matmul(ps[32 * h:32 * h + 32, 6, :], vs[:, k, mt, h], ering[:, HG * (mt % 2) + h],
                                    start=(mt == 0), stop=(mt == TB - 1))
                ins.then_inc(pv_done, 1)

            def turn_max(i, k):
                pe.wait_ge(split_done, i + 1)
                if not isinstance(i, int) or i >= 3:
                    pe.wait_ge(o_norm, i - 2)
                pe.transpose(ps[:, 7, 0:P // 2].bitcast(BF16), mp[:, k].rearrange("p c n -> p (c n)"), idb[:]).then_inc(mT_ready, 1)

            def turn_out(i, k):
                pe.wait_ge(o_evac, i + 1)
                if isinstance(i, int):
                    bank_back(i + 1)
                if not isinstance(i, int) or i + 2 < NGR:
                    pe.wait_ge(mT_copied, i + 3)
                else:
                    pe.wait_ge(o_norm, i)
                for c in range(TB):
                    ins = pe.transpose(ps[:, 7, P * c:P * c + P], oT[:, k, P * c:P * c + P], idf[:])
                ins.then_inc(o_turn, 1)

            def pe_group(i, k):
                static = isinstance(i, int)
                ahead, after = not static or i + 2 < NGR, not static or i + 1 < NGR
                if ahead:
                    pe.wait_ge(stack_ready, (i + 2) // GB + 2)
                for mt in range(TB):
                    for what, h in (("s", 0), ("s", 1), ("m", 0), ("m", 1), ("m", 2), ("s", 2), ("m", 3), ("s", 3)):
                        if what == "m":
                            if ahead:
                                max_scores(i + 2, mt, h)
                            continue
                        if mt == 0 and h == 3 and after:
                            turn_max(i + 1, 1 - k)
                        if mt == 1 and h == 3 and static and i < HEAD_GROUPS:
                            later_sequence(i, 0)
                        if mt == 2 and h == 2 and static and i < HEAD_GROUPS:
                            later_sequence(i, 1)
                        if mt == 3 and h == 2 and after and (not static or i >= 1):
                            turn_out(i - 1, 1 - k)
                        if mt < TB - 1:
                            scores(i, mt + 1, h)
                        elif after:
                            scores(i + 1, 0, h)
                    values(i, k, mt)

            def later_sequence(i, step):
                if step == 0 and (i in TURN_IN or i in QK_IN or i in V_IN):
                    pe.wait_ge(mT_copied, i + 2)
                if step == 0 and i in TURN_IN:
                    turn_in(TURN_IN[i], 7)
                if i in QK_IN:
                    q_or_k(QK_IN[i], step, 7)
                if step == 0 and i in V_IN:
                    v_in(V_IN[i], 7)

            def bank_back(i):
                if i in TURN_IN:
                    pe.wait_ge(s_trs, 2 * B + TURN_IN[i] + 1)
                if i in QK_IN:
                    pe.wait_ge(s_qks, 2 * QK_IN[i] + 2)
                if i in V_IN:
                    pe.wait_ge(s_vvs, V_IN[i] + 1)

            pe.wait_ge(stack_ready, 1)
            for h in range(HG):
                for c in range(TB):
                    max_scores(0, h, c)
            turn_max(0, 0)
            pe.wait_ge(stack_ready, 2)
            for h in range(HG):
                for c in range(TB):
                    max_scores(1, h, c)
                if h == 2:
                    pe.wait_ge(s_qks, 2)
                    turn_in(1, 4)
            pe.wait_ge(s_trs, 2 * B + 2)
            qkv_in(1)
            pe.wait_ge(s_qks, 4)
            pe.wait_ge(s_vvs, 2)
            for h in range(HG):
                scores(0, 0, h)
            for i in range(HEAD_GROUPS):
                pe_group(i, i % 2)
            with pe.Fori(HEAD_GROUPS // 2, NGR // 2 - 1) as j:
                i = pe.snap(j * 2)
                pe_group(i, 0)
                pe_group(i + 1, 1)
            pe_group(NGR - 2, 0)
            pe_group(NGR - 1, 1)
            turn_out(NGR - 2, 0)
            turn_out(NGR - 1, 1)

            def out_in(b):
                pe.wait_ge(o_norm, GB * (b + 1))
                turn(3 * B + b, lambda t: ot[:, t])

            def project(b):
                pe.wait_ge(s_trs, 3 * B + b + 1)
                for t in range(TB):
                    ins = pe.matmul(ps[:, 4 + b, P * t:P * t + P], xT[:, L * b + P * t:L * b + P * t + P], w_o_s[:], start=True, stop=True)
                ins.then_inc(s_pr, 1)

            for b in range(B - 1):
                out_in(b)
            for b in range(B - 1):
                project(b)
            out_in(B - 1)
            project(B - 1)

            def mlp_input(b):
                pe.wait_ge(s_xn, 3 * B + b + 1)
                for t in range(TB):
                    ins = pe.transpose(ps[:, 4 + b, P * t:P * t + P], xt[:, TB * b + t], idf[:])
                ins.then_inc(s_tr, 1)

            def hidden(b, layer):
                for c in range(FC):
                    n = (2 * b + layer) * FC + c
                    if n >= FC:
                        pe.wait_ge(s_hid, n - FC + 1)
                    if layer == 0 and c == 0:
                        pe.wait_ge(s_xp, b + 1)
                    for kk in range(FC if layer else 1):
                        if layer == 1 and c == 0:
                            pe.wait_ge(s_fs, 2 * b * FC + kk + 1)
                        w = w1[:, kk, P * c:P * c + P] if layer else w0[:, P * c:P * c + P]
                        for part in range(NP):
                            ins = pe.matmul(ps[:, c, :], w, h1[:, part, kk] if layer else xp[:, part, L * b:L * b + L],
                                            start=(kk == 0 and part == 0), stop=(part == NP - 1 and (not layer or kk == FC - 1)))
                    ins.then_inc(s_f, 1)

            def mlp_output(b):
                if b == B - 1:
                    pe.wait_ge(s_st, 4 * B + b)
                    for kk in range(FC):
                        pe.wait_ge(s_fs, (2 * b + 1) * FC + kk + 1)
                        for t in range(TB):
                            for part in range(NP):
                                ins = pe.matmul(ps[:, 4 + t, 0:P], h2[:, part, kk, P * t:P * t + P], w2[:, kk],
                                                start=(kk == 0 and part == 0), stop=(kk == FC - 1 and part == NP - 1))
                    ins.then_inc(s_fo, 1)
                    return
                for kk in range(FC):
                    pe.wait_ge(s_fs, (2 * b + 1) * FC + kk + 1)
                for t in range(TB):
                    for kk in range(FC):
                        for part in range(NP):
                            ins = pe.matmul(ps[:, 4 + b, P * t:P * t + P], h2[:, part, kk, P * t:P * t + P], w2[:, kk],
                                            start=(kk == 0 and part == 0), stop=(kk == FC - 1 and part == NP - 1))
                ins.then_inc(s_fo, 1)

            pe.wait_ge(s_kf, 1)
            mlp_input(0)
            mlp_input(1)
            hidden(0, 0)
            mlp_input(2)
            for b in range(B):
                hidden(b, 1)
                if b == 0:
                    mlp_input(3)
                if b + 1 < B:
                    hidden(b + 1, 0)
                mlp_output(b)


def kernel(**inputs):
    import numpy as np
    import concourse.bacc as bacc
    from concourse import mybir as mb
    from concourse.bass_utils import run_bass_kernel_spmd

    a = {k: np.asarray(v) for k, v in inputs.items()}
    wg, wu, wd = a["L0_ffn_Wg"], a["L0_ffn_Wu"], a["L0_ffn_Wd"]
    i = wg.shape[1]
    arrays = {
        "x": a["L0_attn_x"], "a_log": a["L0_attn_A_log"].reshape(-1, 1), "dmat": a["L0_attn_Dmat"],
        "w_in": a["L0_attn_W_in"].T, "b_in": a["L0_attn_b_in"].reshape(2, P).T, "w_xp": a["L0_attn_W_xp"].T,
        "b_xp": a["L0_attn_b_xp"].reshape(-1, 1), "w_out": a["L0_attn_W_out"].T, "b_out": a["L0_attn_b_out"].reshape(1, P),
        "gamma": a["L0_attn_gamma"].reshape(P, 1), "beta": a["L0_attn_beta"].reshape(P, 1),
        "gate_w": a["L0_ffn_gate_w"].T, "gate_bias": a["L0_ffn_gate_bias"].reshape(1, -1),
        "w_gu": np.concatenate([wg, wu], axis=1).transpose(2, 0, 1), "w_d": wd.transpose(2, 0, 1),
        "w_sh": np.concatenate([a["L0_ffn_Sg"], a["L0_ffn_Su"]]).T,
        "w_shd": a["L0_ffn_Sd"].reshape(P, 2, i).transpose(2, 1, 0),
        "w_qkv": np.concatenate([a["L1_attn_Wq"], a["L1_attn_Wk"], a["L1_attn_Wv"]]).T,
        "b_qk": np.stack([a["L1_attn_bq"], a["L1_attn_bk"]], axis=1), "b_v": a["L1_attn_bv"].reshape(1, P),
        "w_o": a["L1_attn_Wo"].T, "b_o": a["L1_attn_bo"].reshape(1, P),
        "k0": a["L1_ffn_k0"], "k1": a["L1_ffn_k1"], "k2": a["L1_ffn_k2"],
        "s012": np.stack([a["L1_ffn_s0"], a["L1_ffn_s1"], a["L1_ffn_s2"]]).reshape(1, 3),
        "ident": np.eye(P, dtype=np.float32),
    }
    arrays = {k: np.ascontiguousarray(v) for k, v in arrays.items()}
    nc = bacc.Bacc("TRN2", target_bir_lowering=False, num_devices=1)
    args = {k: nc.dram_tensor(k, v.shape, mb.dt.from_np(v.dtype), kind="ExternalInput").ap() for k, v in arrays.items()}
    out = nc.dram_tensor("out", a["L0_attn_x"].shape, mb.dt.float32, kind="ExternalOutput").ap()
    build(nc, **args, out=out)
    return run_bass_kernel_spmd(nc, [arrays], core_ids=[0]).results[0]["out"]
```
